# Optimizing a Trainium2 kernel written in Bass

```python
import numpy as np
import jax
import jax.numpy as jnp

def _softmax(x, axis=-1):
    return jax.nn.softmax(x, axis=axis)

def _gelu(x):
    return jax.nn.gelu(x, approximate=True)

def _silu(x):
    return jax.nn.silu(x)

def _sigmoid(x):
    return jax.nn.sigmoid(x)

def _layernorm(x, axis=-1, eps=1e-05):
    m = jnp.mean(x, axis=axis, keepdims=True)
    v = jnp.var(x, axis=axis, keepdims=True)
    return (x - m) / jnp.sqrt(v + eps)

def _scatter_add(tgt, idx, src, axis=0):
    return tgt.at[idx].add(src)

def _segment_sum(src, seg, n):
    return jax.ops.segment_sum(src, seg, n)
kernel_name = 'mk_adaln_ffn_d2_seqx_r4_4a1fcb'

def setup_inputs(seed: int=0):
    np.random.seed(seed)
    _w = jnp.asarray

    def _rec_inputs():
        import jax
        import jax.numpy as jnp
        _rk = jax.random.key(seed)
        x = -0.0003929 + 0.9999 * jax.random.normal(jax.random.fold_in(_rk, 1), (16, 256, 256), jnp.float32)
        _lenS = 256 - jax.random.randint(jax.random.fold_in(_rk, 7), (16,), 0, max(1, 256 // 4) + 1, jnp.int32)
        _lenS2 = 256 - jax.random.randint(jax.random.fold_in(_rk, 8), (16,), 0, max(1, 256 // 4) + 1, jnp.int32)
        itok_B_0_2 = jax.random.randint(jax.random.fold_in(_rk, 11), (16,), 0, 3, jnp.int32)
        itok_B_0_30 = jax.random.randint(jax.random.fold_in(_rk, 12), (16,), 0, 31, jnp.int32)
        return (x, itok_B_0_2, itok_B_0_30)
    x, itok_B_0_2, itok_B_0_30 = _rec_inputs()

    def _L0_cond_setup():
        import jax, jax.numpy as jnp
        import numpy as np
        NEG_INF = -1e+30
        key = jax.random.key(seed)
        k1, k2, k3, k4, k5 = jax.random.split(key, 5)
        B, S, D, A = (16, 256, 256, 64)
        hidden = jax.random.normal(k1, (B, S, D), dtype=jnp.float32)
        W1 = jax.random.normal(k2, (D, A), dtype=jnp.float32) / np.sqrt(D)
        b1 = jax.random.normal(k3, (A,), dtype=jnp.float32) * 0.01
        v = jax.random.normal(k4, (A,), dtype=jnp.float32) / np.sqrt(A)
        prompt_type_ids = jax.random.randint(k5, (B,), 0, 3, dtype=jnp.int32)
        return {'hidden': hidden, 'W1': W1, 'b1': b1, 'v': v, 'prompt_type_ids': prompt_type_ids}
    _L0_cond_all = _L0_cond_setup()
    _L0_cond_in = {k: v for k, v in _L0_cond_all.items() if k in ('W1', 'b1', 'v')}
    del _L0_cond_all

    def _L0_ffn_setup():
        import jax, jax.numpy as jnp
        import numpy as np
        DIM = 256
        INTER = 256
        E = 32
        K = 4
        G = 8
        LG = 4
        ROUTE_SCALE = 1.0
        CAP_FACTOR = 1.25
        B, S = (4, 512)

        def _gate(xf, wg):
            logits = xf @ wg.T
            scores = jax.nn.softmax(logits, axis=-1)
            sg = scores.reshape(-1, G, E // G)
            group_scores = sg.max(axis=-1)
            _, gtop = jax.lax.top_k(group_scores, LG)
            keep_g = jnp.sum(jax.nn.one_hot(gtop, G, dtype=jnp.float32), axis=1) > 0
            masked = jnp.where(keep_g[:, :, None], sg, -jnp.inf).reshape(-1, E)
            _, idx = jax.lax.top_k(masked, K)
            w = jnp.take_along_axis(scores, idx, axis=1)
            w = w / (w.sum(-1, keepdims=True) + 1e-09) * ROUTE_SCALE
            return (w.astype(xf.dtype), idx)

        def _forward(x, wg, w1, w2, w3, sw1, sw2, sw3):
            shape = x.shape
            xf = x.reshape(-1, DIM)
            N = xf.shape[0]
            cap = max(1, int(CAP_FACTOR * N * K / E))
            w, idx = _gate(xf, wg)
            fe = idx.reshape(-1)
            oh = jax.nn.one_hot(fe, E, dtype=jnp.int32)
            pos = (jnp.cumsum(oh, axis=0) * oh).sum(-1) - 1
            keep = pos < cap
            dest = jnp.where(keep, fe * cap + pos, E * cap)
            tok = jnp.arange(N * K, dtype=jnp.int32) // K
            buf_tok = jnp.full((E * cap + 1,), N, jnp.int32).at[dest].set(tok)[:-1]
            buf_w = jnp.zeros((E * cap + 1,), x.dtype).at[dest].set(w.reshape(-1))[:-1]
            xp = jnp.concatenate([xf, jnp.zeros((1, DIM), x.dtype)], axis=0)
            xe = xp[buf_tok].reshape(E, cap, DIM)
            h = jax.nn.silu(jnp.einsum('ecd,edh->ech', xe, w1)) * jnp.einsum('ecd,edh->ech', xe, w3)
            out = jnp.einsum('ech,ehd->ecd', h, w2) * buf_w.reshape(E, cap, 1)
            y = jnp.zeros((N + 1, DIM), x.dtype).at[buf_tok].add(out.reshape(E * cap, DIM))[:N]
            z = jax.nn.silu(xf @ sw1) * (xf @ sw3) @ sw2
            return (y + z).reshape(shape)
        key = jax.random.key(seed)
        ks = jax.random.split(key, 9)
        sd = DIM ** (-0.5)
        si = INTER ** (-0.5)
        x = jax.random.normal(ks[0], (B, S, DIM), jnp.float32)
        wg = jax.random.normal(ks[1], (E, DIM), jnp.float32) * sd
        w1 = jax.random.normal(ks[2], (E, DIM, INTER), jnp.float32) * sd
        w3 = jax.random.normal(ks[3], (E, DIM, INTER), jnp.float32) * sd
        w2 = jax.random.normal(ks[4], (E, INTER, DIM), jnp.float32) * si
        sw1 = jax.random.normal(ks[5], (DIM, INTER), jnp.float32) * sd
        sw3 = jax.random.normal(ks[6], (DIM, INTER), jnp.float32) * sd
        sw2 = jax.random.normal(ks[7], (INTER, DIM), jnp.float32) * si
        return dict(x=x, wg=wg, w1=w1, w2=w2, w3=w3, sw1=sw1, sw2=sw2, sw3=sw3)
    _L0_ffn_all = _L0_ffn_setup()
    _L0_ffn_in = {k: v for k, v in _L0_ffn_all.items() if k in ('wg', 'w1', 'w2', 'w3', 'sw1', 'sw2', 'sw3')}
    del _L0_ffn_all

    def _L1_cond_setup():
        import jax, jax.numpy as jnp
        import numpy as np
        C, I, O = (32, 256, 256)
        B, T = (64, 128)
        key = jax.random.key(seed)
        kx, kc, kw, kb = jax.random.split(key, 4)
        x = jax.random.normal(kx, (B, T, I), dtype=jnp.float32)
        cat_ids = jax.random.randint(kc, (B,), 0, C)
        W = 0.02 * jax.random.normal(kw, (C, I, O), dtype=jnp.float32)
        b = jnp.zeros((C, O), dtype=jnp.float32)
        return {'x': x, 'cat_ids': cat_ids, 'W': W, 'b': b}
    _L1_cond_all = _L1_cond_setup()
    _L1_cond_in = {k: v for k, v in _L1_cond_all.items() if k in ('W', 'b')}
    del _L1_cond_all

    def _L1_ffn_setup():
        import jax, jax.numpy as jnp
        import numpy as np
        import math
        B, T, D, H, E, TOPK, CAPF = (4, 512, 256, 16, 8, 2, 2.0)
        HD = D // H

        def layernorm(x, g, b, eps=1e-05):
            m = jnp.mean(x, -1, keepdims=True)
            v = jnp.mean(jnp.square(x - m), -1, keepdims=True)
            return (x - m) * jax.lax.rsqrt(v + eps) * g + b

        def block_forward(x, ln1_g, ln1_b, Wqkv, Wproj, ln2_g, ln2_b, Wgate, W1, b1, W2, b2):
            Bb, Tt, d = x.shape
            hd = HD
            half = hd // 2
            h = layernorm(x, ln1_g, ln1_b)
            qkv = (h @ Wqkv).reshape(Bb, Tt, H, 3 * hd)
            q, k, v = (qkv[..., :hd], qkv[..., hd:2 * hd], qkv[..., 2 * hd:])
            inv_freq = 1.0 / 10000.0 ** (jnp.arange(0, hd, 2, dtype=jnp.float32) / hd)
            ang = jnp.arange(Tt, dtype=jnp.float32)[:, None] * inv_freq
            sin = jnp.sin(ang)[None, :, None, :].astype(x.dtype)
            cos = jnp.cos(ang)[None, :, None, :].astype(x.dtype)

            def rope(t):
                t1, t2 = (t[..., :half], t[..., half:])
                return jnp.concatenate([t1 * cos - t2 * sin, t1 * sin + t2 * cos], -1)
            q, k = (rope(q), rope(k))
            scores = jnp.einsum('bqhd,bkhd->bhqk', q, k) / math.sqrt(hd)
            causal = jnp.tril(jnp.ones((Tt, Tt), dtype=bool))
            scores = jnp.where(causal, scores, jnp.asarray(-1000000000.0, scores.dtype))
            probs = jax.nn.softmax(scores, axis=-1)
            attn = jnp.einsum('bhqk,bkhd->bqhd', probs, v).reshape(Bb, Tt, d) @ Wproj
            x = x + attn
            h2 = layernorm(x, ln2_g, ln2_b)
            flat = h2.reshape(-1, d)
            N = flat.shape[0]
            capacity = int(math.ceil(CAPF * N / E))
            gates = jax.nn.softmax((flat @ Wgate).astype(jnp.float32), -1).astype(flat.dtype)
            _, top_inds = jax.lax.top_k(gates, TOPK)
            mask = jnp.zeros((N, E), dtype=bool).at[jnp.arange(N)[:, None], top_inds].set(True)
            pos = jnp.cumsum(mask.astype(jnp.int32), axis=0) * mask - 1
            keep = (pos < capacity) & mask
            t_flat = jnp.repeat(jnp.arange(N), TOPK)
            e_flat = top_inds.reshape(-1)
            p = pos[t_flat, e_flat]
            kp = keep[t_flat, e_flat]
            p_eff = jnp.where(kp, p, capacity)
            exp_in = jnp.zeros((E, capacity, d), flat.dtype).at[e_flat, p_eff].set(flat[t_flat], mode='drop')
            hmid = jax.nn.gelu(jnp.einsum('ecd,edf->ecf', exp_in, W1) + b1[:, None, :], approximate=False)
            exp_out = jnp.einsum('ecf,efd->ecd', hmid, W2) + b2[:, None, :]
            gate = gates[t_flat, e_flat] * kp.astype(flat.dtype)
            p_g = jnp.minimum(p_eff, capacity - 1)
            moe = jnp.zeros((N, d), flat.dtype).at[t_flat].add(exp_out[e_flat, p_g] * gate[:, None])
            return x + moe.reshape(Bb, Tt, d)
        key = jax.random.key(seed)
        ks = jax.random.split(key, 8)
        s = 0.02
        return {'x': jax.random.normal(ks[0], (B, T, D), jnp.float32), 'ln1_g': jnp.ones((D,), jnp.float32), 'ln1_b': jnp.zeros((D,), jnp.float32), 'Wqkv': jax.random.normal(ks[1], (D, 3 * D), jnp.float32) * s, 'Wproj': jax.random.normal(ks[2], (D, D), jnp.float32) * s, 'ln2_g': jnp.ones((D,), jnp.float32), 'ln2_b': jnp.zeros((D,), jnp.float32), 'Wgate': jax.random.normal(ks[3], (D, E), jnp.float32) * s, 'W1': jax.random.normal(ks[4], (E, D, 4 * D), jnp.float32) * s, 'b1': jnp.zeros((E, 4 * D), jnp.float32), 'W2': jax.random.normal(ks[5], (E, 4 * D, D), jnp.float32) * s, 'b2': jnp.zeros((E, D), jnp.float32)}
    _L1_ffn_all = _L1_ffn_setup()
    _L1_ffn_in = {k: v for k, v in _L1_ffn_all.items() if k in ('ln1_g', 'ln1_b', 'Wqkv', 'Wproj', 'ln2_g', 'ln2_b', 'Wgate', 'W1', 'b1', 'W2', 'b2')}
    del _L1_ffn_all
    return {'x': x, 'itok_B_0_2': itok_B_0_2, 'itok_B_0_30': itok_B_0_30, 'L0_cond_W1': _L0_cond_in['W1'], 'L0_cond_b1': _L0_cond_in['b1'], 'L0_cond_v': _L0_cond_in['v'], 'L0_ffn_wg': _L0_ffn_in['wg'], 'L0_ffn_w1': _L0_ffn_in['w1'], 'L0_ffn_w2': _L0_ffn_in['w2'], 'L0_ffn_w3': _L0_ffn_in['w3'], 'L0_ffn_sw1': _L0_ffn_in['sw1'], 'L0_ffn_sw2': _L0_ffn_in['sw2'], 'L0_ffn_sw3': _L0_ffn_in['sw3'], 'L1_cond_W': _L1_cond_in['W'], 'L1_cond_b': _L1_cond_in['b'], 'L1_ffn_ln1_g': _L1_ffn_in['ln1_g'], 'L1_ffn_ln1_b': _L1_ffn_in['ln1_b'], 'L1_ffn_Wqkv': _L1_ffn_in['Wqkv'], 'L1_ffn_Wproj': _L1_ffn_in['Wproj'], 'L1_ffn_ln2_g': _L1_ffn_in['ln2_g'], 'L1_ffn_ln2_b': _L1_ffn_in['ln2_b'], 'L1_ffn_Wgate': _L1_ffn_in['Wgate'], 'L1_ffn_W1': _L1_ffn_in['W1'], 'L1_ffn_b1': _L1_ffn_in['b1'], 'L1_ffn_W2': _L1_ffn_in['W2'], 'L1_ffn_b2': _L1_ffn_in['b2']}

def reference(x, itok_B_0_2, itok_B_0_30, L0_cond_W1, L0_cond_b1, L0_cond_v, L0_ffn_wg, L0_ffn_w1, L0_ffn_w2, L0_ffn_w3, L0_ffn_sw1, L0_ffn_sw2, L0_ffn_sw3, L1_cond_W, L1_cond_b, L1_ffn_ln1_g, L1_ffn_ln1_b, L1_ffn_Wqkv, L1_ffn_Wproj, L1_ffn_ln2_g, L1_ffn_ln2_b, L1_ffn_Wgate, L1_ffn_W1, L1_ffn_b1, L1_ffn_W2, L1_ffn_b2):
    import jax
    import jax.numpy as jnp

    def _L0_cond_ref(hidden, W1, b1, v, prompt_type_ids):
        import jax, jax.numpy as jnp
        import numpy as np
        NEG_INF = -1e+30
        B, S, D = hidden.shape
        attn_in = jnp.tanh(jnp.einsum('bsd,da->bsa', hidden, W1) + b1)
        scores = jnp.einsum('bsa,a->bs', attn_in, v)
        idx = jnp.arange(S)
        j = idx[:, None]
        l = idx[None, :]
        prefix_m = l <= j
        postfix_m = l >= j
        cloze_m = l != j
        pt = prompt_type_ids[:, None, None]
        mask = jnp.where(pt == 0, prefix_m[None], jnp.where(pt == 1, postfix_m[None], cloze_m[None]))
        masked_scores = jnp.where(mask, scores[:, None, :], NEG_INF)
        p = jax.nn.softmax(masked_scores, axis=-1)
        cnt = jnp.sum(mask, axis=-1).astype(hidden.dtype)
        pooled = jnp.einsum('bjl,bld->bjd', p, hidden) / cnt[..., None]
        return pooled

    def _L0_ffn_ref(x, wg, w1, w2, w3, sw1, sw2, sw3):
        import jax, jax.numpy as jnp
        import numpy as np
        DIM = 256
        INTER = 256
        E = 32
        K = 4
        G = 8
        LG = 4
        ROUTE_SCALE = 1.0
        CAP_FACTOR = 1.25
        B, S = (4, 512)

        def _gate(xf, wg):
            logits = xf @ wg.T
            scores = jax.nn.softmax(logits, axis=-1)
            sg = scores.reshape(-1, G, E // G)
            group_scores = sg.max(axis=-1)
            _, gtop = jax.lax.top_k(group_scores, LG)
            keep_g = jnp.sum(jax.nn.one_hot(gtop, G, dtype=jnp.float32), axis=1) > 0
            masked = jnp.where(keep_g[:, :, None], sg, -jnp.inf).reshape(-1, E)
            _, idx = jax.lax.top_k(masked, K)
            w = jnp.take_along_axis(scores, idx, axis=1)
            w = w / (w.sum(-1, keepdims=True) + 1e-09) * ROUTE_SCALE
            return (w.astype(xf.dtype), idx)

        def _forward(x, wg, w1, w2, w3, sw1, sw2, sw3):
            shape = x.shape
            xf = x.reshape(-1, DIM)
            N = xf.shape[0]
            cap = max(1, int(CAP_FACTOR * N * K / E))
            w, idx = _gate(xf, wg)
            fe = idx.reshape(-1)
            oh = jax.nn.one_hot(fe, E, dtype=jnp.int32)
            pos = (jnp.cumsum(oh, axis=0) * oh).sum(-1) - 1
            keep = pos < cap
            dest = jnp.where(keep, fe * cap + pos, E * cap)
            tok = jnp.arange(N * K, dtype=jnp.int32) // K
            buf_tok = jnp.full((E * cap + 1,), N, jnp.int32).at[dest].set(tok)[:-1]
            buf_w = jnp.zeros((E * cap + 1,), x.dtype).at[dest].set(w.reshape(-1))[:-1]
            xp = jnp.concatenate([xf, jnp.zeros((1, DIM), x.dtype)], axis=0)
            xe = xp[buf_tok].reshape(E, cap, DIM)
            h = jax.nn.silu(jnp.einsum('ecd,edh->ech', xe, w1)) * jnp.einsum('ecd,edh->ech', xe, w3)
            out = jnp.einsum('ech,ehd->ecd', h, w2) * buf_w.reshape(E, cap, 1)
            y = jnp.zeros((N + 1, DIM), x.dtype).at[buf_tok].add(out.reshape(E * cap, DIM))[:N]
            z = jax.nn.silu(xf @ sw1) * (xf @ sw3) @ sw2
            return (y + z).reshape(shape)
        return _forward(x, wg, w1, w2, w3, sw1, sw2, sw3)

    def _L1_cond_ref(x, cat_ids, W, b):
        import jax, jax.numpy as jnp
        import numpy as np
        C, I, O = (32, 256, 256)
        B, T = (64, 128)
        selected_W = W[cat_ids]
        selected_b = b[cat_ids]
        if x.ndim == 2:
            return jnp.einsum('bi,bio->bo', x, selected_W) + selected_b
        return jnp.einsum('bti,bio->bto', x, selected_W) + selected_b[:, None, :]

    def _L1_ffn_ref(x, ln1_g, ln1_b, Wqkv, Wproj, ln2_g, ln2_b, Wgate, W1, b1, W2, b2):
        import jax, jax.numpy as jnp
        import numpy as np
        import math
        B, T, D, H, E, TOPK, CAPF = (4, 512, 256, 16, 8, 2, 2.0)
        HD = D // H

        def layernorm(x, g, b, eps=1e-05):
            m = jnp.mean(x, -1, keepdims=True)
            v = jnp.mean(jnp.square(x - m), -1, keepdims=True)
            return (x - m) * jax.lax.rsqrt(v + eps) * g + b

        def block_forward(x, ln1_g, ln1_b, Wqkv, Wproj, ln2_g, ln2_b, Wgate, W1, b1, W2, b2):
            Bb, Tt, d = x.shape
            hd = HD
            half = hd // 2
            h = layernorm(x, ln1_g, ln1_b)
            qkv = (h @ Wqkv).reshape(Bb, Tt, H, 3 * hd)
            q, k, v = (qkv[..., :hd], qkv[..., hd:2 * hd], qkv[..., 2 * hd:])
            inv_freq = 1.0 / 10000.0 ** (jnp.arange(0, hd, 2, dtype=jnp.float32) / hd)
            ang = jnp.arange(Tt, dtype=jnp.float32)[:, None] * inv_freq
            sin = jnp.sin(ang)[None, :, None, :].astype(x.dtype)
            cos = jnp.cos(ang)[None, :, None, :].astype(x.dtype)

            def rope(t):
                t1, t2 = (t[..., :half], t[..., half:])
                return jnp.concatenate([t1 * cos - t2 * sin, t1 * sin + t2 * cos], -1)
            q, k = (rope(q), rope(k))
            scores = jnp.einsum('bqhd,bkhd->bhqk', q, k) / math.sqrt(hd)
            causal = jnp.tril(jnp.ones((Tt, Tt), dtype=bool))
            scores = jnp.where(causal, scores, jnp.asarray(-1000000000.0, scores.dtype))
            probs = jax.nn.softmax(scores, axis=-1)
            attn = jnp.einsum('bhqk,bkhd->bqhd', probs, v).reshape(Bb, Tt, d) @ Wproj
            x = x + attn
            h2 = layernorm(x, ln2_g, ln2_b)
            flat = h2.reshape(-1, d)
            N = flat.shape[0]
            capacity = int(math.ceil(CAPF * N / E))
            gates = jax.nn.softmax((flat @ Wgate).astype(jnp.float32), -1).astype(flat.dtype)
            _, top_inds = jax.lax.top_k(gates, TOPK)
            mask = jnp.zeros((N, E), dtype=bool).at[jnp.arange(N)[:, None], top_inds].set(True)
            pos = jnp.cumsum(mask.astype(jnp.int32), axis=0) * mask - 1
            keep = (pos < capacity) & mask
            t_flat = jnp.repeat(jnp.arange(N), TOPK)
            e_flat = top_inds.reshape(-1)
            p = pos[t_flat, e_flat]
            kp = keep[t_flat, e_flat]
            p_eff = jnp.where(kp, p, capacity)
            exp_in = jnp.zeros((E, capacity, d), flat.dtype).at[e_flat, p_eff].set(flat[t_flat], mode='drop')
            hmid = jax.nn.gelu(jnp.einsum('ecd,edf->ecf', exp_in, W1) + b1[:, None, :], approximate=False)
            exp_out = jnp.einsum('ecf,efd->ecd', hmid, W2) + b2[:, None, :]
            gate = gates[t_flat, e_flat] * kp.astype(flat.dtype)
            p_g = jnp.minimum(p_eff, capacity - 1)
            moe = jnp.zeros((N, d), flat.dtype).at[t_flat].add(exp_out[e_flat, p_g] * gate[:, None])
            return x + moe.reshape(Bb, Tt, d)
        return block_forward(x, ln1_g, ln1_b, Wqkv, Wproj, ln2_g, ln2_b, Wgate, W1, b1, W2, b2)
    x = x + _L0_ffn_ref(_L0_cond_ref(x, L0_cond_W1, L0_cond_b1, L0_cond_v, itok_B_0_2), L0_ffn_wg, L0_ffn_w1, L0_ffn_w2, L0_ffn_w3, L0_ffn_sw1, L0_ffn_sw2, L0_ffn_sw3)
    x = x + _L1_ffn_ref(_L1_cond_ref(x, itok_B_0_30, L1_cond_W, L1_cond_b), L1_ffn_ln1_g, L1_ffn_ln1_b, L1_ffn_Wqkv, L1_ffn_Wproj, L1_ffn_ln2_g, L1_ffn_ln2_b, L1_ffn_Wgate, L1_ffn_W1, L1_ffn_b1, L1_ffn_W2, L1_ffn_b2)
    return x

_drawn_inputs = setup_inputs


def setup_inputs(seed=0):
    import zlib

    import numpy as np

    out = dict(_drawn_inputs(seed))
    spreads = {'L1_cond_b': (0.0, 0.1),
     'L1_ffn_ln1_g': (1.0, 0.6),
     'L1_ffn_ln1_b': (0.0, 0.715),
     'L1_ffn_ln2_g': (1.0, 0.6),
     'L1_ffn_ln2_b': (0.0, 0.569),
     'L1_ffn_b1': (0.0, 0.8),
     'L1_ffn_b2': (0.0, 0.353)}
    factors = {'L0_cond_W1': 8.0,
     'L0_cond_b1': 64.0,
     'L0_cond_v': 8.0,
     'L0_ffn_wg': 3.482,
     'L0_ffn_w1': 3.616,
     'L0_ffn_w2': 3.364,
     'L0_ffn_w3': 3.113,
     'L0_ffn_sw1': 2.865,
     'L0_ffn_sw2': 2.818,
     'L0_ffn_sw3': 2.843}
    for name, (base, spread) in spreads.items():
        noise = np.random.default_rng([zlib.crc32(name.encode()), seed]).standard_normal(out[name].shape)
        drawn = base * np.exp(spread * noise) if base else spread * noise
        out[name] = jnp.asarray(drawn.astype(out[name].dtype))
    for name, factor in factors.items():
        out[name] = (out[name] * factor).astype(out[name].dtype)
    return out
```

```python
from contextlib import ExitStack

import numpy as np

import concourse.bass as bass
from concourse import mybir

F32 = mybir.dt.float32
BF16 = mybir.dt.bfloat16
I32 = mybir.dt.int32
U32 = mybir.dt.uint32
ALU = mybir.AluOpType
ACT = mybir.ActivationFunctionType
AX = mybir.AxisListType

P = 128
B, T, D = 16, 256, 256
N = B * T
NT = N // P
TB = T // P
DC = D // P
A0 = 64
E0, K0, G0, KG0 = 32, 4, 8, 4
CAP0 = int(1.25 * N * K0 / E0)
S0 = E0 * CAP0
E1, K1 = 8, 2
CAP1 = -(-2 * N // E1)
S1 = E1 * CAP1
F1 = 4 * D
H, HD = 16, 16
HP = 32
HG = P // HP
NG = H // HG
EPS = 1e-5
NEG = -1e30


class Mark:

    def __init__(self, sem, value):
        self.sem, self.value = sem, value


class Queue:

    def __init__(self, new_sem, name):
        self.new_sem, self.name = new_sem, name
        self.steps, self.seen, self.last = [], {}, None

    def stage(self, what):
        self.sem, self.count = self.new_sem(f"{self.name}_{what}"), 0

    def wait(self, *marks):
        for m in marks:
            if m is not None and self.seen.get(id(m.sem), 0) < m.value:
                self.seen[id(m.sem)] = m.value
                self.steps.append(lambda e, m=m: e.wait_ge(m.sem, m.value))

    def run(self, fn, *marks):
        self.wait(*marks)
        self.steps.append(fn)

    def mark(self, fn, *marks):
        self.wait(*marks)
        self.count += 1
        self.last = Mark(self.sem, self.count)
        self.steps.append(lambda e, s=self.sem: fn(e).then_inc(s, 1))
        return self.last

    def chain(self, fn, *marks):
        return self.mark(fn, self.last, *marks)

    def play(self, engine):
        for step in self.steps:
            step(engine)


class Lane:

    def __init__(self, sem):
        self.sem, self.count = sem, 0

    def dma(self, queue, fn, *marks):
        queue.wait(*marks)
        self.count += 16
        queue.steps.append(lambda e: fn(e).then_inc(self.sem, 16))
        return Mark(self.sem, self.count)


def wide(ap, axis, shape):
    return ap.unsqueeze(axis).broadcast_to(shape)


def shape_constants():
    p = np.arange(P)
    ident = np.eye(P, dtype=np.float32)
    before = (p[:, None] < p[None, :]).astype(np.float32)
    j = np.arange(T).reshape(TB, P).T[:, :, None]
    l = np.arange(T)[None, None, :]
    add = [np.where(m, 0.0, NEG) for m in (l <= j, l >= j, l != j)]
    cnt = [m.sum(-1) * 1.0 for m in (l <= j, l >= j, l != j)]
    pool = np.stack([add[2], add[0] - add[2], add[1] - add[2]], 1).astype(np.float32)
    cnts = np.stack([cnt[2], cnt[0] - cnt[2], cnt[1] - cnt[2]], 1).astype(np.float32)
    inv = (1.0 / 10000.0 ** (np.arange(0, HD, 2, dtype=np.float32) / HD)).astype(np.float32)
    ang = np.arange(T, dtype=np.float32)[:, None] * inv
    cs = np.stack([np.cos(ang), np.sin(ang)]).astype(np.float32)
    rope = np.stack([cs / np.float32(HD ** 0.5), cs], 1)
    rope = rope.reshape(2, 2, TB, P, HD // 2).transpose(3, 2, 0, 1, 4)
    tri_q = np.where(p[None, :] > p[:, None], -1e9, 0.0)
    z = np.zeros((P, P))
    causal = np.stack([
        np.concatenate([z, tri_q, z, tri_q], 1), np.concatenate([tri_q] * 4, 1),
        np.concatenate([tri_q.T, z, tri_q.T, z], 1), np.concatenate([tri_q.T] * 4, 1)], 1)
    heads = (p[:, None] // HP == np.arange(HG)[None, :]).astype(np.float32)
    small = np.concatenate([
        np.tile(np.arange(G0), (P, 1)), np.tile(np.arange(E0), (P, 1)),
        np.tile(np.arange(E0) * CAP0 - S0, (P, 1)), np.tile(np.arange(E1) * CAP1 - S1, (P, 1)),
        p[:, None] + P * np.arange(DC)[None, :], heads], 1)
    f = lambda a: np.ascontiguousarray(a, dtype=np.float32)
    return {"c_ident": f(ident), "c_before": f(before), "c_pool": f(pool), "c_cnt": f(cnts),
            "c_rope": f(rope), "c_causal": f(causal), "c_small": f(small)}


def bass_adaln_ffn(nc, io, out, debug=None):
    ctx = ExitStack()
    with ctx:
        return _build(nc, ctx, io, out, debug)


def _build(nc, ctx, io, out, debug):
    def sem(name):
        return ctx.enter_context(nc.semaphore(name))

    def lanes(name, n):
        return [Lane(sem(f"{name}{i}")) for i in range(n)]

    def sb(name, shape, dt=F32, scope=ctx):
        return scope.enter_context(nc.sbuf_tensor(name, shape, dt))

    pe, act, dve, pool, sp = (Queue(sem, n) for n in ("pe", "act", "dve", "pool", "sp"))
    engines = [pe, act, dve, pool]

    def stage(name):
        for q in engines:
            q.stage(name)

    def meet(*queues):
        ends = [q.last for q in queues]
        for q in queues:
            q.wait(*ends)

    stage("pool0")
    PS = ctx.enter_context(nc.psum_tensor("banks", [P, 8, 512], F32))

    slots0 = nc.dram_tensor("slots0", (S0, D), F32, kind="Internal").ap()
    done0 = nc.dram_tensor("done0", (S0 + 1, D), F32, kind="Internal").ap()
    slots1 = nc.dram_tensor("slots1", (S1, D), F32, kind="Internal").ap()
    done1 = nc.dram_tensor("done1", (S1 + 1, D), F32, kind="Internal").ap()

    X = sb("X", [P, NT, D])
    BIG = sb("BIG", [P, DC * N])
    XFT = BIG[:, :].rearrange("p (c n) -> p c n", c=DC)
    ident = sb("ident", [P, P])
    before = sb("before", [P, P])
    ones = sb("ones", [P, P])
    small = sb("small", [P, G0 + 2 * E0 + E1 + DC + HG])
    iota = small[:, G0:G0 + E0]
    base0 = small[:, G0 + E0:G0 + 2 * E0]
    base1 = small[:, G0 + 2 * E0:G0 + 2 * E0 + E1]
    rows = small[:, G0 + 2 * E0 + E1:G0 + 2 * E0 + E1 + DC]
    heads = small[:, G0 + 2 * E0 + E1 + DC:]
    w_pick0 = sb("w_pick0", [P, NT, K0])
    slot0 = sb("slot0", [P, NT, K0], U32)
    w_pick1 = sb("w_pick1", [P, NT, K1])
    slot1 = sb("slot1", [P, NT, K1], U32)
    cat_row = sb("cat_row", [P, B, DC], U32)
    cat_id = sb("cat_id", [P, B], U32)
    nhalf = sb("nhalf", [P, TB])
    epsc = EPS

    consts = Lane(sem("consts_in"))
    for dst, name in ((ident, "c_ident"), (before, "c_before"), (small, "c_small")):
        c_base = consts.dma(sp, lambda e, d=dst, n=name: e.dma_start(d[:, :], io[n]))
    x_in = lanes("x_in", 4)
    x_v = io["x"].rearrange("b (c p) d -> p (b c) d", p=P)
    x_ready = {}

    def load_x(q, w):
        x_ready[q] = x_in[q].dma(sp, lambda e: e.dma_start(
            X[:, q * 8:q * 8 + w, :], x_v[:, q * 8:q * 8 + w, :]))

    region = ExitStack()
    ctx.enter_context(region)
    s = region
    w1c = sb("w1c", [P, DC, A0], scope=s)
    b1c = sb("b1c", [A0, 1], scope=s)
    vc = sb("vc", [A0, 1], scope=s)
    vb = sb("vb", [A0, P], scope=s)
    wgT = sb("wgT", [P, DC, E0], scope=s)
    poolc = sb("poolc", [P, 3, TB, T], scope=s)
    cntc = sb("cntc", [P, 3, TB], scope=s)
    ids_i = sb("ids_i", [P, 2, B], I32, scope=s)
    ids = sb("ids", [P, 2, B], scope=s)
    kind = sb("kind", [P, 2, B], scope=s)
    cnt = sb("cnt", [P, B, TB], scope=s)
    cat_f = sb("cat_f", [P, B, DC], scope=s)
    zeros = sb("zeros", [P, 4096], scope=s)
    xT = sb("xT", [P, 2, DC, T], scope=s)
    aT = sb("aT", [A0, 2, T], scope=s)
    mask = sb("mask", [P, 2, TB, T], scope=s)
    msc = sb("msc", [P, 2, TB, T], scope=s)
    pr = sb("pr", [P, 2, TB, T], scope=s)
    nmax = sb("nmax", [P, 2, TB], scope=s)
    psum_ = sb("psum_", [P, 2, TB], scope=s)
    pinv = sb("pinv", [P, 2, TB], scope=s)
    prT = sb("prT", [P, 2, TB, T], scope=s)
    NXF = 8
    XF = sb("XF", [P, NXF, TB, D], scope=s)

    load_x(0, 8)
    cond_in = Lane(sem("cond_in"))
    for dst, src in ((w1c, io["L0_cond_W1"].rearrange("(c p) a -> p c a", p=P)), (b1c, io["L0_cond_b1"]),
                     (vc, io["L0_cond_v"]), (wgT, io["L0_ffn_wgT"].rearrange("(c p) e -> p c e", p=P)),
                     (poolc, io["c_pool"]), (cntc, io["c_cnt"])):
        c_cond = cond_in.dma(sp, lambda e, d=dst, s_=src: e.dma_start(d[tuple([slice(None)] * len(d.shape))], s_))
    c_cond = cond_in.dma(sp, lambda e: e.dma_start(ids_i[:, 0, :], io["itok_B_0_2"].partition_broadcast(P)))
    c_cond = cond_in.dma(sp, lambda e: e.dma_start(ids_i[:, 1, :], io["itok_B_0_30"].partition_broadcast(P)))
    for q in range(1, 4):
        load_x(q, 8)

    m_ones = pool.mark(lambda e: e.memset(ones[:, :], 1.0))
    m_zero = pool.mark(lambda e: e.memset(zeros[:, :], 0.0))
    m_nhalf = pool.mark(lambda e: e.memset(nhalf[:, :], -0.5))
    dve.chain(lambda e: e.tensor_copy(ids[:, :, :], ids_i[:, :, :]), c_cond)
    for i in range(2):
        m = dve.mark(lambda e, i=i: e.tensor_scalar(kind[:, i, :], ids[:, 0, :], float(i), None, ALU.is_equal), dve.last)
    for c in range(TB):
        dve.chain(lambda e, c=c: e.tensor_scalar(cnt[:, :, c], kind[:, 0, :], cntc[:, 1, c:c + 1], cntc[:, 0, c:c + 1],
                                                 ALU.mult, ALU.add))
        dve.chain(lambda e, c=c: e.scalar_tensor_tensor(cnt[:, :, c], kind[:, 1, :], cntc[:, 2, c:c + 1],
                                                        cnt[:, :, c], ALU.mult, ALU.add))
    for c in range(DC):
        dve.chain(lambda e, c=c: e.tensor_scalar(cat_f[:, :, c], ids[:, 1, :], float(D), rows[:, c:c + 1],
                                                 ALU.mult, ALU.add))
    dve.chain(lambda e: e.tensor_copy(cat_row[:, :, :], cat_f[:, :, :]))
    m_cat = dve.chain(lambda e: e.tensor_copy(cat_id[:, :], ids[:, 1, :]))
    m_vb = dve.mark(lambda e: e.tensor_copy(vb[:, :], vc[:, :].broadcast_to([A0, P])))

    def fill_rows(dst, n, fill):
        m = None
        per = 4096 // D
        v = dst[0:n, :].rearrange("(k p r) d -> k p (r d)", p=P, r=per)
        for k in range(n // (P * per)):
            m = fill.dma(sp, lambda e, k=k: e.dma_start(v[k], zeros[:, :]), m_zero)
        return m
    filled0 = fill_rows(slots0, S0, Lane(sem("fill0")))
    fill_last = Lane(sem("fill_last"))
    for t_, n_ in ((done0, S0), (done1, S1)):
        fill_end = fill_last.dma(sp, lambda e, t_=t_, n_=n_: e.dma_start(t_[n_:n_ + 1, :], zeros[0:1, 0:D]))
    filled1 = fill_rows(slots1, S1, Lane(sem("fill1")))

    M = {}

    def transposes(bank, src, waits):
        for c in range(DC):
            for t in range(TB):
                fn = lambda e, c=c, t=t: e.transpose(PS[:, bank, c * T + t * P:c * T + (t + 1) * P],
                                                     src(t)[:, c * P:(c + 1) * P], ident[:, :])
                if c == DC - 1 and t == TB - 1:
                    return pe.mark(fn, *waits)
                pe.run(fn, *waits)

    def bank2(bank, n=T):
        return PS[:, bank, :].rearrange("p (a n) -> p a n", n=n)

    def p_transpose(b):
        m = transposes(0, lambda t: X[:, TB * b + t, :], [c_base, x_ready[b // 4], M.get(("xT", b - 1))])
        M["xT", b] = act.mark(lambda e: e.activation(xT[:, b % 2, :, :], bank2(0), ACT.Copy), m, M.get(("hid", b - 2)))

    def p_hidden(b):
        for c in range(DC):
            fn = lambda e, c=c: e.matmul(PS[0:A0, 1, 0:T], w1c[:, c, :], xT[:, b % 2, c, :], start=(c == 0), stop=(c == DC - 1))
            if c < DC - 1:
                pe.run(fn, M["xT", b], M.get(("aT", b - 1)), c_cond)
        M["hid", b] = m = pe.mark(fn)
        M["aT", b] = act.mark(lambda e: e.activation(aT[:, b % 2, :], PS[0:A0, 1, 0:T], ACT.Tanh, bias=b1c[:, 0:1]),
                              m, c_cond, M.get(("sc", b - 2)))

    def p_mask(b):
        i = b % 2
        dve.mark(lambda e: e.scalar_tensor_tensor(mask[:, i, :, :], poolc[:, 1, :, :], kind[:, 0, b:b + 1],
                                                  poolc[:, 0, :, :], ALU.mult, ALU.add), M.get(("msc", b - 2)))
        M["mask", b] = dve.chain(lambda e: e.scalar_tensor_tensor(mask[:, i, :, :], poolc[:, 2, :, :], kind[:, 1, b:b + 1],
                                                                  mask[:, i, :, :], ALU.mult, ALU.add))

    def p_scores(b):
        i = b % 2
        M["sc", b] = m = pe.mark(lambda e: e.matmul(PS[:, 2, 0:T], vb[:, :], aT[:, i, :], start=True, stop=True),
                                 M["aT", b], m_vb, M.get(("msc", b - 1)))
        M["msc", b] = dve.mark(lambda e: e.tensor_tensor(msc[:, i, :, :], mask[:, i, :, :], wide(PS[:, 2, 0:T], 1, [P, TB, T]),
                                                         ALU.add), m, M["mask", b], M.get(("exp", b - 2)))
        m = dve.chain(lambda e: e.tensor_reduce(nmax[:, i, :], msc[:, i, :, :], AX.X, ALU.max, negate=True))
        for c in range(TB):
            m2 = act.mark(lambda e, c=c: e.activation(pr[:, i, c, :], msc[:, i, c, :], ACT.Exp, bias=nmax[:, i, c:c + 1],
                                                      accum_out=psum_[:, i, c:c + 1]), m, M.get(("prT_pe", b - 2)),
                          M.get(("pinv", b - 2)))
        M["exp", b] = m2

    def p_turn(b):
        i = b % 2
        m = None
        for lc in range(TB):
            for jc in range(TB):
                fn = lambda e, lc=lc, jc=jc: e.transpose(PS[:, 3, lc * T + jc * P:lc * T + (jc + 1) * P],
                                                         pr[:, i, jc, lc * P:(lc + 1) * P], ident[:, :])
                if lc == TB - 1 and jc == TB - 1:
                    m = pe.mark(fn)
                else:
                    pe.run(fn, M["exp", b], M.get(("prT", b - 1)))
        M["prT_pe", b] = m
        M["prT", b] = dve.mark(lambda e: e.tensor_copy(prT[:, i, :, :], bank2(3)), m, M.get(("mix", b - 2)))
        dve.mark(lambda e: e.tensor_tensor(psum_[:, i, :], psum_[:, i, :], cnt[:, b, :], ALU.mult), M["exp", b])
        M["pinv", b] = dve.chain(lambda e: e.reciprocal(pinv[:, i, :], psum_[:, i, :]))

    def p_mix(b):
        i = b % 2
        for jc in range(TB):
            for lc in range(TB):
                fn = lambda e, jc=jc, lc=lc: e.matmul(PS[:, 4, jc * D:(jc + 1) * D], prT[:, i, lc, jc * P:(jc + 1) * P],
                                                      X[:, TB * b + lc, :], start=(lc == 0), stop=(lc == TB - 1))
                if jc == TB - 1 and lc == TB - 1:
                    M["mix", b] = m = pe.mark(fn)
                else:
                    pe.run(fn, M["prT", b], M.get(("XF", b - 1)))
        M["XF", b] = dve.mark(lambda e: e.tensor_tensor(XF[:, b % NXF, :, :], bank2(4), wide(pinv[:, i, :], 2, [P, TB, D]),
                                                        ALU.mult), m, M["pinv", b], M.get(("scat", b - NXF)))

    def p_turn_back(b):
        m = transposes(5, lambda t: XF[:, b % NXF, t, :], [M["XF", b], M.get(("XFT", b - 1))])
        M["XFT", b] = act.mark(lambda e: e.activation(XFT[:, :, b * T:(b + 1) * T], bank2(5), ACT.Copy), m)

    R = 4

    class Router:

        def __init__(self, scope, tag, E, K, groups, cap, base, weights, slots):
            self.E, self.K, self.groups, self.cap, self.base = E, K, groups, cap, base
            self.weights, self.slots, self.tag = weights, slots, tag
            f = lambda n, *shape, dt=F32: sb(f"{n}_{tag}", [P, *shape], dt, scope)
            self.nm, self.sh, self.ex = f("nm", R), f("sh", R, E), f("ex", R, E)
            self.tv, self.ti, self.tf = f("tv", R, 8), f("ti", R, 8, dt=U32), f("tf", R, 8)
            self.hit = f("hit", R, K, E)
            self.sel, self.cum = f("sel", R, E), f("cum", R + 1, E)
            self.sm, self.ok, self.sf = f("sm", R, E), f("ok", R, E), f("sf", R, K)
            self.den, self.top = f("den", R), f("top", R)
            self.pick = f("pick", R, K, E)
            if groups:
                self.gs, self.gv, self.gi, self.gf = f("gs", R, groups), f("gv", R, 8), f("gi", R, 8, dt=U32), f("gf", R, 8)
                self.ghit, self.gk, self.gm = f("ghit", R, KG0, groups), f("gk", R, groups), f("gm", R, groups)
                self.cand = f("cand", R, E)
            dve.mark(lambda e: e.memset(self.cum[:, R, :], 0.0))

        def choose(self, g, logits, m_logits):
            E, K, t0 = self.E, self.K, g * R
            S3 = [P, R, E]
            dve.chain(lambda e: e.tensor_reduce(self.nm[:, :], logits, AX.X, ALU.max, negate=True), m_logits)
            m = dve.chain(lambda e: e.tensor_tensor(self.sh[:, :, :], logits, wide(self.nm[:, :], 2, S3), ALU.add))
            m = act.mark(lambda e: e.activation(self.ex[:, :, :], self.sh[:, :, :], ACT.Exp), m)
            M["choose_free" + self.tag] = dve.last
            dve.wait(m)
            cand = self.ex
            if self.groups:
                G = self.groups
                dve.mark(lambda e: e.tensor_reduce(self.gs[:, :, :], self.ex[:, :, :].rearrange("p r (g k) -> p r g k", g=G),
                                                   AX.X, ALU.max))
                for r in range(R):
                    dve.chain(lambda e, r=r: e.max(self.gv[:, r, :], self.gs[:, r, :]))
                for r in range(R):
                    dve.chain(lambda e, r=r: e.max_index(self.gi[:, r, :], self.gv[:, r, :], self.gs[:, r, :]))
                dve.chain(lambda e: e.tensor_copy(self.gf[:, :, :], self.gi[:, :, :]))
                dve.chain(lambda e: e.tensor_tensor(self.ghit[:, :, :, :], wide(wide(iota[:, 0:G], 1, [P, R, G]), 2, [P, R, KG0, G]),
                                                    wide(self.gf[:, :, 0:KG0], 3, [P, R, KG0, G]), ALU.is_equal))
                dve.chain(lambda e: e.tensor_reduce(self.gk[:, :, :], self.ghit[:, :, :, :].rearrange("p r k g -> p r g k"),
                                                    AX.X, ALU.add))
                dve.chain(lambda e: e.tensor_scalar(self.gm[:, :, :], self.gk[:, :, :], -1.0, None, ALU.add))
                v4 = lambda a: a[:, :, :].rearrange("p r (g k) -> p r g k", g=G)
                SG = [P, R, G, E // G]
                dve.chain(lambda e: e.tensor_tensor(v4(self.cand), v4(self.ex), wide(self.gk[:, :, :], 3, SG), ALU.mult))
                dve.chain(lambda e: e.tensor_tensor(v4(self.cand), v4(self.cand), wide(self.gm[:, :, :], 3, SG), ALU.add))
                cand = self.cand
            for r in range(R):
                dve.chain(lambda e, r=r: e.max(self.tv[:, r, :], cand[:, r, :]))
            for r in range(R):
                dve.chain(lambda e, r=r: e.max_index(self.ti[:, r, :], self.tv[:, r, :], cand[:, r, :]))
            dve.chain(lambda e: e.tensor_copy(self.tf[:, :, :], self.ti[:, :, :]))
            S4 = [P, R, K, E]
            dve.chain(lambda e: e.tensor_tensor(self.hit[:, :, :, :], wide(wide(iota[:, 0:E], 1, S3), 2, S4),
                                                wide(self.tf[:, :, 0:K], 3, S4), ALU.is_equal))
            m_sel = dve.chain(lambda e: e.tensor_reduce(self.sel[:, :, :], self.hit[:, :, :, :].rearrange("p r k e -> p r e k"),
                                                        AX.X, ALU.add), M.get(("rank" + self.tag, g - 1)))
            m_cum = dve.chain(lambda e: e.tensor_copy(self.cum[:, 0, :], self.cum[:, R, :]))
            for r in range(R):
                m_cum = dve.chain(lambda e, r=r: e.tensor_tensor(self.cum[:, r + 1, :], self.cum[:, r, :], self.sel[:, r, :], ALU.add))
            M["sel" + self.tag, g] = m_cum
            dve.mark(lambda e: e.tensor_reduce(self.den[:, :], self.ex[:, :, :], AX.X, ALU.add))
            if self.groups:
                dve.mark(lambda e: e.tensor_reduce(self.top[:, :], self.tv[:, :, 0:K], AX.X, ALU.add))
                dve.chain(lambda e: e.scalar_tensor_tensor(self.den[:, :], self.den[:, :], 1e-9, self.top[:, :], ALU.mult, ALU.add))
            dve.chain(lambda e: e.reciprocal(self.den[:, :], self.den[:, :]))
            M["w" + self.tag, g] = dve.chain(lambda e: e.tensor_tensor(
                self.weights[:, t0:t0 + R, :], self.tv[:, :, 0:K], wide(self.den[:, :], 2, [P, R, K]), ALU.mult))

        def rank(self, g, bank):
            E, K, t0 = self.E, self.K, g * R
            for r in range(R):
                o = PS[:, bank, r * E:(r + 1) * E]
                pe.run(lambda e, r=r, o=o: e.matmul(o, before[:, :], self.sel[:, r, :], start=True, stop=False),
                       M["sel" + self.tag, g], M.get(("slot" + self.tag, g - 1)), m_ones)
                fn = lambda e, r=r, o=o: e.matmul(o, ones[:, :], self.cum[:, r, :], start=False, stop=True)
                if r < R - 1:
                    pe.run(fn)
            M["rank" + self.tag, g] = m = pe.mark(fn)
            pos = PS[:, bank, 0:R * E].rearrange("p (r e) -> p r e", r=R)
            S3, S4 = [P, R, E], [P, R, K, E]
            dve.mark(lambda e: e.tensor_scalar(self.ok[:, :, :], pos, float(self.cap), None, ALU.is_lt), m)
            dve.mark(lambda e: e.tensor_tensor(self.sm[:, :, :], pos, wide(self.base, 1, S3), ALU.add))
            dve.chain(lambda e: e.tensor_tensor(self.sm[:, :, :], self.sm[:, :, :], self.ok[:, :, :], ALU.mult))
            dve.chain(lambda e: e.tensor_tensor(self.pick[:, :, :, :], self.hit[:, :, :, :], wide(self.sm[:, :, :], 2, S4), ALU.mult))
            dve.chain(lambda e: e.tensor_reduce(self.sf[:, :, :], self.pick[:, :, :, :], AX.X, ALU.add))
            M["slot" + self.tag, g] = dve.chain(lambda e: e.tensor_scalar(
                self.slots[:, t0:t0 + R, :], self.sf[:, :, :], float(self.cap * E), None, ALU.add))

    router0 = Router(region, "0", E0, K0, G0, CAP0, base0, w_pick0, slot0)
    GB = R // TB
    scat0 = lanes("scat0_", NXF)

    def p_logits(b):
        for t in range(TB):
            r = (TB * b + t) % R
            for c in range(DC):
                fn = lambda e, t=t, c=c, r=r: e.matmul(
                    PS[:, 6, r * E0:(r + 1) * E0], XFT[:, c, (TB * b + t) * P:(TB * b + t + 1) * P], wgT[:, c, :],
                    start=(c == 0), stop=(c == DC - 1))
                if t == TB - 1 and c == DC - 1:
                    M["lg", b] = pe.mark(fn)
                else:
                    pe.run(fn, M["XFT", b], M.get("choose_free0"))
        if b % GB == GB - 1:
            router0.choose(b // GB, PS[:, 6, 0:R * E0].rearrange("p (r e) -> p r e", r=R), M["lg", b])

    def p_dispatch(b):
        if b % GB != GB - 1:
            return
        g = b // GB
        router0.rank(g, 7)
        for bb in range(b - GB + 1, b + 1):
            for t in range(TB):
                for k in range(K0):
                    M["scat", bb] = scat0[bb % NXF].dma(pool, lambda e, bb=bb, t=t, k=k: e.indirect_dma_start(
                        slots0, bass.IndirectOffsetOnAxis(ap=slot0[:, TB * bb + t, k:k + 1], axis=0),
                        XF[:, bb % NXF, t, :], None, bounds_check=S0 - 1, oob_is_err=False),
                        M["slot0", g], M["XF", bb], filled0)

    steps = [p_transpose, p_hidden, p_scores, p_turn, p_mix, p_turn_back, p_logits, p_dispatch]
    for b in range(2):
        p_mask(b)
    for t in range(B + len(steps) - 1):
        for k in reversed(range(len(steps))):
            if 0 <= t - k < B:
                steps[k](t - k)
                if steps[k] is p_scores and t - k + 2 < B:
                    p_mask(t - k + 2)

    stage("shared")
    NW0 = 3
    NXE = 3
    w0 = sb("w0", [P, NW0, 3, DC, D], scope=s)
    xe = sb("xe", [P, NXE, CAP0 // P, D], scope=s)
    xeT = sb("xeT", [P, 2, DC * CAP0], scope=s)
    gate = sb("gate", [P, 2, 512], scope=s)
    hT = sb("hT", [P, 2, 2, CAP0], scope=s)
    res = sb("res", [P, 2, CAP0 // P, D], scope=s)
    w_in = lanes("w_in", NW0)
    xe_in = lanes("xe_in", NXE)
    res_out = lanes("res_out", 2)

    def load_w0(n, srcs, *marks):
        for i, src in enumerate(srcs):
            m = w_in[n % NW0].dma(sp, lambda e, i=i, src=src: e.dma_start(
                w0[:, n % NW0, i, :, :], src.rearrange("(c p) f -> p c f", p=P)), *marks)
        return m

    W0 = {0: load_w0(0, [io["L0_ffn_sw1"], io["L0_ffn_sw3"], io["L0_ffn_sw2"]])}
    for n in (1, 2):
        W0[n] = load_w0(n, [io[f"L0_ffn_w{i}"][n - 1] for i in (1, 3, 2)])

    meet(pe, act, dve)
    CH = 512
    gate_free = {}
    unit = 0
    free_h = [None, None]
    free_o = [None, None]

    def up_unit(wslot, hc, src, n, dst, waits, hT_free):
        nonlocal unit
        i = unit % 2
        unit += 1
        for j in range(2):
            for c in range(DC):
                fn = lambda e, j=j, c=c: e.matmul(PS[:, 2 * i + j, 0:n], w0[:, wslot, j, c, hc * P:(hc + 1) * P], src(c),
                                                  start=(c == 0), stop=(c == DC - 1))
                if c == DC - 1:
                    m = pe.mark(fn)
                else:
                    pe.run(fn, *waits, free_h[i])
                if c == DC - 1 and j == 0:
                    m_gate = m
        m1 = act.mark(lambda e: e.activation(gate[:, i, 0:n], PS[:, 2 * i, 0:n], ACT.Silu), m_gate, gate_free.get(i))
        m2 = dve.mark(lambda e: e.tensor_tensor(dst, gate[:, i, 0:n], PS[:, 2 * i + 1, 0:n], ALU.mult), m1, m, *hT_free)
        gate_free[i] = free_h[i] = m2
        return m2

    z_down = {}
    for k in range(N // CH + 1):
        if k < N // CH:
            for hc in range(2):
                up = up_unit(0, hc, lambda c, k=k: XFT[:, c, k * CH:(k + 1) * CH], CH, hT[:, k % 2, hc, 0:CH],
                             [W0[0]], [z_down.get(k - 2)])
            M["zh", k] = up
        if k > 0:
            kk = k - 1
            for u in range(CH // P // 2):
                i = 4 + u
                for t in range(2):
                    for hc in range(2):
                        fn = lambda e, u=u, t=t, hc=hc, i=i, kk=kk: e.matmul(
                            PS[:, i, t * D:(t + 1) * D], hT[:, kk % 2, hc, (2 * u + t) * P:(2 * u + t + 1) * P],
                            w0[:, 0, 2, hc, :], start=(hc == 0), stop=(hc == 1))
                        if t == 1 and hc == 1:
                            m = pe.mark(fn)
                        else:
                            pe.run(fn, M["zh", kk], free_o[u])
                tt = kk * (CH // P) + 2 * u
                free_o[u] = dve.mark(lambda e, tt=tt, i=i: e.tensor_tensor(
                    X[:, tt:tt + 2, :], X[:, tt:tt + 2, :], bank2(i), ALU.add), m)
            z_down[kk] = m

    stage("experts0")
    meet(pe, act, dve)
    NS0 = CAP0 // P
    all_scattered = [M["scat", b] for b in range(B - NXF, B)]
    XE, O = {}, {}

    def load_xe(n):
        XE[n] = xe_in[n % NXE].dma(sp, lambda e: e.dma_start(
            xe[:, n % NXE, :, :], slots0[n * CAP0:(n + 1) * CAP0, :].rearrange("(s p) d -> p s d", p=P)),
            *all_scattered, M.get(("turned", n - NXE)))

    t_free = [None, None]

    def turn_xe(n):
        k = 0
        for u in range(-(-DC * NS0 // 4)):
            ids_ = range(4 * u, min(4 * u + 4, DC * NS0))
            for q in ids_:
                c, i = divmod(q, NS0)
                fn = lambda e, c=c, i=i, q=q, u=u: e.transpose(
                    PS[:, 4 + u % 2, (q % 4) * P:(q % 4 + 1) * P], xe[:, n % NXE, i, c * P:(c + 1) * P], ident[:, :])
                if q == ids_[-1]:
                    m = pe.mark(fn)
                else:
                    pe.run(fn, XE[n], t_free[u % 2])
            w = len(ids_) * P
            cp = lambda u=u, w=w: (xeT[:, n % 2, 4 * u * P:4 * u * P + w], PS[:, 4 + u % 2, 0:w])
            if u % 2:
                t_free[u % 2] = act.mark(lambda e, cp=cp: e.activation(*cp(), ACT.Copy), m, M.get(("up", n - 2)))
            else:
                t_free[u % 2] = dve.mark(lambda e, cp=cp: e.tensor_copy(*cp()), m, M.get(("up", n - 2)))
            M["xeT", n, u] = t_free[u % 2]
        M["turned", n] = m

    def up_expert(n):
        half = CAP0 // 2
        for hc in range(2):
            for q in range(2):
                m = up_unit((n + 1) % NW0, hc, lambda c, q=q: xeT[:, n % 2, c * CAP0 + q * half:c * CAP0 + (q + 1) * half], half,
                            hT[:, n % 2, hc, q * half:(q + 1) * half],
                            [W0[n + 1]] + [M["xeT", n, u] for u in range(3)], [M.get(("down", n - 2))])
        M["up", n] = pe.last
        M["hT", n] = m

    o_free = [None, None]

    def down_expert(n):
        for u in range(-(-NS0 // 2)):
            tiles = range(2 * u, min(2 * u + 2, NS0))
            for i in tiles:
                for hc in range(2):
                    fn = lambda e, i=i, hc=hc, u=u: e.matmul(
                        PS[:, 6 + u % 2, (i % 2) * D:(i % 2 + 1) * D], hT[:, n % 2, hc, i * P:(i + 1) * P],
                        w0[:, (n + 1) % NW0, 2, hc, :], start=(hc == 0), stop=(hc == 1))
                    if i == tiles[-1] and hc == 1:
                        m = pe.mark(fn)
                    else:
                        pe.run(fn, M["hT", n], o_free[u % 2])
            w = len(tiles)
            cp = lambda u=u, w=w: (res[:, n % 2, 2 * u:2 * u + w, :], PS[:, 6 + u % 2, 0:w * D].rearrange("p (a n) -> p a n", n=D))
            q = dve if u == 1 else act
            if q is dve:
                o_free[u % 2] = dve.mark(lambda e, cp=cp: e.tensor_copy(*cp()), m, O.get(n - 2))
            else:
                o_free[u % 2] = act.mark(lambda e, cp=cp: e.activation(*cp(), ACT.Copy), m, O.get(n - 2))
            M["res", n, u] = o_free[u % 2]
        M["down", n] = m

    def store_res(n):
        O[n] = res_out[n % 2].dma(sp, lambda e: e.dma_start(
            done0[n * CAP0:(n + 1) * CAP0, :].rearrange("(s p) d -> p s d", p=P), res[:, n % 2, :, :]),
            *[M["res", n, u] for u in range(3)])

    for n in range(2):
        load_xe(n)
    turn_xe(0)
    for n in range(E0):
        if n + 2 < E0:
            load_xe(n + 2)
        up_expert(n)
        if n + 1 < E0:
            turn_xe(n + 1)
        down_expert(n)
        if n == 0:
            W0[3] = load_w0(3, [io[f"L0_ffn_w{i}"][2] for i in (1, 3, 2)], z_down[N // CH - 1])
        if n + 4 <= E0:
            W0[n + 4] = load_w0(n + 4, [io[f"L0_ffn_w{i}"][n + 3] for i in (1, 3, 2)], M["down", n])
        store_res(n)
    all_done0 = [O[E0 - 2], O[E0 - 1]]
    region.close()

    stage("attn")
    meet(pe, act, dve, pool)
    region = ExitStack()
    ctx.enter_context(region)
    s = region
    ends = (pe.last, act.last, dve.last, pool.last)
    for q in (sp, pool, act, dve):
        q.wait(*ends, *all_done0, *all_scattered)
    NGA = 2
    G0b = sb("G0b", [P, NGA, TB, K0, D], scope=s)
    WS = sb("WS", [P, 2, DC, D], scope=s)
    BS = sb("BS", [P, 2, D], scope=s)
    wqkv = sb("wqkv", [P, DC, 3 * D], scope=s)
    wproj = sb("wproj", [P, DC, D], scope=s)
    wgate = sb("wgate", [P, DC, E1], scope=s)
    lng = sb("lng", [P, 4, DC], scope=s)
    ropec = sb("ropec", [P, TB, 2, 2, HD // 2], scope=s)
    causal_f = sb("causal_f", [P, 512], scope=s)
    causal = sb("causal", [P, 4, 512], BF16, scope=s)
    ident_b = sb("ident_b", [P, P], BF16, scope=s)
    x1T = sb("x1T", [P, DC, T], scope=s)
    XC = sb("XC", [P, 3, TB, D], scope=s)
    st = sb("st", [P, 2, TB, 6], scope=s)
    mv = sb("mv", [P, 2, TB, 2], scope=s)
    ve = sb("ve", [P, 2, TB], scope=s)
    rs = sb("rs", [P, 2, TB], scope=s)
    xn = sb("xn", [P, TB, D], scope=s)
    hT1 = sb("hT1", [P, DC, T], scope=s)
    QK = sb("QK", [P, 2, TB, 2, H, HP], scope=s)
    VP = sb("VP", [P, 2, TB, H, HP], scope=s)
    rm = sb("rm", [P, 2, 2, H, HD], scope=s)
    qT = sb("qT", [P, NG, T], scope=s)
    qT2 = sb("qT2", [P, NG, T], scope=s)
    KM = sb("KM", [P, NG, HG, T], scope=s)
    NPT = 6
    PT = sb("PT", [P, NPT, 512], scope=s)
    oT = sb("oT", [P, 2, 2, T], scope=s)
    rsum = sb("rsum", [P, TB, H], scope=s)
    at = sb("at", [P, TB, H, HD], scope=s)
    atT = sb("atT", [P, DC, T], scope=s)
    XR = sb("XR", [P, 2, TB, D], scope=s)
    NXN = 4
    XN2 = sb("XN2", [P, NXN, TB, D], scope=s)
    h2T = sb("h2T", [P, DC, T], scope=s)
    router1 = Router(region, "1", E1, K1, 0, CAP1, base1, w_pick1, slot1)
    gat0 = lanes("gat0_", NGA)
    ws_in = lanes("ws_in", 2)
    scat1 = lanes("scat1_", NXN)
    attn_in = Lane(sem("attn_in"))

    for dst, src in ((wqkv[:, :, :], io["L1_ffn_WqkvT"].rearrange("(c p) f -> p c f", p=P)),
                     (wproj[:, :, :], io["L1_ffn_Wproj"].rearrange("(c p) f -> p c f", p=P)),
                     (wgate[:, :, :], io["L1_ffn_Wgate"].rearrange("(c p) f -> p c f", p=P)),
                     (lng[:, :, :], io["ln_cols"]), (ropec[:, :, :, :, :], io["c_rope"])):
        c_attn = attn_in.dma(sp, lambda e, d=dst, s_=src: e.dma_start(d, s_))
    causal_in = Lane(sem("causal_in"))
    m = None
    for i in range(4):
        ml = causal_in.dma(sp, lambda e, i=i: e.dma_start(causal_f[:, :], io["c_causal"][:, i, :]), m)
        m = dve.mark(lambda e, i=i: e.tensor_copy(causal[:, i, :], causal_f[:, :]), ml)
    m_causal = dve.mark(lambda e: e.tensor_copy(ident_b[:, :], ident[:, :]))
    m_qk0 = pool.mark(lambda e: e.memset(QK[:, :, :, :, :, :], 0.0))
    m_vp0 = pool.mark(lambda e: e.memset(VP[:, :, :, :, :], 0.0))
    m_qk0 = pool.mark(lambda e: e.memset(QK[:, :, :, 1, :, HD:HD + 1], 1.0), m_qk0)
    m_vp0 = pool.mark(lambda e: e.memset(VP[:, :, :, :, HD:HD + 1], 1.0), m_vp0)
    W_all = io["L1_cond_W"].rearrange("c i o -> (c i) o")
    w1e_in = lanes("w1e_in", 2)
    W1E = {}

    def load_w1e(n, *marks):
        v = BIG[:, (n % 2) * N:(n % 2 + 1) * N]
        w1e_in[n % 2].dma(sp, lambda e: e.dma_start(v[:, 0:DC * F1].rearrange("p (c f) -> p c f", c=DC),
                                                    io["L1_ffn_W1"][n].rearrange("(c p) f -> p c f", p=P)), *marks)
        W1E[n] = w1e_in[n % 2].dma(sp, lambda e: e.dma_start(v[:, DC * F1:].rearrange("p (c f) -> p c f", f=D),
                                                             io["L1_ffn_W2"][n].rearrange("(c p) f -> p c f", p=P)))

    load_w1e(0)
    load_w1e(1)

    misc_free = [None] * 3

    def misc(i):
        return 5 + i

    def gather(b):
        i = b % 2
        for t in range(TB):
            for k in range(K0):
                M["g0", b] = gat0[b % NGA].dma(pool, lambda e, t=t, k=k: e.indirect_dma_start(
                    G0b[:, b % NGA, t, k, :], None, done0,
                    bass.IndirectOffsetOnAxis(ap=slot0[:, TB * b + t, k:k + 1], axis=0)), M.get(("comb", b - NGA)), fill_end)
        for c in range(DC):
            ws_in[i].dma(pool, lambda e, c=c: e.indirect_dma_start(
                WS[:, i, c, :], None, W_all, bass.IndirectOffsetOnAxis(ap=cat_row[:, b, c:c + 1], axis=0)), M.get(("xc_pe", b - 2)), M.get(("xc", b - 2)))
        M["ws", b] = ws_in[i].dma(pool, lambda e: e.indirect_dma_start(
            BS[:, i, :], None, io["L1_cond_b"], bass.IndirectOffsetOnAxis(ap=cat_id[:, b:b + 1], axis=0)))

    def a_combine(b):
        for t in range(TB):
            tt = TB * b + t
            for k in range(K0):
                M["comb", b] = dve.chain(lambda e, t=t, k=k, tt=tt: e.scalar_tensor_tensor(
                    X[:, tt, :], G0b[:, b % NGA, t, k, :], w_pick0[:, tt, k:k + 1], X[:, tt, :], ALU.mult, ALU.add),
                    M["g0", b])

    def a_turn(b):
        m = transposes(misc(0), lambda t: X[:, TB * b + t, :], [M["comb", b], misc_free[0]])
        misc_free[0] = M["x1T", b] = act.mark(lambda e: e.activation(x1T[:, :, :], bank2(misc(0)), ACT.Copy), m, M.get(("xc_pe", b - 1)))

    def proj_like(bank, src, w, waits):
        for t in range(TB):
            for c in range(DC):
                fn = lambda e, t=t, c=c: e.matmul(PS[:, bank, t * D:(t + 1) * D], src[:, c, t * P:(t + 1) * P], w(c),
                                                  start=(c == 0), stop=(c == DC - 1))
                if t == TB - 1 and c == DC - 1:
                    return pe.mark(fn)
                pe.run(fn, *waits)

    def norm(src, j, dst, dst_free):
        for t in range(TB):
            dve.mark(lambda e, t=t: e.bn_stats(st[:, j, t, :], src[:, t, :]), dve.last)
        for t in range(TB):
            dve.chain(lambda e, t=t: e.bn_aggr(mv[:, j, t, :], st[:, j, t, :]))
        m = dve.chain(lambda e: e.tensor_scalar(ve[:, j, :], mv[:, j, :, 1], epsc, None, ALU.add))
        m = pool.mark(lambda e: e.tensor_tensor(rs[:, j, :], ve[:, j, :], nhalf[:, :], ALU.pow), m, m_nhalf)
        for t in range(TB):
            m2 = dve.mark(lambda e, t=t: e.tensor_scalar(dst[:, t, :], src[:, t, :], mv[:, j, t, 0:1], rs[:, j, t:t + 1],
                                                         ALU.subtract, ALU.mult), m, *dst_free)
        return m2

    def a_matrix(b):
        i = b % 2
        M["xc_pe", b] = m = proj_like(misc(1), x1T, lambda c: WS[:, i, c, :], [M["x1T", b], M["ws", b], misc_free[1]])
        misc_free[1] = M["xc", b] = dve.mark(lambda e: e.tensor_tensor(
            XC[:, b % 3, :, :], bank2(misc(1)), wide(BS[:, i, :], 1, [P, TB, D]), ALU.add), m, M.get(("xr", b - 3)))
        M["xn", b] = norm(XC[:, b % 3, :, :], 0, xn, [M.get(("xn_pe", b - 1))])

    def affine_turn(b, j, src, dst, waits, free):
        m = transposes(misc(j), src, waits)
        for c in range(DC):
            m2 = act.mark(lambda e, c=c: e.activation(dst[:, c, :], PS[:, misc(j), c * T:(c + 1) * T], ACT.Identity,
                                                      bias=lng[:, free[1] + 1, c:c + 1], scale=lng[:, free[1], c:c + 1]), m, free[0], c_attn)
        return m, m2

    def a_norm_turn(b):
        M["xn_pe", b], M["hT1", b] = affine_turn(b, 2, lambda t: xn[:, t, :], hT1, [M["xn", b], misc_free[2], c_attn],
                                                 (M.get(("qkv_pe", b - 1)), 0))
        misc_free[2] = M["hT1", b]

    def a_qkv(b):
        i = b % 2
        for t in range(TB):
            for part, (lo, hi) in enumerate(((0, 512), (512, 768))):
                bank = misc(part)
                for c in range(DC):
                    fn = lambda e, t=t, c=c, lo=lo, hi=hi, bank=bank: e.matmul(
                        PS[:, bank, 0:hi - lo], hT1[:, c, t * P:(t + 1) * P], wqkv[:, c, lo:hi], start=(c == 0), stop=(c == DC - 1))
                    if c == DC - 1:
                        m = pe.mark(fn)
                    else:
                        pe.run(fn, M["hT1", b], misc_free[part], c_attn)
                if part == 0:
                    src = PS[:, bank, :].rearrange("p (q h f) -> p q h f", q=2, h=H)
                    for cs in range(2):
                        for q in range(2):
                            sv = src[:, q, :, :].rearrange("p h (a f) -> p (h a) f", a=2)
                            dv = rm[:, cs, q, :, :].rearrange("p h (a f) -> p (h a) f", a=2)
                            tv = wide(ropec[:, t, cs, q, :], 1, [P, 2 * H, HD // 2])
                            m1 = dve.mark(lambda e, sv=sv, dv=dv, tv=tv: e.tensor_tensor(dv, sv, tv, ALU.mult), m,
                                          M.get("rot"), c_attn)
                    misc_free[0] = m1
                    h8 = HD // 2
                    dst = QK[:, i, t, :, :, :]
                    pool.mark(lambda e, dst=dst: e.tensor_tensor(dst[:, :, :, 0:h8], rm[:, 0, :, :, 0:h8], rm[:, 1, :, :, h8:],
                                                                 ALU.subtract), m1, m_qk0, M.get(("qk_pe2", b - 2)))
                    pool.mark(lambda e, dst=dst: e.memset(dst[:, 0, :, HD:HD + 1], 0.0), M.get(("qk_pe2", b - 2)))
                    M["rot"] = M["qk", b, t] = pool.mark(lambda e, dst=dst: e.tensor_tensor(
                        dst[:, :, :, h8:HD], rm[:, 1, :, :, 0:h8], rm[:, 0, :, :, h8:], ALU.add))
                else:
                    misc_free[1] = M["vp", b, t] = act.mark(lambda e, bank=bank, t=t: e.activation(
                        VP[:, i, t, :, 0:HD], PS[:, bank, 0:D].rearrange("p (h f) -> p h f", h=H), ACT.Copy), m,
                        m_vp0, M.get(("pv", b - 2)))
        M["qkv_pe", b] = m

    def turn_heads(b, q, u, bank, waits):
        for g in range(2):
            for t in range(TB):
                fn = lambda e, g=g, t=t: e.transpose(PS[:, bank, g * T + t * P:g * T + (t + 1) * P],
                                                     QK[:, b % 2, t, q, (2 * u + g) * HG:(2 * u + g + 1) * HG, :].rearrange("p h f -> p (h f)"),
                                                     ident[:, :])
                if g == 1 and t == TB - 1:
                    return pe.mark(fn)
                pe.run(fn, *waits)

    def a_turn_qk(b):
        qk = [M["qk", b, t] for t in range(TB)]
        for u in range(NG // 2):
            bank = u % 3
            m = turn_heads(b, 0, u, misc(bank), qk + [misc_free[bank]])
            misc_free[bank] = M["qT", b] = act.mark(lambda e, u=u, bank=bank: e.activation(
                qT[:, 2 * u:2 * u + 2, :], bank2(misc(bank)), ACT.Copy), m, M.get(("s1", b - 1)))
        for u in range(NG // 2):
            bank = (2 + u) % 3
            m = turn_heads(b, 1, u, misc(bank), [misc_free[bank]])
            for g in range(2):
                mk = dve.mark(lambda e, u=u, g=g, bank=bank: e.tensor_tensor(
                    KM[:, 2 * u + g, :, :], wide(PS[:, misc(bank), g * T:(g + 1) * T], 1, [P, HG, T]),
                    wide(heads, 2, [P, HG, T]), ALU.mult), m, M.get(("s2", b - 1)))
            misc_free[bank] = M["KM", b] = mk

    NSB = 3
    s_free = [None] * NSB
    scount = [0]

    def score_banks(first, emit):
        pass

    def a_scores_max(b):
        i = b % 2
        for g in range(NG):
            for part in range(3):
                bank = scount[0] % NSB
                scount[0] += 1
                mrow = 0 if part < 2 else 1
                pe.run(lambda e, bank=bank, mrow=mrow: e.matmul(PS[:, bank, :], ident_b[:, :], causal[:, mrow, :], start=True, stop=False,
                                                                skip_group_check=True), s_free[bank], m_causal, M["qT", b], M["KM", b])
                if part < 2:
                    for x in range(2):
                        j = 2 * part + x
                        fn = lambda e, bank=bank, x=x, j=j, g=g: e.matmul(PS[:, bank, x * T:(x + 1) * T], qT[:, g, P:T], KM[:, g, j, :],
                                                                          start=False, stop=True, skip_group_check=True)
                        if x == 0:
                            pe.run(fn)
                    m = pe.mark(fn)
                    dst, src = QK[:, i, 1, 0, g * HG + 2 * part:g * HG + 2 * part + 2, HD], PS[:, bank, :].rearrange("p (x k) -> p x k", x=2)
                else:
                    for j in range(HG):
                        fn = lambda e, bank=bank, j=j, g=g: e.matmul(PS[:, bank, j * P:(j + 1) * P], qT[:, g, 0:P], KM[:, g, j, 0:P],
                                                                     start=False, stop=True, skip_group_check=True)
                        if j < HG - 1:
                            pe.run(fn)
                    m = pe.mark(fn)
                    dst, src = QK[:, i, 0, 0, g * HG:(g + 1) * HG, HD], PS[:, bank, :].rearrange("p (x k) -> p x k", x=HG)
                s_free[bank] = dve.mark(lambda e, dst=dst, src=src: e.tensor_reduce(dst, src, AX.X, ALU.max, negate=True), m)
        M["s1", b] = m
        M["max", b] = s_free[bank]

    def a_turn_q2(b):
        for u in range(NG // 2):
            bank = u % 3
            m = turn_heads(b, 0, u, misc(bank), [M["max", b], misc_free[bank]])
            misc_free[bank] = M["qT2", b] = act.mark(lambda e, u=u, bank=bank: e.activation(
                qT2[:, 2 * u:2 * u + 2, :], bank2(misc(bank)), ACT.Copy), m, M.get(("s2", b - 1)))
        M["qk_pe2", b] = m

    pcount = [0]
    p_free = [None] * NPT
    OB = NSB
    ot_free = [None, None]

    def a_attend(b):
        i = b % 2
        pts = {}

        def scores2(g):
            slots = []
            for part in range(3):
                bank = scount[0] % NSB
                scount[0] += 1
                mrow = 2 if part < 2 else 3
                pe.run(lambda e, bank=bank, mrow=mrow: e.matmul(PS[:, bank, :], ident_b[:, :], causal[:, mrow, :], start=True, stop=False,
                                                                skip_group_check=True), s_free[bank], M["qT2", b])
                if part < 2:
                    for x in range(2):
                        j = 2 * part + x
                        fn = lambda e, bank=bank, x=x, j=j: e.matmul(PS[:, bank, x * T:(x + 1) * T], KM[:, g, j, 0:P], qT2[:, g, :],
                                                                     start=False, stop=True, skip_group_check=True)
                        if x == 0:
                            pe.run(fn)
                else:
                    for j in range(HG):
                        fn = lambda e, bank=bank, j=j: e.matmul(PS[:, bank, j * P:(j + 1) * P], KM[:, g, j, P:T], qT2[:, g, P:T],
                                                                start=False, stop=True, skip_group_check=True)
                        if j < HG - 1:
                            pe.run(fn)
                m = pe.mark(fn)
                ps = pcount[0] % NPT
                pcount[0] += 1
                s_free[bank] = act.mark(lambda e, bank=bank, ps=ps: e.activation(PT[:, ps, :], PS[:, bank, :], ACT.Exp), m, p_free[ps])
                slots.append((ps, s_free[bank]))
            pts[g] = slots
            M["s2", b] = m

        def values(g):
            half = g % 2
            (pa, ma), (pb_, mb), (pd, md) = pts[g]
            for j in range(HG):
                hh = g * HG + j
                ps = (pa, pb_)[j // 2]
                o = PS[HP * j:HP * (j + 1), OB + half, 0:T]
                o2 = PS[HP * j:HP * (j + 1), OB + half, P:T]
                pe.run(lambda e, o=o, hh=hh, ps=ps, j=j: e.matmul(o, VP[:, i, 0, hh, :], PT[:, ps, (j % 2) * T:(j % 2 + 1) * T],
                                                                  start=True, stop=False, skip_group_check=True),
                       ma, mb, md, ot_free[half], *[M["vp", b, t] for t in range(TB)])
                fn = lambda e, o2=o2, hh=hh, j=j: e.matmul(o2, VP[:, i, 1, hh, :], PT[:, pd, j * P:(j + 1) * P],
                                                           start=False, stop=True, skip_group_check=True)
                if j < HG - 1:
                    pe.run(fn)
            m = pe.mark(fn)
            for p_ in (pa, pb_, pd):
                p_free[p_] = m
            M["pv", b] = m
            ot_free[half] = M["oT", b, g] = dve.mark(lambda e: e.tensor_copy(oT[:, g // 2, half, :], PS[:, OB + half, 0:T]),
                                                     m, M.get(("o_pe", b - 1)))

        for g in range(NG + 1):
            if g < NG:
                scores2(g)
            if g > 0:
                values(g - 1)

    def a_outputs(b):
        for t in range(TB):
            bank = misc(t)
            for g in range(NG):
                fn = lambda e, t=t, g=g, bank=bank: e.transpose(PS[:, bank, g * P:(g + 1) * P], oT[:, g // 2, g % 2, t * P:(t + 1) * P], ident[:, :])
                if g < NG - 1:
                    pe.run(fn, M["oT", b, 3], M["oT", b, 2], misc_free[t])
            m = pe.mark(fn)
            v = PS[:, bank, :].rearrange("p (h f) -> p h f", h=H)
            dve.mark(lambda e, t=t, v=v: e.reciprocal(rsum[:, t, :], v[:, :, HD]), m)
            misc_free[t] = M["at", b] = dve.chain(lambda e, t=t, v=v: e.tensor_tensor(
                at[:, t, :, :], v[:, :, 0:HD], wide(rsum[:, t, :], 2, [P, H, HD]), ALU.mult), M.get(("at_pe", b - 1)))
        M["o_pe", b] = m

    def a_out_turn(b):
        M["at_pe", b] = m = transposes(misc(2), lambda t: at[:, t, :, :].rearrange("p h f -> p (h f)"), [M["at", b], misc_free[2]])
        misc_free[2] = M["atT", b] = act.mark(lambda e: e.activation(atT[:, :, :], bank2(misc(2)), ACT.Copy), m, M.get(("proj", b - 1)))

    def a_proj(b):
        M["proj", b] = m = proj_like(misc(0), atT, lambda c: wproj[:, c, :], [M["atT", b], misc_free[0]])
        i = b % 2
        misc_free[0] = M["xr", b] = dve.mark(lambda e: e.tensor_tensor(XR[:, i, :, :], bank2(misc(0)), XC[:, b % 3, :, :], ALU.add),
                                             m, M.get(("base", b - 2)))
        M["xn2", b] = norm(XR[:, i, :, :], 1, XN2[:, b % NXN, :, :], [M.get(("scat1", b - NXN)), M.get(("xn2_pe", b - NXN))])
        M["base", b] = pool.mark(lambda e: e.tensor_tensor(X[:, TB * b:TB * b + TB, :], X[:, TB * b:TB * b + TB, :], XR[:, i, :, :], ALU.add),
                                 M["xr", b])

    def a_gate_turn(b):
        M["xn2_pe", b], M["h2T", b] = affine_turn(b, 1, lambda t: XN2[:, b % NXN, t, :], h2T, [M["xn2", b], misc_free[1]],
                                                  (M.get(("lg1", b - 1)), 2))
        misc_free[1] = M["h2T", b]

    def a_gate(b):
        for t in range(TB):
            r = (TB * b + t) % R
            for c in range(DC):
                fn = lambda e, t=t, c=c, r=r: e.matmul(PS[:, misc(2), r * E1:(r + 1) * E1], h2T[:, c, t * P:(t + 1) * P], wgate[:, c, :],
                                                       start=(c == 0), stop=(c == DC - 1))
                if not (t == TB - 1 and c == DC - 1):
                    pe.run(fn, M["h2T", b], misc_free[2])
        M["lg1", b] = pe.mark(fn)
        lgc = lgs[:, (b % GB) * TB * E1:(b % GB + 1) * TB * E1]
        src = PS[:, misc(2), (TB * b % R) * E1:(TB * b % R + TB) * E1]
        misc_free[2] = dve.mark(lambda e: e.tensor_copy(lgc, src), M["lg1", b], dve.last)
        if b % GB == GB - 1:
            router1.choose(b // GB, lgs[:, :].rearrange("p (r e) -> p r e", r=R), dve.last)

    lgs = sb("lgs", [P, R * E1], scope=s)

    def a_dispatch(b):
        if b % GB != GB - 1:
            return
        g = b // GB
        pe.wait(misc_free[0])
        router1.rank(g, misc(0))
        misc_free[0] = M["slot1", g]
        for bb in range(b - GB + 1, b + 1):
            for t in range(TB):
                for k in range(K1):
                    M["scat1", bb] = scat1[bb % NXN].dma(pool, lambda e, bb=bb, t=t, k=k: e.indirect_dma_start(
                        slots1, bass.IndirectOffsetOnAxis(ap=slot1[:, TB * bb + t, k:k + 1], axis=0),
                        XN2[:, bb % NXN, t, :], None, bounds_check=S1 - 1, oob_is_err=False),
                        M["slot1", g], M["xn2", bb], filled1)

    gather(0)
    front = [a_turn, a_matrix, a_norm_turn, a_qkv, a_turn_qk]
    back = [a_outputs, a_out_turn, a_proj, a_gate_turn, a_gate, a_dispatch]

    def lead(b):
        if b + 1 < B:
            gather(b + 1)
        a_combine(b)

    lead(0)
    for f in front:
        f(0)
    for b in range(B + 1):
        if b < B:
            a_scores_max(b)
        if b > 0:
            for f in back[:2]:
                f(b - 1)
        if b + 1 < B:
            lead(b + 1)
            for f in front[:2]:
                f(b + 1)
        if b < B:
            a_turn_q2(b)
        if b > 0:
            a_proj(b - 1)
        if b + 1 < B:
            a_norm_turn(b + 1)
        if b < B:
            a_attend(b)
        if b > 0:
            a_gate_turn(b - 1)
            a_gate(b - 1)
        if b + 1 < B:
            a_qkv(b + 1)
        if b > 0:
            a_dispatch(b - 1)
        if b + 1 < B:
            a_turn_qk(b + 1)
    all_scattered1 = [M["scat1", b] for b in range(B - NXN, B)]
    region.close()

    stage("experts1")
    meet(pe, act, dve, pool)
    region = ExitStack()
    ctx.enter_context(region)
    s = region
    ends = (pe.last, act.last, dve.last, pool.last)
    for q in (sp, pool, act, dve):
        q.wait(*ends, *all_scattered1)
    HS = 512
    NH = CAP1 // HS
    FC = F1 // P
    xe1 = sb("xe1", [P, 3, HS // P, D], scope=s)
    xe1T = sb("xe1T", [P, 2, DC, HS], scope=s)
    h1 = sb("h1", [P, 2, FC, HS], scope=s)
    b1s = sb("b1s", [P, E1, FC], scope=s)
    b2s = sb("b2s", [P, 2, D], scope=s)
    lng1 = sb("lng1", [P, 4, DC], scope=s)
    res1 = sb("res1", [P, 2, HS // P, D], scope=s)
    G1b = sb("G1b", [P, 4, K1, D], scope=s)
    xe1_in = lanes("xe1_in", 3)
    b2_in = lanes("b2_in", 2)
    res1_out = lanes("res1_out", 2)
    e1_in = Lane(sem("e1_in"))
    e1_in.dma(sp, lambda e: e.dma_start(b1s[:, :, :], io["b1_cols"]))
    c_e1 = e1_in.dma(sp, lambda e: e.dma_start(lng1[:, :, :], io["ln_cols"]))
    units = [(n, h) for n in range(E1) for h in range(NH)]
    X1, B2, O1 = {}, {}, {}

    def load1(u):
        n, h = units[u]
        X1[u] = xe1_in[u % 3].dma(sp, lambda e: e.dma_start(
            xe1[:, u % 3, :, :], slots1[n * CAP1 + h * HS:n * CAP1 + (h + 1) * HS, :].rearrange("(s p) d -> p s d", p=P)),
            M.get(("t1", u - 3)))
        if h == 0:
            B2[n] = b2_in[n % 2].dma(sp, lambda e: e.dma_start(b2s[:, n % 2, :], io["L1_ffn_b2"][n].partition_broadcast(P)),
                                     M.get(("r1", u - 2 * NH + NH - 1)))

    tb_free = [None, None]

    def turn1(u):
        for c in range(DC):
            for i in range(HS // P):
                fn = lambda e, c=c, i=i: e.transpose(PS[:, c, i * P:(i + 1) * P], xe1[:, u % 3, i, c * P:(c + 1) * P], ident[:, :])
                if i < HS // P - 1:
                    pe.run(fn, X1[u], tb_free[c])
            m = pe.mark(fn)
            tb_free[c] = M["x1eT", u, c] = dve.mark(lambda e, c=c: e.tensor_scalar(
                xe1T[:, u % 2, c, :], PS[:, c, :], lng1[:, 2, c:c + 1], lng1[:, 3, c:c + 1], ALU.mult, ALU.add),
                m, c_e1, M.get(("u1", u - 2)))
        M["t1", u] = m

    ub_free = [None] * 3
    ub = [0]

    def up1(u):
        n, h = units[u]
        wv = BIG[:, (n % 2) * N:(n % 2) * N + DC * F1].rearrange("p (c f) -> p c f", c=DC)
        for f in range(FC):
            k = ub[0] % 3
            ub[0] += 1
            for c in range(DC):
                fn = lambda e, c=c, f=f, k=k: e.matmul(PS[:, 2 + k, :], wv[:, c, f * P:(f + 1) * P], xe1T[:, u % 2, c, :],
                                                       start=(c == 0), stop=(c == DC - 1))
                if c == 0:
                    pe.run(fn, W1E[n], M["x1eT", u, 0], M["x1eT", u, 1], ub_free[k])
            m = pe.mark(fn)
            ub_free[k] = act.mark(lambda e, f=f, k=k: e.activation(h1[:, u % 2, f, :], PS[:, 2 + k, :], ACT.Gelu, bias=b1s[:, n, f:f + 1]),
                                  m, c_e1, M.get(("d1", u - 2)))
        M["u1", u] = m
        M["h1", u] = ub_free[k]

    db_free = [None, None]

    def down1(u):
        n, h = units[u]
        wv = BIG[:, (n % 2) * N + DC * F1:(n % 2 + 1) * N].rearrange("p (c f) -> p c f", f=D)
        for q in range(HS // P // 2):
            for i in range(2 * q, 2 * q + 2):
                for f in range(FC):
                    fn = lambda e, i=i, f=f, q=q: e.matmul(PS[:, 5 + q, (i % 2) * D:(i % 2 + 1) * D], h1[:, u % 2, f, i * P:(i + 1) * P],
                                                           wv[:, f, :], start=(f == 0), stop=(f == FC - 1))
                    if not (i % 2 and f == FC - 1):
                        pe.run(fn, M["h1", u], db_free[q])
            m = pe.mark(fn)
            db_free[q] = M["r1", u] = dve.mark(lambda e, q=q: e.tensor_tensor(
                res1[:, u % 2, 2 * q:2 * q + 2, :], bank2(5 + q), wide(b2s[:, n % 2, :], 1, [P, 2, D]), ALU.add),
                m, B2[n], O1.get(u - 2))
        M["d1", u] = m
        O1[u] = res1_out[u % 2].dma(sp, lambda e: e.dma_start(
            done1[n * CAP1 + h * HS:n * CAP1 + (h + 1) * HS, :].rearrange("(s p) d -> p s d", p=P), res1[:, u % 2, :, :]), M["r1", u])

    load1(0)
    load1(1)
    turn1(0)
    for u in range(len(units)):
        n, h = units[u]
        if u + 2 < len(units):
            load1(u + 2)
        up1(u)
        if u + 1 < len(units):
            turn1(u + 1)
        down1(u)
        if h == NH - 1 and n + 2 < E1:
            load_w1e(n + 2, M["d1", u])

    stage("final")
    gat1 = lanes("gat1_", 4)
    out_v = out.rearrange("b (c p) d -> p (b c) d", p=P)
    outs = Lane(sem("outs"))
    OUTW = 4
    last_store = None
    for t in range(NT):
        for k in range(K1):
            mg = gat1[t % 4].dma(pool, lambda e, t=t, k=k: e.indirect_dma_start(
                G1b[:, t % 4, k, :], None, done1, bass.IndirectOffsetOnAxis(ap=slot1[:, t, k:k + 1], axis=0)),
                O1[len(units) - 2], O1[len(units) - 1], M.get(("fin", t - 4)), fill_end)
        for k in range(K1):
            M["fin", t] = dve.chain(lambda e, t=t, k=k: e.scalar_tensor_tensor(
                X[:, t, :], G1b[:, t % 4, k, :], w_pick1[:, t, k:k + 1], X[:, t, :], ALU.mult, ALU.add), mg)
        if t % OUTW == OUTW - 1:
            last_store = outs.dma(sp, lambda e, t=t: e.dma_start(out_v[:, t - OUTW + 1:t + 1, :], X[:, t - OUTW + 1:t + 1, :]), M["fin", t])
    sp.wait(last_store, O1[len(units) - 1], O1[len(units) - 2], fill_end, filled1, *all_done0, *all_scattered, *all_scattered1)
    region.close()

    block = ctx.enter_context(nc.Block())

    @block.sync
    def _(e):
        sp.play(e)

    @block.gpsimd
    def _(e):
        pool.play(e)

    @block.tensor
    def _(e):
        pe.play(e)

    @block.scalar
    def _(e):
        act.play(e)

    @block.vector
    def _(e):
        dve.play(e)


def lay_out(inputs):
    a = {k: np.asarray(v) for k, v in inputs.items()}
    m = {k: a[k] for k in ("x", "itok_B_0_2", "itok_B_0_30", "L0_cond_W1", "L0_ffn_w1", "L0_ffn_w2", "L0_ffn_w3",
                           "L0_ffn_sw1", "L0_ffn_sw2", "L0_ffn_sw3", "L1_cond_W", "L1_cond_b", "L1_ffn_Wproj",
                           "L1_ffn_Wgate", "L1_ffn_W1", "L1_ffn_W2", "L1_ffn_b2")}
    m["L0_cond_b1"] = a["L0_cond_b1"].reshape(A0, 1)
    m["L0_cond_v"] = a["L0_cond_v"].reshape(A0, 1)
    m["L0_ffn_wgT"] = a["L0_ffn_wg"].T
    m["L1_ffn_WqkvT"] = a["L1_ffn_Wqkv"].reshape(D, H, 3, HD).transpose(0, 2, 1, 3).reshape(D, 3 * D)
    col = lambda v: v.reshape(DC, P).T
    m["ln_cols"] = np.stack([col(a[f"L1_ffn_{n}"]) for n in ("ln1_g", "ln1_b", "ln2_g", "ln2_b")], 1)
    m["b1_cols"] = a["L1_ffn_b1"].reshape(E1, F1 // P, P).transpose(2, 0, 1)
    m.update(shape_constants())
    return {k: np.ascontiguousarray(v) for k, v in m.items()}


def kernel(**inputs):
    import concourse.bacc as _bacc
    from concourse.bass_utils import run_bass_kernel_spmd as _run

    nc = _bacc.Bacc("TRN2", target_bir_lowering=False, num_devices=1)
    arrays = lay_out(inputs)
    io = {k: nc.dram_tensor(f"in_{k}", v.shape, mybir.dt.from_np(v.dtype), kind="ExternalInput").ap() for k, v in arrays.items()}
    out = nc.dram_tensor("out_0", (B, T, D), F32, kind="ExternalOutput").ap()
    bass_adaln_ffn(nc, io, out)
    r = _run(nc, [{f"in_{k}": v for k, v in arrays.items()}], core_ids=[0])
    return r.results[0]["out_0"]
```

```python
from contextlib import ExitStack

import numpy as np

import concourse.bass as bass
from concourse import mybir

F32 = mybir.dt.float32
BF16 = mybir.dt.bfloat16
I32 = mybir.dt.int32
U32 = mybir.dt.uint32
ALU = mybir.AluOpType
ACT = mybir.ActivationFunctionType
AX = mybir.AxisListType

P = 128
B, T, D = 16, 256, 256
N = B * T
NT = N // P
TB = T // P
DC = D // P
A0 = 64
E0, K0, G0, KG0 = 32, 4, 8, 4
CAP0 = int(1.25 * N * K0 / E0)
S0 = E0 * CAP0
E1, K1 = 8, 2
CAP1 = -(-2 * N // E1)
S1 = E1 * CAP1
F1 = 4 * D
H, HD = 16, 16
HP = 32
HG = P // HP
NG = H // HG
EPS = 1e-5
NEG = -1e30


class Mark:

    def __init__(self, sem, value):
        self.sem, self.value = sem, value


class Queue:

    def __init__(self, new_sem, name):
        self.new_sem, self.name = new_sem, name
        self.steps, self.seen, self.last = [], {}, None

    def stage(self, what):
        self.sem, self.count = self.new_sem(f"{self.name}_{what}"), 0

    def wait(self, *marks):
        for m in marks:
            if m is not None and self.seen.get(id(m.sem), 0) < m.value:
                self.seen[id(m.sem)] = m.value
                self.steps.append(lambda e, m=m: e.wait_ge(m.sem, m.value))

    def run(self, fn, *marks):
        self.wait(*marks)
        self.steps.append(fn)

    def mark(self, fn, *marks):
        self.wait(*marks)
        self.count += 1
        self.last = Mark(self.sem, self.count)
        self.steps.append(lambda e, s=self.sem: fn(e).then_inc(s, 1))
        return self.last

    def chain(self, fn, *marks):
        return self.mark(fn, self.last, *marks)

    def play(self, engine):
        for step in self.steps:
            step(engine)


class Lane:

    def __init__(self, sem):
        self.sem, self.count = sem, 0

    def dma(self, queue, fn, *marks):
        queue.wait(*marks)
        self.count += 16
        queue.steps.append(lambda e: fn(e).then_inc(self.sem, 16))
        return Mark(self.sem, self.count)


def wide(ap, axis, shape):
    return ap.unsqueeze(axis).broadcast_to(shape)


def shape_constants():
    p = np.arange(P)
    ident = np.eye(P, dtype=np.float32)
    before = (p[:, None] < p[None, :]).astype(np.float32)
    j = np.arange(T).reshape(TB, P).T[:, :, None]
    l = np.arange(T)[None, None, :]
    add = [np.where(m, 0.0, NEG) for m in (l <= j, l >= j, l != j)]
    cnt = [m.sum(-1) * 1.0 for m in (l <= j, l >= j, l != j)]
    pool = np.stack([add[2], add[0] - add[2], add[1] - add[2]], 1).astype(np.float32)
    cnts = np.stack([cnt[2], cnt[0] - cnt[2], cnt[1] - cnt[2]], 1).astype(np.float32)
    inv = (1.0 / 10000.0 ** (np.arange(0, HD, 2, dtype=np.float32) / HD)).astype(np.float32)
    ang = np.arange(T, dtype=np.float32)[:, None] * inv
    cs = np.stack([np.cos(ang), np.sin(ang)]).astype(np.float32)
    rope = np.stack([cs / np.float32(HD ** 0.5), cs], 1)
    rope = rope.reshape(2, 2, TB, P, HD // 2).transpose(3, 2, 0, 1, 4)
    tri_q = np.where(p[None, :] > p[:, None], -1e9, 0.0)
    heads = (p[:, None] // HP == np.arange(HG)[None, :]).astype(np.float32)
    small = np.concatenate([
        np.tile(np.arange(G0), (P, 1)), np.tile(np.arange(E0), (P, 1)),
        np.tile(np.arange(E0) * CAP0 - S0, (P, 1)), np.tile(np.arange(E1) * CAP1 - S1, (P, 1)),
        p[:, None] + P * np.arange(DC)[None, :], heads], 1)
    token = (p[:, None] + P * np.arange(NT)[None, :]).astype(np.int32)
    empty = np.zeros((S1, 2), np.float32)
    empty[:, 0] = np.full(S1, N, np.int32).view(np.float32)
    f = lambda a: np.ascontiguousarray(a, dtype=np.float32)
    return {"c_ident": f(ident), "c_before": f(before), "c_pool": f(pool), "c_cnt": f(cnts),
            "c_rope": f(rope), "c_causal": f(tri_q), "c_small": f(small),
            "c_token": token, "c_empty": empty}


def bass_adaln_ffn(nc, io, out, debug=None):
    ctx = ExitStack()
    with ctx:
        return _build(nc, ctx, io, out, debug)


def _build(nc, ctx, io, out, debug):
    def sem(name):
        return ctx.enter_context(nc.semaphore(name))

    def lanes(name, n):
        return [Lane(sem(f"{name}{i}")) for i in range(n)]

    def sb(name, shape, dt=F32, scope=ctx):
        return scope.enter_context(nc.sbuf_tensor(name, shape, dt))

    pe, act, dve, pool, sp = (Queue(sem, n) for n in ("pe", "act", "dve", "pool", "sp"))
    engines = [pe, act, dve, pool]

    def stage(name):
        for q in engines:
            q.stage(name)

    def meet(*queues):
        ends = [q.last for q in queues]
        for q in queues:
            q.wait(*ends)

    stage("pool0")
    PS = ctx.enter_context(nc.psum_tensor("banks", [P, 8, 512], F32))

    pooled = nc.dram_tensor("pooled", (N, D), F32, kind="Internal").ap()
    table0 = nc.dram_tensor("table0", (S0, 1), U32, kind="Internal").ap()
    done0 = nc.dram_tensor("done0", (S0 + 1, D), F32, kind="Internal").ap()
    normed = nc.dram_tensor("normed", (N + 1, D), F32, kind="Internal").ap()
    table1 = nc.dram_tensor("table1", (S1, 2), F32, kind="Internal").ap()

    X = sb("X", [P, NT, D])
    BIG = sb("BIG", [P, DC * N])
    XFT = BIG[:, :].rearrange("p (c n) -> p c n", c=DC)
    ident = sb("ident", [P, P])
    before = sb("before", [P, P])
    ones = sb("ones", [P, P])
    small = sb("small", [P, G0 + 2 * E0 + E1 + DC + HG])
    iota = small[:, G0:G0 + E0]
    base0 = small[:, G0 + E0:G0 + 2 * E0]
    base1 = small[:, G0 + 2 * E0:G0 + 2 * E0 + E1]
    rows = small[:, G0 + 2 * E0 + E1:G0 + 2 * E0 + E1 + DC]
    heads = small[:, G0 + 2 * E0 + E1 + DC:]
    w_pick0 = sb("w_pick0", [P, NT, K0])
    slot0 = sb("slot0", [P, NT, K0], U32)
    pair1 = sb("pair1", [P, NT, K1, 2])
    w_pick1 = pair1[:, :, :, 1]
    token = sb("token", [P, NT], I32)
    slot1 = sb("slot1", [P, NT, K1], U32)
    cat_row = sb("cat_row", [P, B, DC], U32)
    cat_id = sb("cat_id", [P, B], U32)
    idx0 = sb("idx0", [P, E0, CAP0 // P], U32)
    nhalf = sb("nhalf", [P, TB])
    epsc = EPS

    consts = Lane(sem("consts_in"))
    for dst, name in ((ident, "c_ident"), (before, "c_before"), (small, "c_small"), (token, "c_token")):
        c_base = consts.dma(sp, lambda e, d=dst, n=name: e.dma_start(d[:, :], io[n]))
    x_in = lanes("x_in", 4)
    x_v = io["x"].rearrange("b (c p) d -> p (b c) d", p=P)
    x_ready = {}

    def load_x(q, w):
        x_ready[q] = x_in[q].dma(sp, lambda e: e.dma_start(
            X[:, q * 8:q * 8 + w, :], x_v[:, q * 8:q * 8 + w, :]))

    region = ExitStack()
    ctx.enter_context(region)
    s = region
    w1c = sb("w1c", [P, DC, A0], scope=s)
    b1c = sb("b1c", [A0, 1], scope=s)
    vc = sb("vc", [A0, 1], scope=s)
    vb = sb("vb", [A0, P], scope=s)
    wgT = sb("wgT", [P, DC, E0], scope=s)
    poolc = sb("poolc", [P, 3, TB, T], scope=s)
    cntc = sb("cntc", [P, 3, TB], scope=s)
    ids_i = sb("ids_i", [P, 2, B], I32, scope=s)
    ids = sb("ids", [P, 2, B], scope=s)
    kind = sb("kind", [P, 2, B], scope=s)
    cnt = sb("cnt", [P, B, TB], scope=s)
    cat_f = sb("cat_f", [P, B, DC], scope=s)
    zeros = sb("zeros", [P, D], scope=s)
    xT = sb("xT", [P, 2, DC, T], scope=s)
    aT = sb("aT", [A0, 2, T], scope=s)
    mask = sb("mask", [P, 2, TB, T], scope=s)
    msc = sb("msc", [P, 2, TB, T], scope=s)
    pr = sb("pr", [P, 2, TB, T], scope=s)
    nmax = sb("nmax", [P, 2, TB], scope=s)
    psum_ = sb("psum_", [P, 2, TB], scope=s)
    pinv = sb("pinv", [P, 2, TB], scope=s)
    prT = sb("prT", [P, 2, TB, T], scope=s)
    NXF = 4
    xf_out = lanes("xf_out", NXF)
    XF = sb("XF", [P, NXF, TB, D], scope=s)

    load_x(0, 8)
    cond_in = Lane(sem("cond_in"))
    for dst, src in ((w1c, io["L0_cond_W1"].rearrange("(c p) a -> p c a", p=P)), (b1c, io["L0_cond_b1"]),
                     (vc, io["L0_cond_v"]), (wgT, io["L0_ffn_wgT"].rearrange("(c p) e -> p c e", p=P)),
                     (poolc, io["c_pool"]), (cntc, io["c_cnt"])):
        c_cond = cond_in.dma(sp, lambda e, d=dst, s_=src: e.dma_start(d[tuple([slice(None)] * len(d.shape))], s_))
    c_cond = cond_in.dma(sp, lambda e: e.dma_start(ids_i[:, 0, :], io["itok_B_0_2"].partition_broadcast(P)))
    c_cond = cond_in.dma(sp, lambda e: e.dma_start(ids_i[:, 1, :], io["itok_B_0_30"].partition_broadcast(P)))
    for q in range(1, 4):
        load_x(q, 8)

    m_ones = pool.mark(lambda e: e.memset(ones[:, :], 1.0))
    m_zero = pool.mark(lambda e: e.memset(zeros[:, :], 0.0))
    m_nhalf = pool.mark(lambda e: e.memset(nhalf[:, :], -0.5))
    dve.chain(lambda e: e.tensor_copy(ids[:, :, :], ids_i[:, :, :]), c_cond)
    for i in range(2):
        m = dve.mark(lambda e, i=i: e.tensor_scalar(kind[:, i, :], ids[:, 0, :], float(i), None, ALU.is_equal), dve.last)
    for c in range(TB):
        dve.chain(lambda e, c=c: e.tensor_scalar(cnt[:, :, c], kind[:, 0, :], cntc[:, 1, c:c + 1], cntc[:, 0, c:c + 1],
                                                 ALU.mult, ALU.add))
        dve.chain(lambda e, c=c: e.scalar_tensor_tensor(cnt[:, :, c], kind[:, 1, :], cntc[:, 2, c:c + 1],
                                                        cnt[:, :, c], ALU.mult, ALU.add))
    for c in range(DC):
        dve.chain(lambda e, c=c: e.tensor_scalar(cat_f[:, :, c], ids[:, 1, :], float(D), rows[:, c:c + 1],
                                                 ALU.mult, ALU.add))
    dve.chain(lambda e: e.tensor_copy(cat_row[:, :, :], cat_f[:, :, :]))
    m_cat = dve.chain(lambda e: e.tensor_copy(cat_id[:, :], ids[:, 1, :]))
    m_vb = dve.mark(lambda e: e.tensor_copy(vb[:, :], vc[:, :].broadcast_to([A0, P])))

    for k in range(K1):
        m_pair = dve.chain(lambda e, k=k: e.tensor_copy(pair1[:, :, k, 0].bitcast(I32), token[:, :]), c_base)

    filled0 = Lane(sem("fill0")).dma(sp, lambda e: e.dma_start(
        table0.rearrange("(p r) o -> p (r o)", p=P), zeros[:, 0:S0 // P].bitcast(U32)), m_zero)
    filled1 = Lane(sem("fill1")).dma(sp, lambda e: e.dma_start(table1, io["c_empty"]))
    fill_last = Lane(sem("fill_last"))
    for t_, n_ in ((done0, S0), (normed, N)):
        fill_end = fill_last.dma(sp, lambda e, t_=t_, n_=n_: e.dma_start(t_[n_:n_ + 1, :], zeros[0:1, 0:D]), m_zero)

    M = {}

    def transposes(bank, src, waits):
        for c in range(DC):
            for t in range(TB):
                fn = lambda e, c=c, t=t: e.transpose(PS[:, bank, c * T + t * P:c * T + (t + 1) * P],
                                                     src(t)[:, c * P:(c + 1) * P], ident[:, :])
                if c == DC - 1 and t == TB - 1:
                    return pe.mark(fn, *waits)
                pe.run(fn, *waits)

    def bank2(bank, n=T):
        return PS[:, bank, :].rearrange("p (a n) -> p a n", n=n)

    def p_transpose(b):
        m = transposes(0, lambda t: X[:, TB * b + t, :], [c_base, x_ready[b // 4], M.get(("xT", b - 1))])
        M["xT", b] = act.mark(lambda e: e.activation(xT[:, b % 2, :, :], bank2(0), ACT.Copy), m, M.get(("hid", b - 2)))

    def p_hidden(b):
        for c in range(DC):
            fn = lambda e, c=c: e.matmul(PS[0:A0, 1, 0:T], w1c[:, c, :], xT[:, b % 2, c, :], start=(c == 0), stop=(c == DC - 1))
            if c < DC - 1:
                pe.run(fn, M["xT", b], M.get(("aT", b - 1)), c_cond)
        M["hid", b] = m = pe.mark(fn)
        M["aT", b] = act.mark(lambda e: e.activation(aT[:, b % 2, :], PS[0:A0, 1, 0:T], ACT.Tanh, bias=b1c[:, 0:1]),
                              m, c_cond, M.get(("sc", b - 2)))

    def p_mask(b):
        i = b % 2
        dve.mark(lambda e: e.scalar_tensor_tensor(mask[:, i, :, :], poolc[:, 1, :, :], kind[:, 0, b:b + 1],
                                                  poolc[:, 0, :, :], ALU.mult, ALU.add), M.get(("msc", b - 2)))
        M["mask", b] = dve.chain(lambda e: e.scalar_tensor_tensor(mask[:, i, :, :], poolc[:, 2, :, :], kind[:, 1, b:b + 1],
                                                                  mask[:, i, :, :], ALU.mult, ALU.add))

    def p_scores(b):
        i = b % 2
        M["sc", b] = m = pe.mark(lambda e: e.matmul(PS[:, 2, 0:T], vb[:, :], aT[:, i, :], start=True, stop=True),
                                 M["aT", b], m_vb, M.get(("msc", b - 1)))
        M["msc", b] = dve.mark(lambda e: e.tensor_tensor(msc[:, i, :, :], mask[:, i, :, :], wide(PS[:, 2, 0:T], 1, [P, TB, T]),
                                                         ALU.add), m, M["mask", b], M.get(("exp", b - 2)))
        m = dve.chain(lambda e: e.tensor_reduce(nmax[:, i, :], msc[:, i, :, :], AX.X, ALU.max, negate=True))
        for c in range(TB):
            m2 = act.mark(lambda e, c=c: e.activation(pr[:, i, c, :], msc[:, i, c, :], ACT.Exp, bias=nmax[:, i, c:c + 1],
                                                      accum_out=psum_[:, i, c:c + 1]), m, M.get(("prT_pe", b - 2)),
                          M.get(("pinv", b - 2)))
        M["exp", b] = m2

    def p_turn(b):
        i = b % 2
        m = None
        for lc in range(TB):
            for jc in range(TB):
                fn = lambda e, lc=lc, jc=jc: e.transpose(PS[:, 3, lc * T + jc * P:lc * T + (jc + 1) * P],
                                                         pr[:, i, jc, lc * P:(lc + 1) * P], ident[:, :])
                if lc == TB - 1 and jc == TB - 1:
                    m = pe.mark(fn)
                else:
                    pe.run(fn, M["exp", b], M.get(("prT", b - 1)))
        M["prT_pe", b] = m
        M["prT", b] = dve.mark(lambda e: e.tensor_copy(prT[:, i, :, :], bank2(3)), m, M.get(("mix", b - 2)))
        dve.mark(lambda e: e.tensor_tensor(psum_[:, i, :], psum_[:, i, :], cnt[:, b, :], ALU.mult), M["exp", b])
        M["pinv", b] = dve.chain(lambda e: e.reciprocal(pinv[:, i, :], psum_[:, i, :]))

    def p_mix(b):
        i = b % 2
        for jc in range(TB):
            for lc in range(TB):
                fn = lambda e, jc=jc, lc=lc: e.matmul(PS[:, 4, jc * D:(jc + 1) * D], prT[:, i, lc, jc * P:(jc + 1) * P],
                                                      X[:, TB * b + lc, :], start=(lc == 0), stop=(lc == TB - 1))
                if jc == TB - 1 and lc == TB - 1:
                    M["mix", b] = m = pe.mark(fn)
                else:
                    pe.run(fn, M["prT", b], M.get(("XF", b - 1)))
        M["XF", b] = dve.mark(lambda e: e.tensor_tensor(XF[:, b % NXF, :, :], bank2(4), wide(pinv[:, i, :], 2, [P, TB, D]),
                                                        ALU.mult), m, M["pinv", b], M.get(("stored", b - NXF)), M.get(("XFT_pe", b - NXF)))
        M["stored", b] = xf_out[b % NXF].dma(sp, lambda e: e.dma_start(
            pooled[b * T:(b + 1) * T, :].rearrange("(c p) d -> p c d", p=P), XF[:, b % NXF, :, :]), M["XF", b])

    def p_turn_back(b):
        m = transposes(5, lambda t: XF[:, b % NXF, t, :], [M["XF", b], M.get(("XFT", b - 1))])
        M["XFT_pe", b] = m
        M["XFT", b] = act.mark(lambda e: e.activation(XFT[:, :, b * T:(b + 1) * T], bank2(5), ACT.Copy), m)

    R = 4

    class Router:

        def __init__(self, scope, tag, E, K, groups, cap, base, weights, slots):
            self.E, self.K, self.groups, self.cap, self.base = E, K, groups, cap, base
            self.weights, self.slots, self.tag = weights, slots, tag
            f = lambda n, *shape, dt=F32: sb(f"{n}_{tag}", [P, *shape], dt, scope)
            self.nm, self.sh, self.ex = f("nm", R), f("sh", R, E), f("ex", R, E)
            self.tv, self.ti, self.tf = f("tv", R, 8), f("ti", R, 8, dt=U32), f("tf", R, 8)
            self.hit = f("hit", R, K, E)
            self.sel, self.cum = f("sel", R, E), f("cum", R + 1, E)
            self.sm, self.ok, self.sf = f("sm", R, E), f("ok", R, E), f("sf", R, K)
            self.den, self.top = f("den", R), f("top", R)
            self.pick = f("pick", R, K, E)
            if groups:
                self.gs, self.gv, self.gi, self.gf = f("gs", R, groups), f("gv", R, 8), f("gi", R, 8, dt=U32), f("gf", R, 8)
                self.ghit, self.gk, self.gm = f("ghit", R, KG0, groups), f("gk", R, groups), f("gm", R, groups)
                self.cand = f("cand", R, E)
            dve.mark(lambda e: e.memset(self.cum[:, R, :], 0.0))

        def choose(self, g, logits, m_logits):
            E, K, t0 = self.E, self.K, g * R
            S3 = [P, R, E]
            dve.chain(lambda e: e.tensor_reduce(self.nm[:, :], logits, AX.X, ALU.max, negate=True), m_logits)
            m = dve.chain(lambda e: e.tensor_tensor(self.sh[:, :, :], logits, wide(self.nm[:, :], 2, S3), ALU.add))
            m = act.mark(lambda e: e.activation(self.ex[:, :, :], self.sh[:, :, :], ACT.Exp), m)
            M["choose_free" + self.tag] = dve.last
            dve.wait(m)
            cand = self.ex
            if self.groups:
                G = self.groups
                dve.mark(lambda e: e.tensor_reduce(self.gs[:, :, :], self.ex[:, :, :].rearrange("p r (g k) -> p r g k", g=G),
                                                   AX.X, ALU.max))
                for r in range(R):
                    dve.chain(lambda e, r=r: e.max(self.gv[:, r, :], self.gs[:, r, :]))
                for r in range(R):
                    dve.chain(lambda e, r=r: e.max_index(self.gi[:, r, :], self.gv[:, r, :], self.gs[:, r, :]))
                dve.chain(lambda e: e.tensor_copy(self.gf[:, :, :], self.gi[:, :, :]))
                dve.chain(lambda e: e.tensor_tensor(self.ghit[:, :, :, :], wide(wide(iota[:, 0:G], 1, [P, R, G]), 2, [P, R, KG0, G]),
                                                    wide(self.gf[:, :, 0:KG0], 3, [P, R, KG0, G]), ALU.is_equal))
                dve.chain(lambda e: e.tensor_reduce(self.gk[:, :, :], self.ghit[:, :, :, :].rearrange("p r k g -> p r g k"),
                                                    AX.X, ALU.add))
                dve.chain(lambda e: e.tensor_scalar(self.gm[:, :, :], self.gk[:, :, :], -1.0, None, ALU.add))
                v4 = lambda a: a[:, :, :].rearrange("p r (g k) -> p r g k", g=G)
                SG = [P, R, G, E // G]
                dve.chain(lambda e: e.tensor_tensor(v4(self.cand), v4(self.ex), wide(self.gk[:, :, :], 3, SG), ALU.mult))
                dve.chain(lambda e: e.tensor_tensor(v4(self.cand), v4(self.cand), wide(self.gm[:, :, :], 3, SG), ALU.add))
                cand = self.cand
            for r in range(R):
                dve.chain(lambda e, r=r: e.max(self.tv[:, r, :], cand[:, r, :]))
            for r in range(R):
                dve.chain(lambda e, r=r: e.max_index(self.ti[:, r, :], self.tv[:, r, :], cand[:, r, :]))
            dve.chain(lambda e: e.tensor_copy(self.tf[:, :, :], self.ti[:, :, :]))
            S4 = [P, R, K, E]
            dve.chain(lambda e: e.tensor_tensor(self.hit[:, :, :, :], wide(wide(iota[:, 0:E], 1, S3), 2, S4),
                                                wide(self.tf[:, :, 0:K], 3, S4), ALU.is_equal))
            m_sel = dve.chain(lambda e: e.tensor_reduce(self.sel[:, :, :], self.hit[:, :, :, :].rearrange("p r k e -> p r e k"),
                                                        AX.X, ALU.add), M.get(("rank" + self.tag, g - 1)))
            m_cum = dve.chain(lambda e: e.tensor_copy(self.cum[:, 0, :], self.cum[:, R, :]))
            for r in range(R):
                m_cum = dve.chain(lambda e, r=r: e.tensor_tensor(self.cum[:, r + 1, :], self.cum[:, r, :], self.sel[:, r, :], ALU.add))
            M["sel" + self.tag, g] = m_cum
            dve.mark(lambda e: e.tensor_reduce(self.den[:, :], self.ex[:, :, :], AX.X, ALU.add))
            if self.groups:
                dve.mark(lambda e: e.tensor_reduce(self.top[:, :], self.tv[:, :, 0:K], AX.X, ALU.add))
                dve.chain(lambda e: e.scalar_tensor_tensor(self.den[:, :], self.den[:, :], 1e-9, self.top[:, :], ALU.mult, ALU.add))
            dve.chain(lambda e: e.reciprocal(self.den[:, :], self.den[:, :]))
            M["w" + self.tag, g] = dve.chain(lambda e: e.tensor_tensor(
                self.weights[:, t0:t0 + R, :], self.tv[:, :, 0:K], wide(self.den[:, :], 2, [P, R, K]), ALU.mult))

        def rank(self, g, bank):
            E, K, t0 = self.E, self.K, g * R
            for r in range(R):
                o = PS[:, bank, r * E:(r + 1) * E]
                pe.run(lambda e, r=r, o=o: e.matmul(o, before[:, :], self.sel[:, r, :], start=True, stop=False),
                       M["sel" + self.tag, g], M.get(("slot" + self.tag, g - 1)), m_ones)
                fn = lambda e, r=r, o=o: e.matmul(o, ones[:, :], self.cum[:, r, :], start=False, stop=True)
                if r < R - 1:
                    pe.run(fn)
            M["rank" + self.tag, g] = m = pe.mark(fn)
            pos = PS[:, bank, 0:R * E].rearrange("p (r e) -> p r e", r=R)
            S3, S4 = [P, R, E], [P, R, K, E]
            dve.mark(lambda e: e.tensor_scalar(self.ok[:, :, :], pos, float(self.cap), None, ALU.is_lt), m)
            dve.mark(lambda e: e.tensor_tensor(self.sm[:, :, :], pos, wide(self.base, 1, S3), ALU.add))
            dve.chain(lambda e: e.tensor_tensor(self.sm[:, :, :], self.sm[:, :, :], self.ok[:, :, :], ALU.mult))
            dve.chain(lambda e: e.tensor_tensor(self.pick[:, :, :, :], self.hit[:, :, :, :], wide(self.sm[:, :, :], 2, S4), ALU.mult))
            dve.chain(lambda e: e.tensor_reduce(self.sf[:, :, :], self.pick[:, :, :, :], AX.X, ALU.add))
            M["slot" + self.tag, g] = dve.chain(lambda e: e.tensor_scalar(
                self.slots[:, t0:t0 + R, :], self.sf[:, :, :], float(self.cap * E), None, ALU.add))

    router0 = Router(region, "0", E0, K0, G0, CAP0, base0, w_pick0, slot0)
    GB = R // TB
    scat0 = Lane(sem("scat0"))

    def p_logits(b):
        for t in range(TB):
            r = (TB * b + t) % R
            for c in range(DC):
                fn = lambda e, t=t, c=c, r=r: e.matmul(
                    PS[:, 6, r * E0:(r + 1) * E0], XFT[:, c, (TB * b + t) * P:(TB * b + t + 1) * P], wgT[:, c, :],
                    start=(c == 0), stop=(c == DC - 1))
                if t == TB - 1 and c == DC - 1:
                    M["lg", b] = pe.mark(fn)
                else:
                    pe.run(fn, M["XFT", b], M.get("choose_free0"))
        if b % GB == GB - 1:
            router0.choose(b // GB, PS[:, 6, 0:R * E0].rearrange("p (r e) -> p r e", r=R), M["lg", b])

    def p_dispatch(b):
        if b % GB != GB - 1:
            return
        g = b // GB
        router0.rank(g, 7)
        for bb in range(b - GB + 1, b + 1):
            for t in range(TB):
                for k in range(K0):
                    M["scat0"] = scat0.dma(pool, lambda e, bb=bb, t=t, k=k: e.indirect_dma_start(
                        table0, bass.IndirectOffsetOnAxis(ap=slot0[:, TB * bb + t, k:k + 1], axis=0),
                        token[:, TB * bb + t:TB * bb + t + 1].bitcast(U32), None, bounds_check=S0 - 1, oob_is_err=False),
                        M["slot0", g], filled0, c_base)

    steps = [p_transpose, p_hidden, p_scores, p_turn, p_mix, p_turn_back, p_logits, p_dispatch]
    for b in range(2):
        p_mask(b)
    for t in range(B + len(steps) - 1):
        for k in reversed(range(len(steps))):
            if 0 <= t - k < B:
                steps[k](t - k)
                if steps[k] is p_scores and t - k + 2 < B:
                    p_mask(t - k + 2)

    stage("shared")
    NW0 = 3
    NXE = 3
    w0 = sb("w0", [P, NW0, 3, DC, D], scope=s)
    xe = sb("xe", [P, NXE, CAP0 // P, D], scope=s)
    xeT = sb("xeT", [P, 2, DC * CAP0], scope=s)
    gate = sb("gate", [P, 2, 512], scope=s)
    hT = sb("hT", [P, 2, 2, CAP0], scope=s)
    res = sb("res", [P, 2, CAP0 // P, D], scope=s)
    w_in = lanes("w_in", NW0)
    xe_in = lanes("xe_in", NXE)
    res_out = lanes("res_out", 2)

    def load_w0(n, srcs, *marks):
        for i, src in enumerate(srcs):
            m = w_in[n % NW0].dma(sp, lambda e, i=i, src=src: e.dma_start(
                w0[:, n % NW0, i, :, :], src.rearrange("(c p) f -> p c f", p=P)), *marks)
        return m

    W0 = {0: load_w0(0, [io["L0_ffn_sw1"], io["L0_ffn_sw3"], io["L0_ffn_sw2"]])}
    for n in (1, 2):
        W0[n] = load_w0(n, [io[f"L0_ffn_w{i}"][n - 1] for i in (1, 3, 2)])

    meet(pe, act, dve)
    CH = 512
    gate_free = {}
    unit = 0
    free_h = [None, None]
    free_o = [None, None]

    def up_unit(wslot, hc, src, n, dst, waits, hT_free):
        nonlocal unit
        i = unit % 2
        unit += 1
        for j in range(2):
            for c in range(DC):
                fn = lambda e, j=j, c=c: e.matmul(PS[:, 2 * i + j, 0:n], w0[:, wslot, j, c, hc * P:(hc + 1) * P], src(c),
                                                  start=(c == 0), stop=(c == DC - 1))
                if c == DC - 1:
                    m = pe.mark(fn)
                else:
                    pe.run(fn, *waits, free_h[i])
                if c == DC - 1 and j == 0:
                    m_gate = m
        m1 = act.mark(lambda e: e.activation(gate[:, i, 0:n], PS[:, 2 * i, 0:n], ACT.Silu), m_gate, gate_free.get(i))
        m2 = dve.mark(lambda e: e.tensor_tensor(dst, gate[:, i, 0:n], PS[:, 2 * i + 1, 0:n], ALU.mult), m1, m, *hT_free)
        gate_free[i] = free_h[i] = m2
        return m2

    z_down = {}
    for k in range(N // CH + 1):
        if k < N // CH:
            for hc in range(2):
                up = up_unit(0, hc, lambda c, k=k: XFT[:, c, k * CH:(k + 1) * CH], CH, hT[:, k % 2, hc, 0:CH],
                             [W0[0]], [z_down.get(k - 2)])
            M["zh", k] = up
        if k > 0:
            kk = k - 1
            for u in range(CH // P // 2):
                i = 4 + u
                for t in range(2):
                    for hc in range(2):
                        fn = lambda e, u=u, t=t, hc=hc, i=i, kk=kk: e.matmul(
                            PS[:, i, t * D:(t + 1) * D], hT[:, kk % 2, hc, (2 * u + t) * P:(2 * u + t + 1) * P],
                            w0[:, 0, 2, hc, :], start=(hc == 0), stop=(hc == 1))
                        if t == 1 and hc == 1:
                            m = pe.mark(fn)
                        else:
                            pe.run(fn, M["zh", kk], free_o[u])
                tt = kk * (CH // P) + 2 * u
                free_o[u] = dve.mark(lambda e, tt=tt, i=i: e.tensor_tensor(
                    X[:, tt:tt + 2, :], X[:, tt:tt + 2, :], bank2(i), ALU.add), m)
            z_down[kk] = m

    stage("experts0")
    meet(pe, act, dve)
    NS0 = CAP0 // P
    all_stored = [M["stored", b] for b in range(B - NXF, B)]
    m_idx0 = Lane(sem("idx0_in")).dma(sp, lambda e: e.dma_start(
        idx0[:, :, :], table0.rearrange("(e p i) o -> p e (i o)", e=E0, p=P)), M["scat0"])
    XE, O = {}, {}

    def load_xe(n):
        for i in range(NS0):
            XE[n] = xe_in[n % NXE].dma(pool, lambda e, i=i: e.indirect_dma_start(
                xe[:, n % NXE, i, :], None, pooled, bass.IndirectOffsetOnAxis(ap=idx0[:, n, i:i + 1], axis=0)),
                m_idx0, *all_stored, M.get(("turned", n - NXE)))

    t_free = [None, None]

    def turn_xe(n):
        k = 0
        for u in range(-(-DC * NS0 // 4)):
            ids_ = range(4 * u, min(4 * u + 4, DC * NS0))
            for q in ids_:
                c, i = divmod(q, NS0)
                fn = lambda e, c=c, i=i, q=q, u=u: e.transpose(
                    PS[:, 4 + u % 2, (q % 4) * P:(q % 4 + 1) * P], xe[:, n % NXE, i, c * P:(c + 1) * P], ident[:, :])
                if q == ids_[-1]:
                    m = pe.mark(fn)
                else:
                    pe.run(fn, XE[n], t_free[u % 2])
            w = len(ids_) * P
            cp = lambda u=u, w=w: (xeT[:, n % 2, 4 * u * P:4 * u * P + w], PS[:, 4 + u % 2, 0:w])
            if u % 2:
                t_free[u % 2] = act.mark(lambda e, cp=cp: e.activation(*cp(), ACT.Copy), m, M.get(("up", n - 2)))
            else:
                t_free[u % 2] = dve.mark(lambda e, cp=cp: e.tensor_copy(*cp()), m, M.get(("up", n - 2)))
            M["xeT", n, u] = t_free[u % 2]
        M["turned", n] = m

    def up_expert(n):
        half = CAP0 // 2
        for hc in range(2):
            for q in range(2):
                m = up_unit((n + 1) % NW0, hc, lambda c, q=q: xeT[:, n % 2, c * CAP0 + q * half:c * CAP0 + (q + 1) * half], half,
                            hT[:, n % 2, hc, q * half:(q + 1) * half],
                            [W0[n + 1]] + [M["xeT", n, u] for u in range(3)], [M.get(("down", n - 2))])
        M["up", n] = pe.last
        M["hT", n] = m

    o_free = [None, None]

    def down_expert(n):
        for u in range(-(-NS0 // 2)):
            tiles = range(2 * u, min(2 * u + 2, NS0))
            for i in tiles:
                for hc in range(2):
                    fn = lambda e, i=i, hc=hc, u=u: e.matmul(
                        PS[:, 6 + u % 2, (i % 2) * D:(i % 2 + 1) * D], hT[:, n % 2, hc, i * P:(i + 1) * P],
                        w0[:, (n + 1) % NW0, 2, hc, :], start=(hc == 0), stop=(hc == 1))
                    if i == tiles[-1] and hc == 1:
                        m = pe.mark(fn)
                    else:
                        pe.run(fn, M["hT", n], o_free[u % 2])
            w = len(tiles)
            cp = lambda u=u, w=w: (res[:, n % 2, 2 * u:2 * u + w, :], PS[:, 6 + u % 2, 0:w * D].rearrange("p (a n) -> p a n", n=D))
            q = dve if u == 1 else act
            if q is dve:
                o_free[u % 2] = dve.mark(lambda e, cp=cp: e.tensor_copy(*cp()), m, O.get(n - 2))
            else:
                o_free[u % 2] = act.mark(lambda e, cp=cp: e.activation(*cp(), ACT.Copy), m, O.get(n - 2))
            M["res", n, u] = o_free[u % 2]
        M["down", n] = m

    def store_res(n):
        O[n] = res_out[n % 2].dma(sp, lambda e: e.dma_start(
            done0[n * CAP0:(n + 1) * CAP0, :].rearrange("(p s) d -> p s d", p=P), res[:, n % 2, :, :]),
            *[M["res", n, u] for u in range(3)])

    for n in range(2):
        load_xe(n)
    turn_xe(0)
    for n in range(E0):
        if n + 2 < E0:
            load_xe(n + 2)
        up_expert(n)
        if n + 1 < E0:
            turn_xe(n + 1)
        down_expert(n)
        if n == 0:
            W0[3] = load_w0(3, [io[f"L0_ffn_w{i}"][2] for i in (1, 3, 2)], z_down[N // CH - 1])
        if n + 4 <= E0:
            W0[n + 4] = load_w0(n + 4, [io[f"L0_ffn_w{i}"][n + 3] for i in (1, 3, 2)], M["down", n])
        store_res(n)
    all_done0 = [O[E0 - 2], O[E0 - 1]]
    region.close()

    stage("attn")
    meet(pe, act, dve, pool)
    region = ExitStack()
    ctx.enter_context(region)
    s = region
    ends = (pe.last, act.last, dve.last, pool.last)
    for q in (sp, pool, act, dve):
        q.wait(*ends, *all_done0)
    NGA = 2
    G0b = sb("G0b", [P, NGA, TB, K0, D], scope=s)
    WS = sb("WS", [P, 2, DC, D], scope=s)
    BS = sb("BS", [P, 2, D], scope=s)
    wqkv = sb("wqkv", [P, DC, 3 * D], scope=s)
    wproj = sb("wproj", [P, DC, D], scope=s)
    wgate = sb("wgate", [P, DC, E1], scope=s)
    lng = sb("lng", [P, 4, DC], scope=s)
    ropec = sb("ropec", [P, TB, 2, 2, HD // 2], scope=s)
    causal_f = sb("causal_f", [P, P], scope=s)
    causal = sb("causal", [P, HG, P], BF16, scope=s)
    ident_b = sb("ident_b", [P, P], BF16, scope=s)
    x1T = sb("x1T", [P, DC, T], scope=s)
    XC = sb("XC", [P, 3, TB, D], scope=s)
    st = sb("st", [P, 2, TB, 6], scope=s)
    mv = sb("mv", [P, 2, TB, 2], scope=s)
    ve = sb("ve", [P, 2, TB], scope=s)
    rs = sb("rs", [P, 2, TB], scope=s)
    xn = sb("xn", [P, TB, D], scope=s)
    hT1 = sb("hT1", [P, DC, T], scope=s)
    QK = sb("QK", [P, TB, 2, H, HP], scope=s)
    VP = sb("VP", [P, 2, TB, H, HP], scope=s)
    rm = sb("rm", [P, 2, 2, 2, H, HD], scope=s)
    qT = sb("qT", [P, NG, T], scope=s)
    KM = sb("KM", [P, NG, HG, T], scope=s)
    NPN = 2
    smax = sb("smax", [P, NPN, 2 * HG], scope=s)
    PN = sb("PN", [P, NPN, 3, 512], scope=s)
    PT = sb("PT", [P, NPN, 3, 512], scope=s)
    oT = sb("oT", [P, 2, NG, T], scope=s)
    rsum = sb("rsum", [P, TB, H], scope=s)
    at = sb("at", [P, TB, H, HD], scope=s)
    atT = sb("atT", [P, DC, T], scope=s)
    XR = sb("XR", [P, 2, TB, D], scope=s)
    NXN = 2
    XN2 = sb("XN2", [P, NXN, TB, D], scope=s)
    h2T = sb("h2T", [P, DC, T], scope=s)
    lgs = sb("lgs", [P, R * E1], scope=s)
    router1 = Router(region, "1", E1, K1, 0, CAP1, base1, w_pick1, slot1)
    gat0 = lanes("gat0_", NGA)
    ws_in = lanes("ws_in", 2)
    scat1 = Lane(sem("scat1"))
    xn_out = lanes("xn_out", NXN)
    base_out = Lane(sem("base_out"))
    attn_in = Lane(sem("attn_in"))
    out_v = out.rearrange("b (c p) d -> p (b c) d", p=P)

    for dst, src in ((causal_f[:, :], io["c_causal"]),
                     (wqkv[:, :, :], io["L1_ffn_WqkvT"].rearrange("(c p) f -> p c f", p=P)),
                     (wproj[:, :, :], io["L1_ffn_Wproj"].rearrange("(c p) f -> p c f", p=P)),
                     (wgate[:, :, :], io["L1_ffn_Wgate"].rearrange("(c p) f -> p c f", p=P)),
                     (lng[:, :, :], io["ln_cols"]), (ropec[:, :, :, :, :], io["c_rope"])):
        c_attn = attn_in.dma(sp, lambda e, d=dst, s_=src: e.dma_start(d, s_))
    W_all = io["L1_cond_W"].rearrange("c i o -> (c i) o")
    w1e_in = lanes("w1e_in", 2)
    W1E = {}

    def load_w1e(n, *marks):
        v = BIG[:, (n % 2) * N:(n % 2 + 1) * N]
        w1e_in[n % 2].dma(sp, lambda e: e.dma_start(v[:, 0:DC * F1].rearrange("p (c f) -> p c f", c=DC),
                                                    io["L1_ffn_W1"][n].rearrange("(c p) f -> p c f", p=P)), *marks)
        W1E[n] = w1e_in[n % 2].dma(sp, lambda e: e.dma_start(v[:, DC * F1:].rearrange("p (c f) -> p c f", f=D),
                                                             io["L1_ffn_W2"][n].rearrange("(c p) f -> p c f", p=P)))

    load_w1e(0)
    load_w1e(1)

    errands = []

    def run_errands(n):
        for _ in range(min(n, len(errands))):
            errands.pop(0)()

    def gather(b):
        def result(t, k):
            M["g0", b] = gat0[b % NGA].dma(pool, lambda e: e.indirect_dma_start(
                G0b[:, b % NGA, t, k, :], None, done0,
                bass.IndirectOffsetOnAxis(ap=slot0[:, TB * b + t, k:k + 1], axis=0)), M.get(("comb", b - NGA)), fill_end)

        def matrix(c):
            ws_in[b % 2].dma(pool, lambda e: e.indirect_dma_start(
                WS[:, b % 2, c, :], None, W_all, bass.IndirectOffsetOnAxis(ap=cat_row[:, b, c:c + 1], axis=0)),
                M.get(("xc_pe", b - 2)))

        def bias():
            M["ws", b] = ws_in[b % 2].dma(pool, lambda e: e.indirect_dma_start(
                BS[:, b % 2, :], None, io["L1_cond_b"], bass.IndirectOffsetOnAxis(ap=cat_id[:, b:b + 1], axis=0)),
                M.get(("xc", b - 2)))

        for t in range(TB):
            for k in range(K0):
                errands.append(lambda t=t, k=k: result(t, k))
        for c in range(DC):
            errands.append(lambda c=c: matrix(c))
        errands.append(bias)

    gather(0)
    run_errands(8)
    m_qk0 = pool.mark(lambda e: e.memset(QK[:, :, :, :, :], 0.0))
    m_vp0 = pool.mark(lambda e: e.memset(VP[:, :, :, :, :], 0.0))
    m_vp0 = pool.mark(lambda e: e.memset(VP[:, :, :, :, HD:HD + 1], 1.0), m_vp0)
    run_errands(99)
    gather(1)
    run_errands(99)
    for j in range(HG):
        dve.mark(lambda e, j=j: e.tensor_copy(causal[:, j, :], causal_f[:, :]), c_attn)
    m_causal = dve.mark(lambda e: e.tensor_copy(ident_b[:, :], ident[:, :]))

    TBANK, OBANK, LBANK = 3, 5, 6
    light_free = [None, None]
    lcount = [0]

    def light():
        i = lcount[0] % 2
        lcount[0] += 1
        return i, LBANK + i, light_free[i]

    def combine(b, half=None):
        for t in range(TB) if half is None else (half,):
            tt = TB * b + t
            for k in range(K0):
                M["comb", b] = dve.chain(lambda e, t=t, k=k, tt=tt: e.scalar_tensor_tensor(
                    X[:, tt, :], G0b[:, b % NGA, t, k, :], w_pick0[:, tt, k:k + 1], X[:, tt, :], ALU.mult, ALU.add),
                    M["g0", b])

    def a_turn(b):
        i, bank, free = light()
        m = transposes(bank, lambda t: X[:, TB * b + t, :], [M["comb", b], free])
        light_free[i] = M["x1T", b] = act.mark(lambda e: e.activation(x1T[:, :, :], bank2(bank), ACT.Copy),
                                               m, M.get(("xc_pe", b - 1)))

    def tokens_by(bank, src, w, waits):
        for t in range(TB):
            for c in range(DC):
                fn = lambda e, t=t, c=c: e.matmul(PS[:, bank, t * D:(t + 1) * D], src[:, c, t * P:(t + 1) * P], w(c),
                                                  start=(c == 0), stop=(c == DC - 1))
                if t == TB - 1 and c == DC - 1:
                    return pe.mark(fn)
                pe.run(fn, *waits)

    pending = []

    def run_pending():
        while pending:
            pending.pop(0)()

    def norm(src, j, dst, dst_free, then):
        for t in range(TB):
            dve.mark(lambda e, t=t: e.bn_stats(st[:, j, t, :], src[:, t, :]), dve.last)
        for t in range(TB):
            dve.chain(lambda e, t=t: e.bn_aggr(mv[:, j, t, :], st[:, j, t, :]))
        m = dve.chain(lambda e: e.tensor_scalar(ve[:, j, :], mv[:, j, :, 1], EPS, None, ALU.add))
        m = pool.mark(lambda e: e.tensor_tensor(rs[:, j, :], ve[:, j, :], nhalf[:, :], ALU.pow), m, m_nhalf)

        def scale():
            for t in range(TB):
                m2 = dve.mark(lambda e, t=t: e.tensor_scalar(dst[:, t, :], src[:, t, :], mv[:, j, t, 0:1], rs[:, j, t:t + 1],
                                                             ALU.subtract, ALU.mult), m, *dst_free)
            then(m2)

        pending.append(scale)

    def a_matrix(b):
        i, bank, free = light()
        M["xc_pe", b] = m = tokens_by(bank, x1T, lambda c: WS[:, b % 2, c, :], [M["x1T", b], M["ws", b], free])
        light_free[i] = M["xc", b] = dve.mark(lambda e: e.tensor_tensor(
            XC[:, b % 3, :, :], bank2(bank), wide(BS[:, b % 2, :], 1, [P, TB, D]), ALU.add), m, M.get(("xr", b - 3)))
        norm(XC[:, b % 3, :, :], 0, xn, [M.get(("xn_pe", b - 1))], lambda m: M.update({("xn", b): m}))

    def affine_turn(src, waits, j, dst, dst_free):
        i, bank, free = light()
        m = transposes(bank, src, [*waits, free])
        for c in range(DC):
            light_free[i] = act.mark(lambda e, c=c: e.activation(
                dst[:, c, :], PS[:, bank, c * T:(c + 1) * T], ACT.Identity,
                bias=lng[:, j + 1, c:c + 1], scale=lng[:, j, c:c + 1]), m, dst_free, c_attn)
        return m, light_free[i]

    def a_norm_turn(b):
        M["xn_pe", b], M["hT1", b] = affine_turn(lambda t: xn[:, t, :], [M["xn", b]], 0, hT1, M.get(("v_pe", b - 1)))

    def a_qk(b, t):
        i, bank, free = light()
        for c in range(DC):
            fn = lambda e, c=c: e.matmul(PS[:, bank, :], hT1[:, c, t * P:(t + 1) * P], wqkv[:, c, 0:2 * D],
                                         start=(c == 0), stop=(c == DC - 1))
            if c < DC - 1:
                pe.run(fn, M["hT1", b], free, c_attn)
        m = pe.mark(fn)
        halves = "p q (h a f) -> p q (h a) f"
        src = PS[:, bank, :].rearrange("p (q h f) -> p q h f", q=2, f=HD // 2)
        for cs in range(2):
            m1 = dve.mark(lambda e, cs=cs: e.tensor_tensor(
                rm[:, t, cs, :, :, :].rearrange("p q h (a f) -> p q (h a) f", a=2), src,
                wide(ropec[:, t, cs, :, :], 2, [P, 2, 2 * H, HD // 2]), ALU.mult), m, M.get(("rot", t)), c_attn)
        light_free[i] = m1
        h8 = HD // 2
        dst = QK[:, t, :, :, :]
        pool.mark(lambda e: e.tensor_tensor(dst[:, :, :, 0:h8], rm[:, t, 0, :, :, 0:h8], rm[:, t, 1, :, :, h8:], ALU.subtract),
                  m1, m_qk0, M.get(("qk_pe", b - 1)))
        M["rot", t] = M["qk", b, t] = pool.mark(lambda e: e.tensor_tensor(
            dst[:, :, :, h8:HD], rm[:, t, 1, :, :, 0:h8], rm[:, t, 0, :, :, h8:], ALU.add))

    def a_v(b):
        i, bank, free = light()
        M["v_pe", b] = m = tokens_by(bank, hT1, lambda c: wqkv[:, c, 2 * D:3 * D], [M["hT1", b], free])
        light_free[i] = M["vp", b] = act.mark(lambda e: e.activation(
            VP[:, b % 2, :, :, 0:HD], PS[:, bank, :].rearrange("p (t h f) -> p t h f", t=TB, h=H), ACT.Copy), m,
            m_vp0, M.get(("pv", b - 2)))

    def a_turn_heads(b, q, u):
        i, bank, free = light()
        for g in range(2):
            for t in range(TB):
                fn = lambda e, g=g, t=t: e.transpose(
                    PS[:, bank, g * T + t * P:g * T + (t + 1) * P],
                    QK[:, t, q, (2 * u + g) * HG:(2 * u + g + 1) * HG, :].rearrange("p h f -> p (h f)"), ident[:, :])
                if not (g == 1 and t == TB - 1):
                    pe.run(fn, M["qk", b, 0], M["qk", b, 1], free)
        M["qk_pe", b] = m = pe.mark(fn)
        if q == 0:
            light_free[i] = M["qT", b, u] = act.mark(lambda e: e.activation(
                qT[:, 2 * u:2 * u + 2, :], bank2(bank), ACT.Copy), m, M.get(("scores", b - 1, 2 * u + 1)))
        else:
            for g in range(2):
                mk = dve.mark(lambda e, g=g: e.tensor_tensor(
                    KM[:, 2 * u + g, :, :], wide(PS[:, bank, g * T:(g + 1) * T], 1, [P, HG, T]),
                    wide(heads, 2, [P, HG, T]), ALU.mult), m, M.get(("scores", b - 1, 2 * u + 1)))
            light_free[i] = M["KM", b, u] = mk

    s_free = [None] * 3

    def scores(b, g):
        slot = g % NPN
        for part in range(3):
            if part < 2:
                o = PS[:, part, :].rearrange("p (x h k) -> p x h k", x=2, h=2)[:, :, 1, :]
                mask_ = causal[:, 0:2, :]
            else:
                o, mask_ = PS[:, part, :].rearrange("p (x k) -> p x k", x=HG), causal[:, :, :]
            pe.run(lambda e, o=o, mask_=mask_: e.matmul(o, ident_b[:, :], mask_, start=True, stop=False, skip_group_check=True),
                   s_free[part], m_causal, M["qT", b, g // 2], M["KM", b, g // 2])
            if part < 2:
                for x in range(2):
                    fn = lambda e, x=x, part=part: e.matmul(PS[:, part, x * T:(x + 1) * T], qT[:, g, P:T], KM[:, g, 2 * part + x, :],
                                                            start=False, stop=True, skip_group_check=True)
                    if x == 0:
                        pe.run(fn)
                heads_, width, col = 2, T, 2 * part
            else:
                for j in range(HG):
                    fn = lambda e, j=j, part=part: e.matmul(PS[:, part, j * P:(j + 1) * P], qT[:, g, 0:P], KM[:, g, j, 0:P],
                                                            start=False, stop=True, skip_group_check=True)
                    if j < HG - 1:
                        pe.run(fn)
                heads_, width, col = HG, P, HG
            m = pe.mark(fn)
            M["smax", b, g, part] = dve.mark(lambda e, part=part, col=col, heads_=heads_: e.tensor_reduce(
                smax[:, slot, col:col + heads_], PS[:, part, :].rearrange("p (x k) -> p x k", x=heads_), AX.X, ALU.max, negate=True),
                m, M.get(("exp", slot)))
        M["scores", b, g] = pe.last

    def exponentials(b, g, part):
        slot = g % NPN
        heads_, width, col = (2, T, 2 * part) if part < 2 else (HG, P, HG)
        for x in range(heads_):
            s_free[part] = act.mark(lambda e, x=x: e.activation(
                PN[:, slot, part, x * width:(x + 1) * width], PS[:, part, x * width:(x + 1) * width], ACT.Exp,
                bias=smax[:, slot, col + x:col + x + 1]), M["smax", b, g, part], M.get(("turned_p", slot)))
        M["exp", slot] = M["exp", b, g] = s_free[part]

    t_free1 = [None, None]
    tcount = [0]

    def turn_p(b, g, part):
        slot = g % NPN
        i = tcount[0] % 2
        tcount[0] += 1
        bank = TBANK + i
        if part < 2:
            srcs = []
            for x in range(2):
                j = 2 * part + x
                srcs += [PN[:, slot, 2, j * P:(j + 1) * P], PN[:, slot, part, x * T:x * T + P]]
        else:
            srcs = [PN[:, slot, j // 2, (j % 2) * T + P:(j % 2 + 1) * T] for j in range(HG)]
        for k, src in enumerate(srcs):
            fn = lambda e, k=k, src=src: e.transpose(PS[:, bank, k * P:(k + 1) * P], src, ident[:, :])
            if k < HG - 1:
                pe.run(fn, M["exp", b, g], t_free1[i])
        m = pe.mark(fn)
        if part < 2:
            t_free1[i] = act.mark(lambda e: e.activation(PT[:, slot, part, :], PS[:, bank, :], ACT.Copy), m, M.get(("pv", slot)))
        else:
            t_free1[i] = dve.mark(lambda e: e.tensor_copy(PT[:, slot, part, :], PS[:, bank, :]), m, M.get(("pv", slot)))
        M["PT", b, g, part] = t_free1[i]
        M["turned_p", slot] = m

    o_free1 = [None]

    def values(b, g):
        slot = g % NPN
        for j in range(HG):
            hh = g * HG + j
            rows_ = slice(HP * j, HP * (j + 1))
            pe.run(lambda e, hh=hh, j=j, rows_=rows_: e.matmul(
                PS[rows_, OBANK, 0:T], VP[:, b % 2, 0, hh, :], PT[:, slot, j // 2, (j % 2) * T:(j % 2 + 1) * T],
                start=True, stop=False, skip_group_check=True), *[M["PT", b, g, q] for q in range(3)], o_free1[0], M["vp", b])
            fn = lambda e, hh=hh, j=j, rows_=rows_: e.matmul(
                PS[rows_, OBANK, P:T], VP[:, b % 2, 1, hh, :], PT[:, slot, 2, j * P:(j + 1) * P],
                start=False, stop=True, skip_group_check=True)
            if j < HG - 1:
                pe.run(fn)
        M["pv", b] = M["pv", slot] = m = pe.mark(fn)
        o_free1[0] = M["oT", b] = act.mark(lambda e: e.activation(oT[:, b % 2, g, :], PS[:, OBANK, 0:T], ACT.Copy), m, M.get(("o_pe", b - 2)))

    def a_outputs(b, t):
        i, bank, free = light()
        for g in range(NG):
            fn = lambda e, g=g: e.transpose(PS[:, bank, g * P:(g + 1) * P], oT[:, b % 2, g, t * P:(t + 1) * P], ident[:, :])
            if g < NG - 1:
                pe.run(fn, M["oT", b], free)
        M["o_pe", b] = m = pe.mark(fn)
        v = PS[:, bank, :].rearrange("p (h f) -> p h f", h=H)
        dve.mark(lambda e: e.reciprocal(rsum[:, t, :], v[:, :, HD]), m)
        light_free[i] = M["at", b] = dve.chain(lambda e: e.tensor_tensor(
            at[:, t, :, :], v[:, :, 0:HD], wide(rsum[:, t, :], 2, [P, H, HD]), ALU.mult), M.get(("at_pe", b - 1)))

    def a_out_turn(b):
        i, bank, free = light()
        M["at_pe", b] = m = transposes(bank, lambda t: at[:, t, :, :].rearrange("p h f -> p (h f)"), [M["at", b], free])
        light_free[i] = M["atT", b] = act.mark(lambda e: e.activation(atT[:, :, :], bank2(bank), ACT.Copy), m, M.get(("proj", b - 1)))

    def a_proj(b):
        i, bank, free = light()
        M["proj", b] = m = tokens_by(bank, atT, lambda c: wproj[:, c, :], [M["atT", b], free])
        j = b % 2
        light_free[i] = M["xr", b] = dve.mark(lambda e: e.tensor_tensor(XR[:, j, :, :], bank2(bank), XC[:, b % 3, :, :], ALU.add),
                                              m, M.get(("base", b - 2)))

        def store(m2):
            M["xn2", b] = m2
            M["xn_out", b] = xn_out[b % NXN].dma(sp, lambda e: e.dma_start(
                normed[b * T:(b + 1) * T, :].rearrange("(c p) d -> p c d", p=P), XN2[:, b % NXN, :, :]), m2)

        norm(XR[:, j, :, :], 1, XN2[:, b % NXN, :, :], [M.get(("xn_out", b - NXN)), M.get(("xn2_pe", b - NXN))], store)
        M["base", b] = pool.mark(lambda e: e.tensor_tensor(X[:, TB * b:TB * b + TB, :], X[:, TB * b:TB * b + TB, :], XR[:, j, :, :], ALU.add),
                                 M["xr", b])
        M["base_out"] = base_out.dma(sp, lambda e: e.dma_start(out_v[:, TB * b:TB * b + TB, :], X[:, TB * b:TB * b + TB, :]), M["base", b])

    def a_gate_turn(b):
        M["xn2_pe", b], M["h2T", b] = affine_turn(lambda t: XN2[:, b % NXN, t, :], [M["xn2", b]], 2, h2T, M.get(("lg1", b - 1)))

    def a_gate(b):
        i, bank, free = light()
        for t in range(TB):
            for c in range(DC):
                fn = lambda e, t=t, c=c: e.matmul(PS[:, bank, t * E1:(t + 1) * E1], h2T[:, c, t * P:(t + 1) * P], wgate[:, c, :],
                                                  start=(c == 0), stop=(c == DC - 1))
                if not (t == TB - 1 and c == DC - 1):
                    pe.run(fn, M["h2T", b], free)
        M["lg1", b] = pe.mark(fn)
        half = (b % GB) * TB * E1
        light_free[i] = dve.mark(lambda e: e.tensor_copy(lgs[:, half:half + TB * E1], PS[:, bank, 0:TB * E1]), M["lg1", b], dve.last)
        if b % GB == GB - 1:
            router1.choose(b // GB, lgs[:, :].rearrange("p (r e) -> p r e", r=R), dve.last)

    def a_dispatch(b):
        if b % GB != GB - 1:
            return
        g = b // GB
        i, bank, free = light()
        pe.wait(free)
        router1.rank(g, bank)
        light_free[i] = M["slot1", g]

        def entry(tt, k):
            M["scat1"] = scat1.dma(pool, lambda e: e.indirect_dma_start(
                table1, bass.IndirectOffsetOnAxis(ap=slot1[:, tt, k:k + 1], axis=0),
                pair1[:, tt, k, :], None, bounds_check=S1 - 1, oob_is_err=False), M["slot1", g], M["w1", g], m_pair, filled1)

        for tt in range(g * R, (g + 1) * R):
            for k in range(K1):
                errands.append(lambda tt=tt, k=k: entry(tt, k))

    def light_stages(b, g, gap):
        run_pending()
        for f, off in PLAN[g, gap]:
            if 0 <= b + off < B and not (b < 0 and f is gather):
                f(b + off)
        run_errands(2)

    PLAN = {
        (0, 0): [(a_turn, 1)], (0, 1): [(a_gate, -2)], (0, 2): [(a_matrix, 1)], (0, 3): [(a_dispatch, -2)],
        (1, 0): [(a_norm_turn, 1)], (1, 1): [(lambda b: a_qk(b, 0), 1)], (1, 2): [(lambda b: a_qk(b, 1), 1)],
        (1, 3): [(lambda b: combine(b, 0) if b > 1 else None, 2), (lambda b: a_outputs(b, 0), -1), (lambda b: a_outputs(b, 1), -1)],
        (2, 0): [(a_out_turn, -1)], (2, 1): [(a_v, 1)], (2, 2): [(a_proj, -1)], (2, 3): [(lambda b: combine(b, 1) if b > 1 else None, 2), (lambda b: a_turn_heads(b, 0, 0), 1)],
        (3, 0): [(lambda b: a_turn_heads(b, 1, 0), 1)], (3, 1): [(a_gate_turn, -1)],
        (3, 2): [(lambda b: a_turn_heads(b, 0, 1), 1), (gather, 3)], (3, 3): [(lambda b: a_turn_heads(b, 1, 1), 1)],
    }

    combine(0)
    combine(1)
    gather(2)
    for g in range(NG):
        for gap in range(4):
            light_stages(-1, g, gap)
    for b in range(B + 2):
        for g in range(NG):
            b1, g1 = (b, g - 1) if g >= 1 else (b - 1, g - 1 + NG)
            b2, g2 = (b, g - 2) if g >= 2 else (b - 1, g - 2 + NG)
            if b < B:
                scores(b, g)
            light_stages(b, g, 0)
            if b < B:
                exponentials(b, g, 0)
            if 0 <= b1 < B:
                turn_p(b1, g1, 0)
                turn_p(b1, g1, 1)
            if b < B:
                exponentials(b, g, 1)
            light_stages(b, g, 1)
            if 0 <= b1 < B:
                turn_p(b1, g1, 2)
            if b < B:
                exponentials(b, g, 2)
            light_stages(b, g, 2)
            if 0 <= b2 < B:
                values(b2, g2)
            light_stages(b, g, 3)
    run_errands(99)
    region.close()

    stage("experts1")
    meet(pe, act, dve, pool)
    region = ExitStack()
    ctx.enter_context(region)
    s = region
    ends = (pe.last, act.last, dve.last, pool.last)
    all_normed = [M["xn_out", b] for b in range(B - NXN, B)]
    for q in (sp, pool, act, dve):
        q.wait(*ends, *all_normed)
    HS = 512
    NH = CAP1 // HS
    NS1 = HS // P
    FC = F1 // P
    tab = sb("tab", [P, E1, CAP1 // P, 2], scope=s)
    xe1 = sb("xe1", [P, 3, NS1, D], scope=s)
    xe1T = sb("xe1T", [P, 2, DC, HS], scope=s)
    h1 = sb("h1", [P, 2, FC, HS], scope=s)
    b1s = sb("b1s", [P, E1, FC], scope=s)
    b2s = sb("b2s", [P, 2, D], scope=s)
    lng1 = sb("lng1", [P, 4, DC], scope=s)
    res1 = sb("res1", [P, 3, NS1, D], scope=s)
    xe1_in = lanes("xe1_in", 3)
    b2_in = lanes("b2_in", 2)
    res1_out = lanes("res1_out", 3)
    tab_in = Lane(sem("tab_in")).dma(sp, lambda e: e.dma_start(
        tab[:, :, :, :], table1.rearrange("(e p i) w -> p e i w", e=E1, p=P)), M["scat1"])
    e1_in = Lane(sem("e1_in"))
    e1_in.dma(sp, lambda e: e.dma_start(b1s[:, :, :], io["b1_cols"]))
    c_e1 = e1_in.dma(sp, lambda e: e.dma_start(lng1[:, :, :], io["ln_cols"]))
    units = [(n, h) for n in range(E1) for h in range(NH)]
    X1, B2, O1 = {}, {}, {}

    def who(n, h, i):
        return tab[:, n, h * NS1 + i, 0:1].bitcast(U32)

    def load1(u):
        n, h = units[u]
        for i in range(NS1):
            X1[u] = xe1_in[u % 3].dma(pool, lambda e, i=i: e.indirect_dma_start(
                xe1[:, u % 3, i, :], None, normed, bass.IndirectOffsetOnAxis(ap=who(n, h, i), axis=0)),
                tab_in, M.get(("t1", u - 3)), fill_end)
        if h == 0:
            B2[n] = b2_in[n % 2].dma(sp, lambda e: e.dma_start(b2s[:, n % 2, :], io["L1_ffn_b2"][n].partition_broadcast(P)),
                                     M.get(("r1", u - NH - 1)))

    tb_free = [None, None]

    def turn1(u):
        for c in range(DC):
            for i in range(NS1):
                fn = lambda e, c=c, i=i: e.transpose(PS[:, c, i * P:(i + 1) * P], xe1[:, u % 3, i, c * P:(c + 1) * P], ident[:, :])
                if i < NS1 - 1:
                    pe.run(fn, X1[u], tb_free[c])
            m = pe.mark(fn)
            tb_free[c] = M["x1eT", u, c] = dve.mark(lambda e, c=c: e.tensor_scalar(
                xe1T[:, u % 2, c, :], PS[:, c, :], lng1[:, 2, c:c + 1], lng1[:, 3, c:c + 1], ALU.mult, ALU.add),
                m, c_e1, M.get(("u1", u - 2)))
        M["t1", u] = m

    ub_free = [None] * 3
    ub = [0]

    def up1(u):
        n, h = units[u]
        wv = BIG[:, (n % 2) * N:(n % 2) * N + DC * F1].rearrange("p (c f) -> p c f", c=DC)
        for f in range(FC):
            k = ub[0] % 3
            ub[0] += 1
            for c in range(DC):
                fn = lambda e, c=c, f=f, k=k: e.matmul(PS[:, 2 + k, :], wv[:, c, f * P:(f + 1) * P], xe1T[:, u % 2, c, :],
                                                       start=(c == 0), stop=(c == DC - 1))
                if c == 0:
                    pe.run(fn, W1E[n], M["x1eT", u, 0], M["x1eT", u, 1], ub_free[k])
            m = pe.mark(fn)
            ub_free[k] = act.mark(lambda e, f=f, k=k: e.activation(h1[:, u % 2, f, :], PS[:, 2 + k, :], ACT.Gelu, bias=b1s[:, n, f:f + 1]),
                                  m, c_e1, M.get(("d1", u - 2)))
        M["u1", u] = m
        M["h1", u] = ub_free[k]

    db_free = [None, None]

    def down1(u):
        n, h = units[u]
        wv = BIG[:, (n % 2) * N + DC * F1:(n % 2 + 1) * N].rearrange("p (c f) -> p c f", f=D)
        for q in range(NS1 // 2):
            for i in range(2 * q, 2 * q + 2):
                for f in range(FC):
                    fn = lambda e, i=i, f=f, q=q: e.matmul(PS[:, 5 + q, (i % 2) * D:(i % 2 + 1) * D], h1[:, u % 2, f, i * P:(i + 1) * P],
                                                           wv[:, f, :], start=(f == 0), stop=(f == FC - 1))
                    if not (i % 2 and f == FC - 1):
                        pe.run(fn, M["h1", u], db_free[q])
            m = pe.mark(fn)
            db_free[q] = M["r1", u] = dve.mark(lambda e, q=q: e.tensor_tensor(
                res1[:, u % 3, 2 * q:2 * q + 2, :], bank2(5 + q), wide(b2s[:, n % 2, :], 1, [P, 2, D]), ALU.add),
                m, B2[n], O1.get(u - 3))
            for i in range(2 * q, 2 * q + 2):
                mg = dve.mark(lambda e, i=i: e.tensor_scalar(res1[:, u % 3, i, :], res1[:, u % 3, i, :],
                                                             tab[:, n, h * NS1 + i, 1:2], None, ALU.mult), M["r1", u])
                O1[u] = res1_out[u % 3].dma(pool, lambda e, i=i: e.indirect_dma_start(
                    out_rows, bass.IndirectOffsetOnAxis(ap=who(n, h, i), axis=0), res1[:, u % 3, i, :], None,
                    bounds_check=N - 1, oob_is_err=False, compute_op=ALU.add),
                    mg, M["base_out"], *[O1.get(v) for v in range(u - 2 - h, u - h)])
        M["d1", u] = m

    out_rows = out.rearrange("b t d -> (b t) d")
    load1(0)
    load1(1)
    turn1(0)
    for u in range(len(units)):
        n, h = units[u]
        up1(u)
        if u + 1 < len(units):
            turn1(u + 1)
        if u + 2 < len(units):
            load1(u + 2)
        down1(u)
        if h == NH - 1 and n + 2 < E1:
            load_w1e(n + 2, M["d1", u])
    sp.wait(*[O1[u] for u in range(len(units) - 3, len(units))], M["base_out"], fill_end, filled0, filled1,
            *all_done0, *all_stored, *all_normed, M["scat0"], M["scat1"])
    region.close()

    block = ctx.enter_context(nc.Block())

    @block.sync
    def _(e):
        sp.play(e)

    @block.gpsimd
    def _(e):
        pool.play(e)

    @block.tensor
    def _(e):
        pe.play(e)

    @block.scalar
    def _(e):
        act.play(e)

    @block.vector
    def _(e):
        dve.play(e)


def lay_out(inputs):
    a = {k: np.asarray(v) for k, v in inputs.items()}
    m = {k: a[k] for k in ("x", "itok_B_0_2", "itok_B_0_30", "L0_cond_W1", "L0_ffn_w1", "L0_ffn_w2", "L0_ffn_w3",
                           "L0_ffn_sw1", "L0_ffn_sw2", "L0_ffn_sw3", "L1_cond_W", "L1_cond_b", "L1_ffn_Wproj",
                           "L1_ffn_Wgate", "L1_ffn_W1", "L1_ffn_W2", "L1_ffn_b2")}
    m["L0_cond_b1"] = a["L0_cond_b1"].reshape(A0, 1)
    m["L0_cond_v"] = a["L0_cond_v"].reshape(A0, 1)
    m["L0_ffn_wgT"] = a["L0_ffn_wg"].T
    m["L1_ffn_WqkvT"] = a["L1_ffn_Wqkv"].reshape(D, H, 3, HD).transpose(0, 2, 1, 3).reshape(D, 3 * D)
    col = lambda v: v.reshape(DC, P).T
    m["ln_cols"] = np.stack([col(a[f"L1_ffn_{n}"]) for n in ("ln1_g", "ln1_b", "ln2_g", "ln2_b")], 1)
    m["b1_cols"] = a["L1_ffn_b1"].reshape(E1, F1 // P, P).transpose(2, 0, 1)
    m.update(shape_constants())
    return {k: np.ascontiguousarray(v) for k, v in m.items()}


def kernel(**inputs):
    import concourse.bacc as _bacc
    from concourse.bass_utils import run_bass_kernel_spmd as _run

    nc = _bacc.Bacc("TRN2", target_bir_lowering=False, num_devices=1)
    arrays = lay_out(inputs)
    io = {k: nc.dram_tensor(f"in_{k}", v.shape, mybir.dt.from_np(v.dtype), kind="ExternalInput").ap() for k, v in arrays.items()}
    out = nc.dram_tensor("out_0", (B, T, D), F32, kind="ExternalOutput").ap()
    bass_adaln_ffn(nc, io, out)
    r = _run(nc, [{f"in_{k}": v for k, v in arrays.items()}], core_ids=[0])
    return r.results[0]["out_0"]
```

```python
from contextlib import ExitStack

import numpy as np

import concourse.bass as bass
from concourse import mybir

F32 = mybir.dt.float32
BF16 = mybir.dt.bfloat16
F32R = mybir.dt.float32r
I32 = mybir.dt.int32
U32 = mybir.dt.uint32
ALU = mybir.AluOpType
ACT = mybir.ActivationFunctionType
AX = mybir.AxisListType

P = 128
B, T, D = 16, 256, 256
N = B * T
NT = N // P
TB = T // P
DC = D // P
A0 = 64
E0, K0, G0, KG0 = 32, 4, 8, 4
CAP0 = int(1.25 * N * K0 / E0)
S0 = E0 * CAP0
E1, K1 = 8, 2
CAP1 = -(-2 * N // E1)
S1 = E1 * CAP1
F1 = 4 * D
H, HD = 16, 16
HP = 32
HG = P // HP
NG = H // HG
EPS = 1e-5
NEG = -1e30


class Mark:

    def __init__(self, sem, value):
        self.sem, self.value = sem, value


class Queue:

    def __init__(self, new_sem, name):
        self.new_sem, self.name = new_sem, name
        self.steps, self.seen, self.last = [], {}, None

    def stage(self, what):
        self.sem, self.count = self.new_sem(f"{self.name}_{what}"), 0

    def wait(self, *marks):
        for m in marks:
            if m is not None and self.seen.get(id(m.sem), 0) < m.value:
                self.seen[id(m.sem)] = m.value
                self.steps.append(lambda e, m=m: e.wait_ge(m.sem, m.value))

    def run(self, fn, *marks):
        self.wait(*marks)
        self.steps.append(fn)

    def mark(self, fn, *marks):
        self.wait(*marks)
        self.count += 1
        self.last = Mark(self.sem, self.count)
        self.steps.append(lambda e, s=self.sem: fn(e).then_inc(s, 1))
        return self.last

    def chain(self, fn, *marks):
        return self.mark(fn, self.last, *marks)

    def play(self, engine):
        for step in self.steps:
            step(engine)


class Lane:

    def __init__(self, sem):
        self.sem, self.count = sem, 0

    def dma(self, queue, fn, *marks):
        queue.wait(*marks)
        self.count += 16
        queue.steps.append(lambda e: fn(e).then_inc(self.sem, 16))
        return Mark(self.sem, self.count)


def wide(ap, axis, shape):
    return ap.unsqueeze(axis).broadcast_to(shape)


def shape_constants():
    p = np.arange(P)
    ident = np.eye(P, dtype=np.float32)
    before = (p[:, None] < p[None, :]).astype(np.float32)
    j = np.arange(T).reshape(TB, P).T[:, :, None]
    l = np.arange(T)[None, None, :]
    side = np.broadcast_to(np.sign(l - j), (P, TB, T))
    cnt = [m.sum(-1) * 1.0 for m in (l <= j, l >= j, l != j)]
    cnts = np.stack([cnt[2], cnt[0] - cnt[2], cnt[1] - cnt[2]], 1).astype(np.float32)
    inv = (1.0 / 10000.0 ** (np.arange(0, HD, 2, dtype=np.float32) / HD)).astype(np.float32)
    ang = np.arange(T, dtype=np.float32)[:, None] * inv
    cs = np.stack([np.cos(ang), np.sin(ang)]).astype(np.float32)
    rope = np.stack([cs / np.float32(HD ** 0.5), cs], 1)
    rope = rope.reshape(2, 2, TB, P, HD // 2).transpose(3, 2, 0, 1, 4)
    tri_q = np.where(p[None, :] > p[:, None], -1e9, 0.0)
    small = np.concatenate([
        np.tile(np.arange(G0), (P, 1)), np.tile(np.arange(E0), (P, 1)),
        np.tile(np.arange(E0) * CAP0 - S0, (P, 1)), np.tile(np.arange(E1) * CAP1 - S1, (P, 1)),
        p[:, None] + P * np.arange(DC)[None, :]], 1)
    token = (p[:, None] + P * np.arange(NT)[None, :]).astype(np.int32)
    empty = np.zeros((S1, 2), np.float32)
    empty[:, 0] = np.full(S1, N, np.int32).view(np.float32)
    f = lambda a: np.ascontiguousarray(a, dtype=np.float32)
    return {"c_ident": f(ident), "c_before": f(before), "c_side": f(side), "c_cnt": f(cnts),
            "c_rope": f(rope), "c_causal": f(tri_q), "c_small": f(small),
            "c_token": token, "c_empty": empty}


def bass_adaln_ffn(nc, io, out):
    ctx = ExitStack()
    with ctx:
        return _build(nc, ctx, io, out)


def _build(nc, ctx, io, out):
    def sem(name):
        return ctx.enter_context(nc.semaphore(name))

    def lanes(name, n):
        return [Lane(sem(f"{name}{i}")) for i in range(n)]

    def sb(name, shape, dt=F32, scope=ctx):
        return scope.enter_context(nc.sbuf_tensor(name, shape, dt))

    pe, act, dve, pool, sp = (Queue(sem, n) for n in ("pe", "act", "dve", "pool", "sp"))
    engines = [pe, act, dve, pool]

    def stage(name):
        for q in engines:
            q.stage(name)

    def meet(*queues):
        ends = [q.last for q in queues]
        for q in queues:
            q.wait(*ends)

    stage("pool0")
    PS = ctx.enter_context(nc.psum_tensor("banks", [P, 8, 512], F32))

    pooled = nc.dram_tensor("pooled", (N, D), F32, kind="Internal").ap()
    table0 = nc.dram_tensor("table0", (S0, 1), U32, kind="Internal").ap()
    done0 = nc.dram_tensor("done0", (S0 + 1, D), F32, kind="Internal").ap()
    normed = nc.dram_tensor("normed", (N + 1, D), F32, kind="Internal").ap()
    table1 = nc.dram_tensor("table1", (S1, 2), F32, kind="Internal").ap()

    X = sb("X", [P, NT, D])
    BIG = sb("BIG", [P, DC * N])
    XFT = BIG[:, :].rearrange("p (c n) -> p c n", c=DC)
    ident = sb("ident", [P, P])
    before = sb("before", [P, P])
    ones = sb("ones", [P, P])
    small = sb("small", [P, G0 + 2 * E0 + E1 + DC])
    iota = small[:, G0:G0 + E0]
    base0 = small[:, G0 + E0:G0 + 2 * E0]
    base1 = small[:, G0 + 2 * E0:G0 + 2 * E0 + E1]
    rows = small[:, G0 + 2 * E0 + E1:]
    w_pick0 = sb("w_pick0", [P, NT, K0])
    slot0 = sb("slot0", [P, NT, K0], U32)
    pair1 = sb("pair1", [P, NT, K1, 2])
    w_pick1 = pair1[:, :, :, 1]
    token = sb("token", [P, NT], I32)
    slot1 = sb("slot1", [P, NT, K1], U32)
    cat_row = sb("cat_row", [P, B, DC], U32)
    cat_id = sb("cat_id", [P, B], U32)
    idx0 = sb("idx0", [P, E0, CAP0 // P], U32)
    nhalf = sb("nhalf", [P, TB])

    consts = Lane(sem("consts_in"))
    for dst, name in ((ident, "c_ident"), (before, "c_before"), (small, "c_small"), (token, "c_token")):
        c_base = consts.dma(sp, lambda e, d=dst, n=name: e.dma_start(d[:, :], io[n]))
    x_in = lanes("x_in", 4)
    x_v = io["x"].rearrange("b (c p) d -> p (b c) d", p=P)
    x_ready = {}
    M = {}

    def load_x(q, w):
        x_ready[q] = x_in[q].dma(sp, lambda e: e.dma_start(
            X[:, q * 8:q * 8 + w, :], x_v[:, q * 8:q * 8 + w, :]))

    NW0 = 3
    layer0 = ExitStack()
    ctx.enter_context(layer0)
    w0 = sb("w0", [P, NW0, 3, DC * D], scope=layer0)
    R = 4

    class Router:

        def __init__(self, scope, tag, E, K, groups, cap, base, weights, slots):
            self.E, self.K, self.groups, self.cap, self.base = E, K, groups, cap, base
            self.weights, self.slots, self.tag = weights, slots, tag
            f = lambda n, *shape, dt=F32: sb(f"{n}_{tag}", [P, *shape], dt, scope)
            self.nm, self.sh, self.ex = f("nm", R), f("sh", R, E), f("ex", R, E)
            self.tv, self.ti, self.tf = f("tv", R, 8), f("ti", R, 8, dt=U32), f("tf", R, 8)
            self.hit = f("hit", R, K, E)
            self.sel, self.cum = f("sel", R, E), f("cum", R + 1, E)
            self.sm, self.ok, self.sf = f("sm", R, E), f("ok", R, E), f("sf", R, K)
            self.den, self.top = f("den", R), f("top", R)
            self.pick = f("pick", R, K, E)
            if groups:
                self.gs, self.gv, self.gi, self.gf = f("gs", R, groups), f("gv", R, 8), f("gi", R, 8, dt=U32), f("gf", R, 8)
                self.ghit, self.gk, self.gm = f("ghit", R, KG0, groups), f("gk", R, groups), f("gm", R, groups)
                self.cand = f("cand", R, E)
            self.todo = []
            dve.mark(lambda e: e.memset(self.cum[:, R, :], 0.0))

        def choose(self, g, logits, m_logits):
            E, K, t0 = self.E, self.K, g * R
            later = lambda fn, key=None: self.todo.append(lambda: dve.chain(fn, M.get(key)))
            S3 = [P, R, E]
            dve.chain(lambda e: e.tensor_reduce(self.nm[:, :], logits, AX.X, ALU.max, negate=True), m_logits)
            m = dve.chain(lambda e: e.tensor_tensor(self.sh[:, :, :], logits, wide(self.nm[:, :], 2, S3), ALU.add))
            m = act.mark(lambda e: e.activation(self.ex[:, :, :], self.sh[:, :, :], ACT.Exp), m)
            M["choose_free" + self.tag] = dve.last
            self.todo.append(lambda: dve.wait(m))
            cand = self.ex
            if self.groups:
                G = self.groups
                later(lambda e: e.tensor_reduce(self.gs[:, :, :], self.ex[:, :, :].rearrange("p r (g k) -> p r g k", g=G),
                                                   AX.X, ALU.max))
                for r in range(R):
                    later(lambda e, r=r: e.max(self.gv[:, r, :], self.gs[:, r, :]))
                for r in range(R):
                    later(lambda e, r=r: e.max_index(self.gi[:, r, :], self.gv[:, r, :], self.gs[:, r, :]))
                later(lambda e: e.tensor_copy(self.gf[:, :, :], self.gi[:, :, :]))
                later(lambda e: e.tensor_tensor(self.ghit[:, :, :, :], wide(wide(iota[:, 0:G], 1, [P, R, G]), 2, [P, R, KG0, G]),
                                                    wide(self.gf[:, :, 0:KG0], 3, [P, R, KG0, G]), ALU.is_equal))
                later(lambda e: e.tensor_reduce(self.gk[:, :, :], self.ghit[:, :, :, :].rearrange("p r k g -> p r g k"),
                                                    AX.X, ALU.add))
                later(lambda e: e.tensor_scalar(self.gm[:, :, :], self.gk[:, :, :], -1.0, None, ALU.add))
                v4 = lambda a: a[:, :, :].rearrange("p r (g k) -> p r g k", g=G)
                SG = [P, R, G, E // G]
                later(lambda e: e.tensor_tensor(v4(self.cand), v4(self.ex), wide(self.gk[:, :, :], 3, SG), ALU.mult))
                later(lambda e: e.tensor_tensor(v4(self.cand), v4(self.cand), wide(self.gm[:, :, :], 3, SG), ALU.add))
                cand = self.cand
            for r in range(R):
                later(lambda e, r=r: e.max(self.tv[:, r, :], cand[:, r, :]))
            for r in range(R):
                later(lambda e, r=r: e.max_index(self.ti[:, r, :], self.tv[:, r, :], cand[:, r, :]))
            later(lambda e: e.tensor_copy(self.tf[:, :, :], self.ti[:, :, :]))
            S4 = [P, R, K, E]
            later(lambda e: e.tensor_tensor(self.hit[:, :, :, :], wide(wide(iota[:, 0:E], 1, S3), 2, S4),
                                                wide(self.tf[:, :, 0:K], 3, S4), ALU.is_equal))
            later(lambda e: e.tensor_reduce(self.sel[:, :, :], self.hit[:, :, :, :].rearrange("p r k e -> p r e k"),
                                            AX.X, ALU.add), ("rank" + self.tag, g - 1))
            later(lambda e: e.tensor_copy(self.cum[:, 0, :], self.cum[:, R, :]))
            for r in range(R):
                later(lambda e, r=r: e.tensor_tensor(self.cum[:, r + 1, :], self.cum[:, r, :], self.sel[:, r, :], ALU.add))
            self.todo.append(lambda: M.update({("sel" + self.tag, g): dve.last}))
            later(lambda e: e.tensor_reduce(self.den[:, :], self.ex[:, :, :], AX.X, ALU.add))
            if self.groups:
                later(lambda e: e.tensor_reduce(self.top[:, :], self.tv[:, :, 0:K], AX.X, ALU.add))
                later(lambda e: e.scalar_tensor_tensor(self.den[:, :], self.den[:, :], 1e-9, self.top[:, :], ALU.mult, ALU.add))
            later(lambda e: e.reciprocal(self.den[:, :], self.den[:, :]))
            later(lambda e: e.tensor_tensor(
                self.weights[:, t0:t0 + R, :], self.tv[:, :, 0:K], wide(self.den[:, :], 2, [P, R, K]), ALU.mult))
            self.todo.append(lambda: M.update({("w" + self.tag, g): dve.last}))

        def go_on(self, n=99):
            for _ in range(min(n, len(self.todo))):
                self.todo.pop(0)()

        def rank(self, g, bank):
            E, K, t0 = self.E, self.K, g * R
            for r in range(R):
                o = PS[:, bank, r * E:(r + 1) * E]
                pe.run(lambda e, r=r, o=o: e.matmul(o, before[:, :], self.sel[:, r, :], start=True, stop=False),
                       M["sel" + self.tag, g], M.get(("slot" + self.tag, g - 1)), m_ones)
                fn = lambda e, r=r, o=o: e.matmul(o, ones[:, :], self.cum[:, r, :], start=False, stop=True)
                if r < R - 1:
                    pe.run(fn)
            M["rank" + self.tag, g] = m = pe.mark(fn)
            pos = PS[:, bank, 0:R * E].rearrange("p (r e) -> p r e", r=R)
            S3, S4 = [P, R, E], [P, R, K, E]
            dve.mark(lambda e: e.tensor_scalar(self.ok[:, :, :], pos, float(self.cap), None, ALU.is_lt), m)
            dve.mark(lambda e: e.tensor_tensor(self.sm[:, :, :], pos, wide(self.base, 1, S3), ALU.add))
            dve.chain(lambda e: e.tensor_tensor(self.sm[:, :, :], self.sm[:, :, :], self.ok[:, :, :], ALU.mult))
            dve.chain(lambda e: e.tensor_tensor(self.pick[:, :, :, :], self.hit[:, :, :, :], wide(self.sm[:, :, :], 2, S4), ALU.mult))
            dve.chain(lambda e: e.tensor_reduce(self.sf[:, :, :], self.pick[:, :, :, :], AX.X, ALU.add))
            M["slot" + self.tag, g] = dve.chain(lambda e: e.tensor_scalar(
                self.slots[:, t0:t0 + R, :], self.sf[:, :, :], float(self.cap * E), None, ALU.add))

    router0 = Router(layer0, "0", E0, K0, G0, CAP0, base0, w_pick0, slot0)
    region = ExitStack()
    layer0.enter_context(region)
    s = region
    w1c = sb("w1c", [P, DC, A0], scope=s)
    b1c = sb("b1c", [A0, 1], scope=s)
    vc = sb("vc", [A0, 1], scope=s)
    vb = sb("vb", [A0, P], scope=s)
    wgT = sb("wgT", [P, DC, E0], scope=s)
    side = sb("side", [P, TB, T], scope=s)
    cntc = sb("cntc", [P, 3, TB], scope=s)
    ids_i = sb("ids_i", [P, 2, B], I32, scope=s)
    ids = sb("ids", [P, 2, B], scope=s)
    kind = sb("kind", [P, 2, B], scope=s)
    left_out = sb("left_out", [P, B], scope=s)
    cnt = sb("cnt", [P, B, TB], scope=s)
    cat_f = sb("cat_f", [P, B, DC], scope=s)
    zeros = sb("zeros", [P, D], scope=s)
    xT = sb("xT", [P, 2, DC, T], scope=s)
    aT = sb("aT", [A0, 2, T], scope=s)
    mask = sb("mask", [P, 2, TB, T], scope=s)
    msc = sb("msc", [P, 2, TB, T], scope=s)
    pr = sb("pr", [P, 2, TB, T], scope=s)
    nmax = sb("nmax", [P, 2, TB], scope=s)
    psum_ = sb("psum_", [P, 2, TB], scope=s)
    pinv = sb("pinv", [P, 2, TB], scope=s)
    prT = sb("prT", [P, 2, TB, T], scope=s)
    NXF = 4
    xf_out = lanes("xf_out", NXF)
    XF = sb("XF", [P, NXF, TB, D], scope=s)

    load_x(0, 8)
    cond_in = Lane(sem("cond_in"))
    for dst, src in ((w1c, io["L0_cond_W1"].rearrange("(c p) a -> p c a", p=P)), (b1c, io["L0_cond_b1"]),
                     (vc, io["L0_cond_v"]), (wgT, io["L0_ffn_wgT"].rearrange("(c p) e -> p c e", p=P)),
                     (side, io["c_side"]), (cntc, io["c_cnt"])):
        c_cond = cond_in.dma(sp, lambda e, d=dst, s_=src: e.dma_start(d[tuple([slice(None)] * len(d.shape))], s_))
    c_cond = cond_in.dma(sp, lambda e: e.dma_start(ids_i[:, 0, :], io["itok_B_0_2"].partition_broadcast(P)))
    c_cond = cond_in.dma(sp, lambda e: e.dma_start(ids_i[:, 1, :], io["itok_B_0_30"].partition_broadcast(P)))
    for q in range(1, 4):
        load_x(q, 8)

    m_ones = pool.mark(lambda e: e.memset(ones[:, :], 1.0))
    m_zero = pool.mark(lambda e: e.memset(zeros[:, :], 0.0))
    m_nhalf = pool.mark(lambda e: e.memset(nhalf[:, :], -0.5))
    dve.chain(lambda e: e.tensor_copy(ids[:, :, :], ids_i[:, :, :]), c_cond)
    for i in range(2):
        m = dve.mark(lambda e, i=i: e.tensor_scalar(kind[:, i, :], ids[:, 0, :], float(i), None, ALU.is_equal), dve.last)
    dve.chain(lambda e: e.tensor_tensor(left_out[:, :], kind[:, 0, :], kind[:, 1, :], ALU.subtract))
    for c in range(TB):
        dve.chain(lambda e, c=c: e.tensor_scalar(cnt[:, :, c], kind[:, 0, :], cntc[:, 1, c:c + 1], cntc[:, 0, c:c + 1],
                                                 ALU.mult, ALU.add))
        dve.chain(lambda e, c=c: e.scalar_tensor_tensor(cnt[:, :, c], kind[:, 1, :], cntc[:, 2, c:c + 1],
                                                        cnt[:, :, c], ALU.mult, ALU.add))
    for c in range(DC):
        dve.chain(lambda e, c=c: e.tensor_scalar(cat_f[:, :, c], ids[:, 1, :], float(D), rows[:, c:c + 1],
                                                 ALU.mult, ALU.add))
    dve.chain(lambda e: e.tensor_copy(cat_row[:, :, :], cat_f[:, :, :]))
    m_cat = dve.chain(lambda e: e.tensor_copy(cat_id[:, :], ids[:, 1, :]))
    m_left = dve.last
    m_vb = dve.mark(lambda e: e.tensor_copy(vb[:, :], vc[:, :].broadcast_to([A0, P])))

    for k in range(K1):
        m_pair = dve.chain(lambda e, k=k: e.tensor_copy(pair1[:, :, k, 0].bitcast(I32), token[:, :]), c_base)

    filled0 = Lane(sem("fill0")).dma(sp, lambda e: e.dma_start(
        table0.rearrange("(p r) o -> p (r o)", p=P), zeros[:, 0:S0 // P].bitcast(U32)), m_zero)
    filled1 = Lane(sem("fill1")).dma(sp, lambda e: e.dma_start(table1, io["c_empty"]))
    fill_last = Lane(sem("fill_last"))
    for t_, n_ in ((done0, S0), (normed, N)):
        fill_end = fill_last.dma(sp, lambda e, t_=t_, n_=n_: e.dma_start(t_[n_:n_ + 1, :], zeros[0:1, 0:D]), m_zero)

    def transposes(bank, src, waits):
        for c in range(DC):
            for t in range(TB):
                fn = lambda e, c=c, t=t: e.transpose(PS[:, bank, c * T + t * P:c * T + (t + 1) * P],
                                                     src(t)[:, c * P:(c + 1) * P], ident[:, :])
                if c == DC - 1 and t == TB - 1:
                    return pe.mark(fn, *waits)
                pe.run(fn, *waits)

    def bank2(bank, n=T):
        return PS[:, bank, :].rearrange("p (a n) -> p a n", n=n)

    def p_transpose(b):
        m = transposes(0, lambda t: X[:, TB * b + t, :], [c_base, x_ready[b // 4], M.get(("xT", b - 1))])
        M["xT", b] = act.mark(lambda e: e.activation(xT[:, b % 2, :, :], bank2(0), ACT.Copy), m, M.get(("hid", b - 2)))

    def p_hidden(b):
        for c in range(DC):
            fn = lambda e, c=c: e.matmul(PS[0:A0, 1, 0:T], w1c[:, c, :], xT[:, b % 2, c, :], start=(c == 0), stop=(c == DC - 1))
            if c < DC - 1:
                pe.run(fn, M["xT", b], M.get(("aT", b - 1)), c_cond)
        M["hid", b] = m = pe.mark(fn)
        M["aT", b] = act.mark(lambda e: e.activation(aT[:, b % 2, :], PS[0:A0, 1, 0:T], ACT.Tanh, bias=b1c[:, 0:1]),
                              m, c_cond, M.get(("sc", b - 2)))

    def p_mask(b):
        i = b % 2
        M["mask", b] = dve.mark(lambda e: e.tensor_scalar(mask[:, i, :, :], side[:, :, :], left_out[:, b:b + 1], NEG,
                                                          ALU.is_equal, ALU.mult), M.get(("msc", b - 2)), m_left)

    def p_scores(b):
        i = b % 2
        M["sc", b] = m = pe.mark(lambda e: e.matmul(PS[:, 2, 0:T], vb[:, :], aT[:, i, :], start=True, stop=True),
                                 M["aT", b], m_vb, M.get(("msc", b - 1)))
        M["msc", b] = dve.mark(lambda e: e.tensor_tensor(msc[:, i, :, :], mask[:, i, :, :], wide(PS[:, 2, 0:T], 1, [P, TB, T]),
                                                         ALU.add), m, M["mask", b], M.get(("exp", b - 2)))
        m = dve.chain(lambda e: e.tensor_reduce(nmax[:, i, :], msc[:, i, :, :], AX.X, ALU.max, negate=True))
        for c in range(TB):
            m2 = act.mark(lambda e, c=c: e.activation(pr[:, i, c, :], msc[:, i, c, :], ACT.Exp, bias=nmax[:, i, c:c + 1],
                                                      accum_out=psum_[:, i, c:c + 1]), m, M.get(("prT_pe", b - 2)),
                          M.get(("pinv", b - 2)))
        M["exp", b] = m2

    def p_turn(b):
        i = b % 2
        m = None
        for lc in range(TB):
            for jc in range(TB):
                fn = lambda e, lc=lc, jc=jc: e.transpose(PS[:, 3, lc * T + jc * P:lc * T + (jc + 1) * P],
                                                         pr[:, i, jc, lc * P:(lc + 1) * P], ident[:, :])
                if lc == TB - 1 and jc == TB - 1:
                    m = pe.mark(fn)
                else:
                    pe.run(fn, M["exp", b], M.get(("prT", b - 1)))
        M["prT_pe", b] = m
        M["prT", b] = act.mark(lambda e: e.activation(prT[:, i, :, :], bank2(3), ACT.Copy), m, M.get(("mix", b - 2)))
        dve.mark(lambda e: e.tensor_tensor(psum_[:, i, :], psum_[:, i, :], cnt[:, b, :], ALU.mult), M["exp", b])
        M["pinv", b] = dve.chain(lambda e: e.reciprocal(pinv[:, i, :], psum_[:, i, :]))

    def p_mix(b):
        i = b % 2
        for jc in range(TB):
            for lc in range(TB):
                fn = lambda e, jc=jc, lc=lc: e.matmul(PS[:, 4, jc * D:(jc + 1) * D], prT[:, i, lc, jc * P:(jc + 1) * P],
                                                      X[:, TB * b + lc, :], start=(lc == 0), stop=(lc == TB - 1))
                if jc == TB - 1 and lc == TB - 1:
                    M["mix", b] = m = pe.mark(fn)
                else:
                    pe.run(fn, M["prT", b], M.get(("XF", b - 1)))
        for c in range(TB):
            M["XF", b] = act.mark(lambda e, c=c: e.activation(
                XF[:, b % NXF, c, :], PS[:, 4, c * D:(c + 1) * D], ACT.Copy, scale=pinv[:, i, c:c + 1]),
                m, M["pinv", b], M.get(("stored", b - NXF)), M.get(("XFT_pe", b - NXF)))
        M["stored", b] = xf_out[b % NXF].dma(sp, lambda e: e.dma_start(
            pooled[b * T:(b + 1) * T, :].rearrange("(c p) d -> p c d", p=P), XF[:, b % NXF, :, :]), M["XF", b])

    def p_turn_back(b):
        m = transposes(5, lambda t: XF[:, b % NXF, t, :], [M["XF", b], M.get(("XFT", b - 1))])
        M["XFT_pe", b] = m
        M["XFT", b] = act.mark(lambda e: e.activation(XFT[:, :, b * T:(b + 1) * T], bank2(5), ACT.Copy), m)

    GB = R // TB
    scat0 = Lane(sem("scat0"))

    def p_logits(b):
        for t in range(TB):
            r = (TB * b + t) % R
            for c in range(DC):
                fn = lambda e, t=t, c=c, r=r: e.matmul(
                    PS[:, 6, r * E0:(r + 1) * E0], XFT[:, c, (TB * b + t) * P:(TB * b + t + 1) * P], wgT[:, c, :],
                    start=(c == 0), stop=(c == DC - 1))
                if t == TB - 1 and c == DC - 1:
                    M["lg", b] = pe.mark(fn)
                else:
                    pe.run(fn, M["XFT", b], M.get("choose_free0"))
        if b % GB == GB - 1:
            router0.go_on()
            router0.choose(b // GB, PS[:, 6, 0:R * E0].rearrange("p (r e) -> p r e", r=R), M["lg", b])

    def p_dispatch(b, bank=7, *marks):
        if b % GB != GB - 1:
            return
        g = b // GB
        pe.wait(*marks)
        router0.rank(g, bank)
        for bb in range(b - GB + 1, b + 1):
            for t in range(TB):
                for k in range(K0):
                    M["scat0"] = scat0.dma(pool, lambda e, bb=bb, t=t, k=k: e.indirect_dma_start(
                        table0, bass.IndirectOffsetOnAxis(ap=slot0[:, TB * bb + t, k:k + 1], axis=0),
                        token[:, TB * bb + t:TB * bb + t + 1].bitcast(U32), None, bounds_check=S0 - 1, oob_is_err=False),
                        M["slot0", g], filled0, c_base)

    steps = [p_transpose, p_hidden, p_scores, p_turn, p_mix, p_turn_back, p_logits, None, p_dispatch]
    for b in range(2):
        p_mask(b)
    for t in range(B + steps.index(p_logits)):
        for k in reversed(range(len(steps))):
            if steps[k] and 0 <= t - k < B:
                steps[k](t - k)
                if steps[k] is p_scores and t - k + 2 < B:
                    p_mask(t - k + 2)
            if t < B + 5:
                router0.go_on(3)

    all_stored = [M["stored", b] for b in range(B - NXF, B)]
    region.close()
    s = layer0
    stage("experts0")
    meet(pe, act, dve)
    ends = (pe.last, act.last, dve.last)
    for q in (act, dve, pool):
        q.wait(*ends, *all_stored, filled0, fill_end)
    NS0 = CAP0 // P
    NXE = 3
    CH = 512
    NCH = N // CH
    hi_w, lo_w = (sb(n, [P, 2, 3, DC, D], F32R, s) for n in ("hi_w", "lo_w"))
    hi_x, lo_x = (sb(n, [P, 2, DC * CAP0], F32R, s) for n in ("hi_x", "lo_x"))
    hi_h, lo_h = (sb(n, [P, 2, 2, CAP0], F32R, s) for n in ("hi_h", "lo_h"))
    xe = sb("xe", [P, NXE, NS0, D], scope=s)
    gate = sb("gate", [P, 2, 512], scope=s)
    hidden = sb("hidden", [P, 2, 512], scope=s)
    res = sb("res", [P, 2, NS0, D], scope=s)
    w_in = lanes("w_in", NW0)
    xe_in = lanes("xe_in", NXE)
    res_out = lanes("res_out", 2)

    def split(hi, lo, x, hi_marks, lo_marks=()):
        m_hi = act.mark(lambda e: e.activation(hi, x, ACT.Copy), *hi_marks)
        m_lo = dve.mark(lambda e: e.tensor_tensor(lo, x, hi.bitcast(F32), ALU.subtract), m_hi, *lo_marks)
        return m_hi, m_lo

    def product(o, a, b, start, stop, marked, *waits):
        for k, (i, j) in enumerate(((0, 0), (0, 1), (1, 0))):
            fn = lambda e, k=k, i=i, j=j: e.matmul(o, a[i], b[j], start=start and k == 0, stop=stop and k == 2,
                                                   skip_group_check=True)
            if marked and k == 2:
                return pe.mark(fn)
            pe.run(fn, *waits)

    parts = [(0, k) for k in range(NCH)] + [(n + 1, 0) for n in range(E0)]
    NPT = len(parts)
    W0, U, Dn = {}, {}, {}

    def load_w0(j):
        names = ("L0_ffn_sw1", "L0_ffn_sw3", "L0_ffn_sw2") if j == 0 else ("L0_ffn_w1", "L0_ffn_w3", "L0_ffn_w2")
        for i, name in enumerate(names):
            src = io[name] if j == 0 else io[name][j - 1]
            W0[j] = w_in[j % NW0].dma(sp, lambda e, i=i, src=src: e.dma_start(
                w0[:, j % NW0, i, :].rearrange("p (c f) -> p c f", c=DC), src.rearrange("(c p) f -> p c f", p=P)),
                *[M.get(("w_split", j - NW0, q)) for q in range(3)])

    def split_w(j, i):
        if j > E0:
            return
        flat = lambda t: t[:, j % 2, i, :, :].rearrange("p c f -> p (c f)")
        free = Dn.get(j - 2) if i == 2 else U.get(j - 2)
        _, M["w_split", j, i] = split(flat(hi_w), flat(lo_w), w0[:, j % NW0, i, :], [W0[j], free])

    for j in range(NW0):
        load_w0(j)
    w1e_in = lanes("w1e_in", 2)
    W1E = {}

    def load_w1e(n, *marks):
        v = BIG[:, (n % 2) * N:(n % 2 + 1) * N]
        w1e_in[n % 2].dma(sp, lambda e: e.dma_start(v[:, 0:DC * F1].rearrange("p (c f) -> p c f", c=DC),
                                                    io["L1_ffn_W1"][n].rearrange("(c p) f -> p c f", p=P)), *marks)
        W1E[n] = w1e_in[n % 2].dma(sp, lambda e: e.dma_start(v[:, DC * F1:].rearrange("p (c f) -> p c f", f=D),
                                                             io["L1_ffn_W2"][n].rearrange("(c p) f -> p c f", p=P)))

    XE, O = {}, {}

    def load_xe(n):
        for i in range(NS0):
            XE[n] = xe_in[n % NXE].dma(pool, lambda e, i=i: e.indirect_dma_start(
                xe[:, n % NXE, i, :], None, pooled, bass.IndirectOffsetOnAxis(ap=idx0[:, n, i:i + 1], axis=0)),
                M["idx0"], *all_stored, M.get(("turned", n - NXE)))

    TURN, OUT = 4, 6
    t_free, o_free, free_h, hidden_free = [None] * 2, [None] * 2, [None] * 2, [None] * 2

    def tokens_x(k):
        i = k % 2
        for c in range(DC):
            _, M["x", k, c] = split(
                hi_x[:, i, c * CH:(c + 1) * CH], lo_x[:, i, c * CH:(c + 1) * CH], XFT[:, c, k * CH:(k + 1) * CH],
                [M.get(("up", k - 2))])

    def turn_xe(n, us):
        pt = NCH + n
        for u in us:
            tiles = range(4 * u, min(4 * u + 4, DC * NS0))
            for q in tiles:
                c, i = divmod(q, NS0)
                fn = lambda e, c=c, i=i, q=q, u=u: e.transpose(
                    PS[:, TURN + u % 2, (q % 4) * P:(q % 4 + 1) * P], xe[:, n % NXE, i, c * P:(c + 1) * P], ident[:, :])
                if q < tiles[-1]:
                    pe.run(fn, XE[n], t_free[u % 2])
            m = pe.mark(fn)
            w = len(tiles) * P
            cols = slice(4 * u * P, 4 * u * P + w)
            _, M["x", pt, u] = split(hi_x[:, pt % 2, cols], lo_x[:, pt % 2, cols],
                                         PS[:, TURN + u % 2, 0:w], [m, M.get(("up", pt - 2))])
            t_free[u % 2] = M["x", pt, u]
        M["turned", n] = m

    unit = [0]
    waiting = []

    def up_unit(pt, hc, q, w):
        j, i = parts[pt][0], unit[0] % 2
        unit[0] += 1
        width = CH if j == 0 else CAP0
        for k in range(2):
            for c in range(DC):
                col = slice(c * width + q * w, c * width + (q + 1) * w)
                m = product(PS[:, 2 * i + k, 0:w], [t[:, j % 2, k, c, hc * P:(hc + 1) * P] for t in (hi_w, lo_w)],
                            [t[:, pt % 2, col] for t in (hi_x, lo_x)], c == 0, c == DC - 1, c == DC - 1,
                            M["w_split", j, k], *[M.get(("x", pt, u)) for u in range(3)], free_h[i])
            if k == 0:
                m_gate = m
        m1 = act.mark(lambda e: e.activation(gate[:, i, 0:w], PS[:, 2 * i, 0:w], ACT.Silu), m_gate, free_h[i])
        m2 = dve.mark(lambda e: e.tensor_tensor(hidden[:, i, 0:w], gate[:, i, 0:w], PS[:, 2 * i + 1, 0:w], ALU.mult),
                      m1, m, hidden_free[i])
        free_h[i] = m2

        def finish():
            dst = (slice(None), pt % 2, hc, slice(q * w, (q + 1) * w))
            _, M["h", pt, hc, q] = split(hi_h[dst], lo_h[dst], hidden[:, i, 0:w],
                                                            [m2, M.get(("down", pt - 2))])
            hidden_free[i] = M["h", pt, hc, q]

        flush()
        waiting.append(finish)
        M["up", pt] = U[j] = m

    def flush():
        while waiting:
            waiting.pop(0)()

    def down_pair(pt, u):
        j = parts[pt][0]
        n_tiles = (CH if j == 0 else CAP0) // P
        tiles = range(2 * u, min(2 * u + 2, n_tiles))
        if not tiles:
            return
        bank = OUT + u % 2
        ready = [M.get(("h", pt, hc, q)) for hc in range(2) for q in range(2)]
        for i in tiles:
            for hc in range(2):
                m = product(PS[:, bank, (i % 2) * D:(i % 2 + 1) * D], [t[:, pt % 2, hc, i * P:(i + 1) * P] for t in (hi_h, lo_h)],
                            [t[:, j % 2, 2, hc, :] for t in (hi_w, lo_w)], hc == 0, hc == 1, i == tiles[-1] and hc == 1,
                            *ready, M["w_split", j, 2], o_free[u % 2])
        w = len(tiles)
        if j == 0:
            tt = parts[pt][1] * n_tiles + 2 * u
            o_free[u % 2] = dve.mark(lambda e: e.tensor_tensor(X[:, tt:tt + 2, :], X[:, tt:tt + 2, :], bank2(bank), ALU.add), m)
        else:
            n = j - 1
            o_free[u % 2] = M["res", n, u] = dve.mark(lambda e: e.tensor_copy(
                res[:, n % 2, 2 * u:2 * u + w, :], PS[:, bank, 0:w * D].rearrange("p (a n) -> p a n", n=D)), m, O.get(n - 2))
        M["down", pt] = Dn[j] = m

    def store_res(n):
        O[n] = res_out[n % 2].dma(sp, lambda e: e.dma_start(
            done0[n * CAP0:(n + 1) * CAP0, :].rearrange("(p s) d -> p s d", p=P), res[:, n % 2, :, :]),
            *[M["res", n, u] for u in range(3)])

    for i in range(3):
        split_w(0, i)
    load_w0(NW0)
    tokens_x(0)
    PD = 3
    for pt in range(NPT + 1):
        if pt < NPT:
            j, k = parts[pt]
            if j:
                for h in range(4):
                    up_unit(pt, h // 2, h % 2, CAP0 // 2)
                    if h < 2:
                        split_w(j + 1, h)
                if j + 1 < E0:
                    load_xe(j + 1)
            else:
                for h in range(2):
                    up_unit(pt, h, 0, CH)
                    router0.go_on(6)
                    if k == NCH - 1:
                        split_w(1, h)
        if pt >= NPT - 1:
            flush()
        nxt = pt + 1
        turning = nxt < NPT and parts[nxt][0] > 0
        if turning:
            turn_xe(parts[nxt][0] - 1, range(2))
        elif nxt < NPT:
            tokens_x(nxt)
        if pt == PD:
            router0.go_on()
            p_dispatch(B - 1, TURN + 1)
            M["idx0"] = Lane(sem("idx0_in")).dma(sp, lambda e: e.dma_start(
                idx0[:, :, :], table0.rearrange("(e p i) o -> p e (i o)", e=E0, p=P)), M["scat0"])
            for n in range(2):
                load_xe(n)
            t_free[1] = M["slot0", N // P // R - 1]
        if pt > 0:
            down_pair(pt - 1, 0)
        if turning:
            turn_xe(parts[nxt][0] - 1, range(2, 3))
        if pt > 0:
            down_pair(pt - 1, 1)
            down_pair(pt - 1, 2)
            if parts[pt - 1][0]:
                store_res(parts[pt - 1][0] - 1)
        if pt < NPT and (j or k == NCH - 1):
            split_w(j + 1, 2)
            if j + 1 + NW0 <= E0:
                load_w0(j + 1 + NW0)
            if j in (8, 16):
                load_w1e(j // 8 - 1, *[M["x", NCH - 1, c] for c in range(DC)])
    all_done0 = [O[E0 - 2], O[E0 - 1]]
    layer0.close()

    stage("attn")
    meet(pe, act, dve, pool)
    region = ExitStack()
    ctx.enter_context(region)
    s = region
    ends = (pe.last, act.last, dve.last, pool.last)
    for q in (sp, pool, act, dve):
        q.wait(*ends, *all_done0)
    NGA = 2
    got0 = sb("got0", [P, NGA, TB, K0, D], scope=s)
    WS = sb("WS", [P, 2, DC, D], scope=s)
    BS = sb("BS", [P, 2, D], scope=s)
    wqkv = sb("wqkv", [P, DC, 3 * D], scope=s)
    wproj = sb("wproj", [P, DC, D], scope=s)
    wgate = sb("wgate", [P, DC, E1], scope=s)
    lng = sb("lng", [P, 4, DC], scope=s)
    ropec = sb("ropec", [P, TB, 2, 2, HD // 2], scope=s)
    causal_f = sb("causal_f", [P, P], scope=s)
    causal = sb("causal", [P, HG, P], BF16, scope=s)
    ident_b = sb("ident_b", [P, P], BF16, scope=s)
    x1T = sb("x1T", [P, DC, T], scope=s)
    XC = sb("XC", [P, 3, TB, D], scope=s)
    st = sb("st", [P, 2, TB, 6], scope=s)
    mv = sb("mv", [P, 2, TB, 2], scope=s)
    ve = sb("ve", [P, 2, TB], scope=s)
    rs = sb("rs", [P, 2, TB], scope=s)
    xn = sb("xn", [P, TB, D], scope=s)
    hT1 = sb("hT1", [P, DC, T], scope=s)
    NPART = 4
    QK = sb("QK", [P, TB, 2, H, NPART, HD], F32R, s)
    VP = sb("VP", [P, 2, TB, H, HP], scope=s)
    rm = sb("rm", [P, 2, 2, 2, H, HD], scope=s)
    HQ = P // (NPART * HD)
    qT = sb("qT", [P, NG, HG // HQ, T], F32R, s)
    kT = sb("kT", [P, NG, HG // HQ, T], F32R, s)
    NPN = 2
    smax = sb("smax", [P, NPN, 2 * HG], scope=s)
    PN = sb("PN", [P, NPN, 3, 512], scope=s)
    PT = sb("PT", [P, NPN, 3, 512], scope=s)
    oT = sb("oT", [P, 2, NG, T], scope=s)
    rsum = sb("rsum", [P, TB, H], scope=s)
    at = sb("at", [P, TB, H, HD], scope=s)
    atT = sb("atT", [P, DC, T], scope=s)
    XR = sb("XR", [P, 2, TB, D], scope=s)
    NXN = 2
    XN2 = sb("XN2", [P, NXN, TB, D], scope=s)
    h2T = atT
    lgs = sb("lgs", [P, R * E1], scope=s)
    router1 = Router(region, "1", E1, K1, 0, CAP1, base1, w_pick1, slot1)
    gat0 = lanes("gat0_", NGA * TB)
    ws_in = lanes("ws_in", 2)
    scat1 = Lane(sem("scat1"))
    xn_out = lanes("xn_out", NXN)
    base_out = Lane(sem("base_out"))
    attn_in = Lane(sem("attn_in"))
    out_v = out.rearrange("b (c p) d -> p (b c) d", p=P)

    for dst, src in ((causal_f[:, :], io["c_causal"]),
                     (wqkv[:, :, :], io["L1_ffn_WqkvT"].rearrange("(c p) f -> p c f", p=P)),
                     (wproj[:, :, :], io["L1_ffn_Wproj"].rearrange("(c p) f -> p c f", p=P)),
                     (wgate[:, :, :], io["L1_ffn_Wgate"].rearrange("(c p) f -> p c f", p=P)),
                     (lng[:, :, :], io["ln_cols"]), (ropec[:, :, :, :, :], io["c_rope"])):
        c_attn = attn_in.dma(sp, lambda e, d=dst, s_=src: e.dma_start(d, s_))
    W_all = io["L1_cond_W"].rearrange("c i o -> (c i) o")
    errands = []

    def run_errands(n):
        for _ in range(min(n, len(errands))):
            errands.pop(0)()

    def gather(b):
        def result(t, k):
            M["g0", b, t] = gat0[b % NGA * TB + t].dma(pool, lambda e: e.indirect_dma_start(
                got0[:, b % NGA, t, k, :], None, done0,
                bass.IndirectOffsetOnAxis(ap=slot0[:, TB * b + t, k:k + 1], axis=0)), M.get(("comb", b - NGA)), fill_end)

        def matrix(c):
            ws_in[b % 2].dma(pool, lambda e: e.indirect_dma_start(
                WS[:, b % 2, c, :], None, W_all, bass.IndirectOffsetOnAxis(ap=cat_row[:, b, c:c + 1], axis=0)),
                M.get(("xc_pe", b - 2)))

        def bias():
            M["ws", b] = ws_in[b % 2].dma(pool, lambda e: e.indirect_dma_start(
                BS[:, b % 2, :], None, io["L1_cond_b"], bass.IndirectOffsetOnAxis(ap=cat_id[:, b:b + 1], axis=0)),
                M.get(("xc", b - 2)))

        errands[0:0] = [lambda t=t, k=k: result(t, k) for t in range(TB) for k in range(K0)] + [
            lambda c=c: matrix(c) for c in range(DC)] + [bias]

    gather(0)
    dve.mark(lambda e: e.memset(VP[:, :, :, :, :], 0.0))
    m_vp0 = dve.chain(lambda e: e.memset(VP[:, :, :, :, HD:HD + 1], 1.0))
    run_errands(99)
    gather(1)
    run_errands(99)
    for j in range(HG):
        dve.mark(lambda e, j=j: e.tensor_copy(causal[:, j, :], causal_f[:, :]), c_attn)
    m_causal = dve.mark(lambda e: e.tensor_copy(ident_b[:, :], ident[:, :]))

    TBANK, OBANK, LBANK = 3, 5, 6
    light_free = [None, None]
    lcount = [0]

    def light():
        i = lcount[0] % 2
        lcount[0] += 1
        return i, LBANK + i, light_free[i]

    def combine(b, half=None):
        for t in range(TB) if half is None else (half,):
            tt = TB * b + t
            for k in range(K0):
                M["comb", b] = dve.chain(lambda e, t=t, k=k, tt=tt: e.scalar_tensor_tensor(
                    X[:, tt, :], got0[:, b % NGA, t, k, :], w_pick0[:, tt, k:k + 1], X[:, tt, :], ALU.mult, ALU.add),
                    M["g0", b, t])

    def a_turn(b):
        i, bank, free = light()
        m = transposes(bank, lambda t: X[:, TB * b + t, :], [M["comb", b], free])
        light_free[i] = M["x1T", b] = act.mark(lambda e: e.activation(x1T[:, :, :], bank2(bank), ACT.Copy),
                                               m, M.get(("xc_pe", b - 1)))

    def tokens_by(bank, src, w, waits):
        for t in range(TB):
            for c in range(DC):
                fn = lambda e, t=t, c=c: e.matmul(PS[:, bank, t * D:(t + 1) * D], src[:, c, t * P:(t + 1) * P], w(c),
                                                  start=(c == 0), stop=(c == DC - 1))
                if t == TB - 1 and c == DC - 1:
                    return pe.mark(fn)
                pe.run(fn, *waits)

    pending = [[], []]

    def run_pending():
        pending.append([])
        for f in pending.pop(0):
            f()

    def norm(src, j, dst, dst_free, then):
        for t in range(TB):
            dve.mark(lambda e, t=t: e.bn_stats(st[:, j, t, :], src[:, t, :]), dve.last)
        for t in range(TB):
            dve.chain(lambda e, t=t: e.bn_aggr(mv[:, j, t, :], st[:, j, t, :]))
        m = dve.chain(lambda e: e.tensor_scalar(ve[:, j, :], mv[:, j, :, 1], EPS, None, ALU.add))
        m = pool.mark(lambda e: e.tensor_tensor(rs[:, j, :], ve[:, j, :], nhalf[:, :], ALU.pow), m, m_nhalf)

        def scale():
            for t in range(TB):
                m2 = dve.mark(lambda e, t=t: e.tensor_scalar(dst[:, t, :], src[:, t, :], mv[:, j, t, 0:1], rs[:, j, t:t + 1],
                                                             ALU.subtract, ALU.mult), m, *dst_free)
            then(m2)

        pending[-1].append(scale)

    def a_matrix(b):
        i, bank, free = light()
        M["xc_pe", b] = m = tokens_by(bank, x1T, lambda c: WS[:, b % 2, c, :], [M["x1T", b], M["ws", b], free])
        light_free[i] = M["xc", b] = dve.mark(lambda e: e.tensor_tensor(
            XC[:, b % 3, :, :], bank2(bank), wide(BS[:, b % 2, :], 1, [P, TB, D]), ALU.add), m, M.get(("xr", b - 3)))
        norm(XC[:, b % 3, :, :], 0, xn, [M.get(("xn_pe", b - 1))], lambda m: M.update({("xn", b): m}))

    def affine_turn(src, waits, j, dst, dst_free):
        i, bank, free = light()
        m = transposes(bank, src, [*waits, free])
        for c in range(DC):
            light_free[i] = act.mark(lambda e, c=c: e.activation(
                dst[:, c, :], PS[:, bank, c * T:(c + 1) * T], ACT.Identity,
                bias=lng[:, j + 1, c:c + 1], scale=lng[:, j, c:c + 1]), m, dst_free, c_attn)
        return m, light_free[i]

    def a_norm_turn(b):
        M["xn_pe", b], M["hT1", b] = affine_turn(lambda t: xn[:, t, :], [M["xn", b]], 0, hT1, M.get(("v_pe", b - 1)))

    def a_qk(b, t):
        i, bank, free = light()
        for c in range(DC):
            fn = lambda e, c=c: e.matmul(PS[:, bank, :], hT1[:, c, t * P:(t + 1) * P], wqkv[:, c, 0:2 * D],
                                         start=(c == 0), stop=(c == DC - 1))
            if c < DC - 1:
                pe.run(fn, M["hT1", b], free, c_attn)
        m = pe.mark(fn)
        halves = "p q (h a f) -> p q (h a) f"
        src = PS[:, bank, :].rearrange("p (q h f) -> p q h f", q=2, f=HD // 2)
        for cs in range(2):
            m1 = dve.mark(lambda e, cs=cs: e.tensor_tensor(
                rm[:, t, cs, :, :, :].rearrange("p q h (a f) -> p q (h a) f", a=2), src,
                wide(ropec[:, t, cs, :, :], 2, [P, 2, 2 * H, HD // 2]), ALU.mult), m, M.get(("qk_split", b - 1, t)), c_attn)
        light_free[i] = m1
        h8 = HD // 2
        dst = rm[:, t, 0, :, :, :]
        pool.mark(lambda e: e.tensor_tensor(dst[:, :, :, 0:h8], rm[:, t, 0, :, :, 0:h8], rm[:, t, 1, :, :, h8:], ALU.subtract),
                  m1)
        M["qk", b, t] = pool.mark(lambda e: e.tensor_tensor(
            dst[:, :, :, h8:], rm[:, t, 1, :, :, 0:h8], rm[:, t, 0, :, :, h8:], ALU.add))

    def a_split_qk(b, t):
        for q in range(2):
            x = wide(rm[:, t, 0, q, :, :], 2, [P, H, 2, HD])
            hi, lo = ((QK[:, t, q, :, 0::2, :], QK[:, t, q, :, 1::2, :]) if q == 0 else
                      (QK[:, t, q, :, 0:2, :], QK[:, t, q, :, 2:4, :]))
            _, M["qk_split", b, t] = split(hi, lo, x, [M["qk", b, t], M.get(("qk_pe", b - 1))])

    def a_v(b):
        i, bank, free = light()
        M["v_pe", b] = m = tokens_by(bank, hT1, lambda c: wqkv[:, c, 2 * D:3 * D], [M["hT1", b], free])
        light_free[i] = M["vp", b] = act.mark(lambda e: e.activation(
            VP[:, b % 2, :, :, 0:HD], PS[:, bank, :].rearrange("p (t h f) -> p t h f", t=TB, h=H), ACT.Copy), m,
            m_vp0, M.get(("pv", b - 2)))

    def a_turn_heads(b, q, g):
        i, bank, free = light()
        for x in range(HG // HQ):
            for t in range(TB):
                h0 = g * HG + x * HQ
                fn = lambda e, x=x, t=t, h0=h0: e.transpose(
                    PS[:, bank, x * T + t * P:x * T + (t + 1) * P],
                    QK[:, t, q, h0:h0 + HQ, :, :].rearrange("p h s f -> p (h s f)").bitcast(F32), ident[:, :])
                if not (x == HG // HQ - 1 and t == TB - 1):
                    pe.run(fn, M["qk_split", b, 0], M["qk_split", b, 1], free)
        M["qk_pe", b] = m = pe.mark(fn)
        if q == 0:
            light_free[i] = M["qT", b, g] = act.mark(lambda e: e.activation(
                qT[:, g, :, :], bank2(bank), ACT.Copy), m, M.get(("scores", b - 1, g)))
        else:
            light_free[i] = M["kT", b, g] = dve.mark(lambda e: e.tensor_copy(
                kT[:, g, :, :], bank2(bank)), m, M.get(("scores", b - 1, g)))

    s_free = [None] * 3

    def open_masked(b, g, part, o, mask):
        pe.run(lambda e: e.matmul(o, ident_b[:, :], mask, start=True, stop=False, skip_group_check=True),
               s_free[part], m_causal, M["qT", b, g], M["kT", b, g])

    def scores(b, g):
        slot = g % NPN
        rows_ = P // HQ
        head = lambda t_, j, c0, c1: t_[(j % HQ) * rows_:(j % HQ + 1) * rows_, g, j // HQ, c0:c1]
        marks = [None] * 3
        for r in range(HQ):
            open_masked(b, g, r, PS[:, r, :].rearrange("p (x h k) -> p x h k", x=2, h=2)[:, :, 1, :], causal[:, 0:2, :])
            for x in range(2):
                fn = lambda e, x=x, r=r: e.matmul(PS[:, r, x * T:(x + 1) * T], head(qT, r + 2 * x, P, T), head(kT, r + 2 * x, 0, T),
                                                  start=False, stop=True, skip_group_check=True)
                if x == 0:
                    pe.run(fn)
            marks[r] = pe.mark(fn)
            if r == 0:
                open_masked(b, g, 2, PS[:, 2, :].rearrange("p (x k) -> p x k", x=HG), causal[:, :, :])
            pe.wait(marks[2])
            for j in (r, r + 2):
                fn = lambda e, j=j: e.matmul(PS[:, 2, j * P:(j + 1) * P], head(qT, j, 0, P), head(kT, j, 0, P),
                                             start=False, stop=True, skip_group_check=True)
                if j == r:
                    pe.run(fn)
            marks[2] = pe.mark(fn)
        for part in range(3):
            heads_, col = (2, 2 * part) if part < 2 else (HG, HG)
            M["smax", b, g, part] = dve.mark(lambda e, part=part, col=col, heads_=heads_: e.tensor_reduce(
                smax[:, slot, col:col + heads_], PS[:, part, :].rearrange("p (x k) -> p x k", x=heads_), AX.X, ALU.max, negate=True),
                marks[part], M.get(("exp", slot)))
        M["scores", b, g] = pe.last

    def exponentials(b, g, part):
        slot = g % NPN
        heads_, width, col = (2, T, 2 * part) if part < 2 else (HG, P, HG)
        for x in range(heads_):
            s_free[part] = act.mark(lambda e, x=x: e.activation(
                PN[:, slot, part, x * width:(x + 1) * width], PS[:, part, x * width:(x + 1) * width], ACT.Exp,
                bias=smax[:, slot, col + x:col + x + 1]), M["smax", b, g, part], M.get(("turned_p", slot)))
        M["exp", slot] = M["exp", b, g] = s_free[part]

    t_free1 = [None, None]
    tcount = [0]

    def turn_p(b, g, part):
        slot = g % NPN
        i = tcount[0] % 2
        tcount[0] += 1
        bank = TBANK + i
        if part < 2:
            srcs = []
            for x in range(2):
                j = part + 2 * x
                srcs += [PN[:, slot, 2, j * P:(j + 1) * P], PN[:, slot, part, x * T:x * T + P]]
        else:
            srcs = [PN[:, slot, j % 2, (j // 2) * T + P:(j // 2 + 1) * T] for j in range(HG)]
        for k, src in enumerate(srcs):
            fn = lambda e, k=k, src=src: e.transpose(PS[:, bank, k * P:(k + 1) * P], src, ident[:, :])
            if k < HG - 1:
                pe.run(fn, M["exp", b, g], t_free1[i])
        m = pe.mark(fn)
        if part < 2:
            t_free1[i] = act.mark(lambda e: e.activation(PT[:, slot, part, :], PS[:, bank, :], ACT.Copy), m, M.get(("pv", slot)))
        else:
            t_free1[i] = dve.mark(lambda e: e.tensor_copy(PT[:, slot, part, :], PS[:, bank, :]), m, M.get(("pv", slot)))
        M["PT", b, g, part] = t_free1[i]
        M["turned_p", slot] = m

    o_free1 = [None]

    def values(b, g):
        slot = g % NPN
        for j in range(HG):
            hh = g * HG + j
            rows_ = slice(HP * j, HP * (j + 1))
            pe.run(lambda e, hh=hh, j=j, rows_=rows_: e.matmul(
                PS[rows_, OBANK, 0:T], VP[:, b % 2, 0, hh, :], PT[:, slot, j % 2, (j // 2) * T:(j // 2 + 1) * T],
                start=True, stop=False, skip_group_check=True), *[M["PT", b, g, q] for q in range(3)], o_free1[0], M["vp", b])
            fn = lambda e, hh=hh, j=j, rows_=rows_: e.matmul(
                PS[rows_, OBANK, P:T], VP[:, b % 2, 1, hh, :], PT[:, slot, 2, j * P:(j + 1) * P],
                start=False, stop=True, skip_group_check=True)
            if j < HG - 1:
                pe.run(fn)
        M["pv", b] = M["pv", slot] = m = pe.mark(fn)
        o_free1[0] = M["oT", b] = act.mark(lambda e: e.activation(oT[:, b % 2, g, :], PS[:, OBANK, 0:T], ACT.Copy),
                                               m, M.get(("o_pe", b - 2)))

    def a_outputs(b, t):
        i, bank, free = light()
        for g in range(NG):
            fn = lambda e, g=g: e.transpose(PS[:, bank, g * P:(g + 1) * P], oT[:, b % 2, g, t * P:(t + 1) * P], ident[:, :])
            if g < NG - 1:
                pe.run(fn, M["oT", b], free)
        M["o_pe", b] = m = pe.mark(fn)
        v = PS[:, bank, :].rearrange("p (h f) -> p h f", h=H)
        dve.mark(lambda e: e.reciprocal(rsum[:, t, :], v[:, :, HD]), m)
        light_free[i] = M["at", b] = dve.chain(lambda e: e.tensor_tensor(
            at[:, t, :, :], v[:, :, 0:HD], wide(rsum[:, t, :], 2, [P, H, HD]), ALU.mult), M.get(("at_pe", b - 1)))

    def a_out_turn(b):
        i, bank, free = light()
        M["at_pe", b] = m = transposes(bank, lambda t: at[:, t, :, :].rearrange("p h f -> p (h f)"), [M["at", b], free])
        light_free[i] = M["atT", b] = act.mark(lambda e: e.activation(atT[:, :, :], bank2(bank), ACT.Copy), m,
                                               M.get(("proj", b - 1)), M.get(("lg1", b - 1)))

    def a_proj(b):
        i, bank, free = light()
        M["proj", b] = m = tokens_by(bank, atT, lambda c: wproj[:, c, :], [M["atT", b], free])
        j = b % 2
        light_free[i] = M["xr", b] = dve.mark(lambda e: e.tensor_tensor(XR[:, j, :, :], bank2(bank), XC[:, b % 3, :, :], ALU.add),
                                              m, M.get(("base", b - 2)))

        def store(m2):
            M["xn2", b] = m2
            M["xn_out", b] = xn_out[b % NXN].dma(sp, lambda e: e.dma_start(
                normed[b * T:(b + 1) * T, :].rearrange("(c p) d -> p c d", p=P), XN2[:, b % NXN, :, :]), m2)

        norm(XR[:, j, :, :], 1, XN2[:, b % NXN, :, :], [M.get(("xn_out", b - NXN)), M.get(("xn2_pe", b - NXN))], store)
        M["base", b] = pool.mark(lambda e: e.tensor_tensor(X[:, TB * b:TB * b + TB, :], X[:, TB * b:TB * b + TB, :], XR[:, j, :, :], ALU.add),
                                 M["xr", b])
        M["base_out"] = base_out.dma(sp, lambda e: e.dma_start(out_v[:, TB * b:TB * b + TB, :], X[:, TB * b:TB * b + TB, :]), M["base", b])

    def a_gate_turn(b):
        M["xn2_pe", b], M["h2T", b] = affine_turn(lambda t: XN2[:, b % NXN, t, :], [M["xn2", b]], 2, h2T, M.get(("lg1", b - 1)))

    def a_gate(b):
        i, bank, free = light()
        for t in range(TB):
            for c in range(DC):
                fn = lambda e, t=t, c=c: e.matmul(PS[:, bank, t * E1:(t + 1) * E1], h2T[:, c, t * P:(t + 1) * P], wgate[:, c, :],
                                                  start=(c == 0), stop=(c == DC - 1))
                if not (t == TB - 1 and c == DC - 1):
                    pe.run(fn, M["h2T", b], free)
        M["lg1", b] = pe.mark(fn)
        half = (b % GB) * TB * E1
        light_free[i] = dve.mark(lambda e: e.tensor_copy(lgs[:, half:half + TB * E1], PS[:, bank, 0:TB * E1]), M["lg1", b], dve.last)

    def a_choose(b):
        if b % GB == GB - 1:
            router1.choose(b // GB, lgs[:, :].rearrange("p (r e) -> p r e", r=R), dve.last)
            router1.go_on()

    def a_dispatch(b):
        if b % GB != GB - 1:
            return
        g = b // GB
        i, bank, free = light()
        pe.wait(free)
        router1.rank(g, bank)
        light_free[i] = M["slot1", g]

        def entry(tt, k):
            M["scat1"] = scat1.dma(pool, lambda e: e.indirect_dma_start(
                table1, bass.IndirectOffsetOnAxis(ap=slot1[:, tt, k:k + 1], axis=0),
                pair1[:, tt, k, :], None, bounds_check=S1 - 1, oob_is_err=False), M["slot1", g], M["w1", g], m_pair, filled1)

        for tt in range(g * R, (g + 1) * R):
            for k in range(K1):
                errands.append(lambda tt=tt, k=k: entry(tt, k))

    def light_stages(b, g, gap):
        run_pending()
        for f, off in PLAN[g, gap]:
            if 0 <= b + off < B:
                f(b + off)
        run_errands(1)

    turn = lambda q, g: lambda b: a_turn_heads(b, q, g)
    qk = lambda t: lambda b: a_qk(b, t)
    split_qk = lambda t: lambda b: a_split_qk(b, t)
    outputs = lambda t: lambda b: a_outputs(b, t)
    add = lambda t: lambda b: combine(b, t) if b > 0 else None
    PLAN = {
        (0, 0): [(gather, 3), (a_turn, 1), (turn(0, 1), 0)],
        (0, 1): [(turn(1, 1), 0), (a_matrix, 1), (a_gate_turn, -2)],
        (0, 2): [],
        (0, 3): [(a_gate, -2)],
        (1, 0): [(turn(0, 2), 0), (add(0), 2)],
        (1, 1): [(a_norm_turn, 1), (turn(1, 2), 0)],
        (1, 2): [(a_choose, -2)],
        (1, 3): [(qk(0), 1)],
        (2, 0): [(turn(0, 3), 0), (outputs(0), -1), (outputs(1), -1), (add(1), 2)],
        (2, 1): [(turn(1, 3), 0)],
        (2, 2): [(qk(1), 1), (a_out_turn, -1)],
        (2, 3): [(split_qk(0), 1)],
        (3, 0): [(split_qk(1), 1)],
        (3, 1): [(a_proj, -1), (a_v, 1)],
        (3, 2): [(turn(0, 0), 1), (turn(1, 0), 1)],
        (3, 3): [(a_dispatch, -2)],
    }

    combine(0)
    for g in range(NG):
        for gap in range(4):
            light_stages(-1, g, gap)
    for b in range(B + 2):
        for g in range(NG):
            b1, g1 = (b, g - 1) if g >= 1 else (b - 1, g - 1 + NG)
            b2, g2 = (b, g - 2) if g >= 2 else (b - 1, g - 2 + NG)
            if b < B:
                scores(b, g)
            light_stages(b, g, 0)
            if b < B:
                exponentials(b, g, 0)
            if 0 <= b1 < B:
                turn_p(b1, g1, 0)
                turn_p(b1, g1, 1)
            if b < B:
                exponentials(b, g, 1)
            light_stages(b, g, 1)
            if 0 <= b1 < B:
                turn_p(b1, g1, 2)
            if b < B:
                exponentials(b, g, 2)
            light_stages(b, g, 2)
            if 0 <= b2 < B:
                values(b2, g2)
            light_stages(b, g, 3)
    run_errands(99)
    region.close()

    stage("experts1")
    meet(pe, act, dve, pool)
    region = ExitStack()
    ctx.enter_context(region)
    s = region
    ends = (pe.last, act.last, dve.last, pool.last)
    all_normed = [M["xn_out", b] for b in range(B - NXN, B)]
    for q in (sp, pool, act, dve):
        q.wait(*ends, *all_normed, M["base_out"])
    HS = 512
    NH = CAP1 // HS
    NS1 = HS // P
    FC = F1 // P
    tab = sb("tab", [P, E1, CAP1 // P, 2], scope=s)
    xe1 = X[:, 0:3 * NS1, :].rearrange("p (u i) d -> p u i d", u=3)
    res1 = X[:, 3 * NS1:6 * NS1, :].rearrange("p (u i) d -> p u i d", u=3)
    hi_w1, lo_w1 = (sb(n, [P, 2, 2 * DC * F1], F32R, s) for n in ("hi_w1", "lo_w1"))
    hi_x1, lo_x1 = (sb(n, [P, 2, DC, HS], F32R, s) for n in ("hi_x1", "lo_x1"))
    hi_h1, lo_h1 = (sb(n, [P, FC, HS], F32R, s) for n in ("hi_h1", "lo_h1"))
    x1 = sb("x1", [P, 2, HS], scope=s)
    NHF = 3
    hidden1 = sb("hidden1", [P, NHF, HS], scope=s)
    b1s = sb("b1s", [P, E1, FC], scope=s)
    b2s = sb("b2s", [P, 2, D], scope=s)
    lng1 = sb("lng1", [P, 4, DC], scope=s)
    xe1_in = lanes("xe1_in", 3)
    b2_in = lanes("b2_in", 2)
    res1_out = lanes("res1_out", 3)
    tab_in = Lane(sem("tab_in")).dma(sp, lambda e: e.dma_start(
        tab[:, :, :, :], table1.rearrange("(e p i) w -> p e i w", e=E1, p=P)), M["scat1"])
    e1_in = Lane(sem("e1_in"))
    e1_in.dma(sp, lambda e: e.dma_start(b1s[:, :, :], io["b1_cols"]))
    c_e1 = e1_in.dma(sp, lambda e: e.dma_start(lng1[:, :, :], io["ln_cols"]))
    units = [(n, h) for n in range(E1) for h in range(NH)]
    X1, B2, O1 = {}, {}, {}

    def who(n, h, i):
        return tab[:, n, h * NS1 + i, 0:1].bitcast(U32)

    def load1(u):
        n, h = units[u]
        for i in range(NS1):
            X1[u] = xe1_in[u % 3].dma(pool, lambda e, i=i: e.indirect_dma_start(
                xe1[:, u % 3, i, :], None, normed, bass.IndirectOffsetOnAxis(ap=who(n, h, i), axis=0)),
                tab_in, M.get(("t1", u - 3)), fill_end)
        if h == 0:
            B2[n] = b2_in[n % 2].dma(sp, lambda e: e.dma_start(b2s[:, n % 2, :], io["L1_ffn_b2"][n].partition_broadcast(P)),
                                     M.get(("r1", u - NH - 1)))

    NWQ = 8
    WQ = 2 * DC * F1 // NWQ

    def split_w1(n, k):
        if n >= E1:
            return
        cols = slice(k * WQ, (k + 1) * WQ)
        free = M.get(("u1", NH * (n - 1) - 1)) if k < NWQ // 2 else M.get(("d1", NH * (n - 1) - 1))
        _, M["w1_split", n] = split(hi_w1[:, n % 2, cols], lo_w1[:, n % 2, cols],
                                    BIG[:, (n % 2) * N + k * WQ:(n % 2) * N + (k + 1) * WQ], [W1E[n], free])

    tb_free, x1_free = [None, None], [None, None]

    def turn1(u):
        for c in range(DC):
            for i in range(NS1):
                fn = lambda e, c=c, i=i: e.transpose(PS[:, c, i * P:(i + 1) * P], xe1[:, u % 3, i, c * P:(c + 1) * P], ident[:, :])
                if i < NS1 - 1:
                    pe.run(fn, X1[u], tb_free[c])
            m = pe.mark(fn)
            tb_free[c] = dve.mark(lambda e, c=c: e.tensor_scalar(
                x1[:, c, :], PS[:, c, :], lng1[:, 2, c:c + 1], lng1[:, 3, c:c + 1], ALU.mult, ALU.add),
                m, c_e1, x1_free[c])
            _, M["x1eT", u, c] = split(hi_x1[:, u % 2, c, :], lo_x1[:, u % 2, c, :], x1[:, c, :],
                                       [tb_free[c], M.get(("u1", u - 2))])
            x1_free[c] = M["x1eT", u, c]
        M["t1", u] = m

    ub_free, hf_free = [None] * 3, [None] * NHF
    ub = [0]
    waiting1 = []

    def up1(u):
        n, h = units[u]
        for f in range(FC):
            k, hs = ub[0] % 3, ub[0] % NHF
            ub[0] += 1
            for c in range(DC):
                col = c * F1 + f * P
                m = product(PS[:, 2 + k, :], [t[:, n % 2, col:col + P] for t in (hi_w1, lo_w1)],
                            [t[:, u % 2, c, :] for t in (hi_x1, lo_x1)], c == 0, c == DC - 1, c == DC - 1,
                            M["w1_split", n], M["x1eT", u, 0], M["x1eT", u, 1], ub_free[k])
            ub_free[k] = mh = act.mark(lambda e, f=f, k=k, hs=hs: e.activation(
                hidden1[:, hs, :], PS[:, 2 + k, :], ACT.Gelu, bias=b1s[:, n, f:f + 1]), m, c_e1, hf_free[hs])

            def finish(f=f, hs=hs, mh=mh):
                _, M["h1", u, f] = split(hi_h1[:, f, :], lo_h1[:, f, :], hidden1[:, hs, :], [mh, M.get(("d1", u - 1))])
                hf_free[hs] = M["h1", u, f]

            if waiting1:
                waiting1.pop()()
            waiting1.append(finish)
            if f % 2:
                split_w1(n + 1, h * NWQ // 2 + f // 2)
        waiting1.pop()()
        M["u1", u] = m

    db_free = [None, None]

    def down1(u):
        n, h = units[u]
        for f in range(FC):
            for i in range(NS1):
                col = DC * F1 + f * D
                last = f == FC - 1 and i % 2 == 1
                m = product(PS[:, 5 + i // 2, (i % 2) * D:(i % 2 + 1) * D], [t[:, f, i * P:(i + 1) * P] for t in (hi_h1, lo_h1)],
                            [t[:, n % 2, col:col + D] for t in (hi_w1, lo_w1)], f == 0 and i % 2 == 0, last, last,
                            M["h1", u, f], db_free[i // 2])
                if last:
                    done(u, i // 2, m)
        M["d1", u] = m

    def done(u, q, m):
        n, h = units[u]
        db_free[q] = M["r1", u] = dve.mark(lambda e: e.tensor_tensor(
            res1[:, u % 3, 2 * q:2 * q + 2, :], bank2(5 + q), wide(b2s[:, n % 2, :], 1, [P, 2, D]), ALU.add),
            m, B2[n], O1.get(u - 3))
        for i in range(2 * q, 2 * q + 2):
            mg = dve.mark(lambda e, i=i: e.tensor_scalar(res1[:, u % 3, i, :], res1[:, u % 3, i, :],
                                                         tab[:, n, h * NS1 + i, 1:2], None, ALU.mult), M["r1", u])
            O1[u] = res1_out[u % 3].dma(pool, lambda e, i=i: e.indirect_dma_start(
                out_rows, bass.IndirectOffsetOnAxis(ap=who(n, h, i), axis=0), res1[:, u % 3, i, :], None,
                bounds_check=N - 1, oob_is_err=False, compute_op=ALU.add),
                mg, M["base_out"], *[O1.get(v) for v in range(u - 2 - h, u - h)])

    out_rows = out.rearrange("b t d -> (b t) d")
    load1(0)
    load1(1)
    for k in range(NWQ):
        split_w1(0, k)
    turn1(0)
    for u in range(len(units)):
        n, h = units[u]
        up1(u)
        if u + 1 < len(units):
            turn1(u + 1)
        if u + 2 < len(units):
            load1(u + 2)
        down1(u)
        if h == NH - 1 and n + 2 < E1:
            load_w1e(n + 2, M["w1_split", n])
    sp.wait(*[O1[u] for u in range(len(units) - 3, len(units))], M["base_out"], fill_end, filled0, filled1,
            *all_done0, *all_stored, *all_normed, M["scat0"], M["scat1"])
    region.close()

    block = ctx.enter_context(nc.Block())

    @block.sync
    def _(e):
        sp.play(e)

    @block.gpsimd
    def _(e):
        pool.play(e)

    @block.tensor
    def _(e):
        pe.play(e)

    @block.scalar
    def _(e):
        act.play(e)

    @block.vector
    def _(e):
        dve.play(e)


def lay_out(inputs):
    a = {k: np.asarray(v) for k, v in inputs.items()}
    m = {k: a[k] for k in ("x", "itok_B_0_2", "itok_B_0_30", "L0_cond_W1", "L0_ffn_w1", "L0_ffn_w2", "L0_ffn_w3",
                           "L0_ffn_sw1", "L0_ffn_sw2", "L0_ffn_sw3", "L1_cond_W", "L1_cond_b", "L1_ffn_Wproj",
                           "L1_ffn_Wgate", "L1_ffn_W1", "L1_ffn_W2", "L1_ffn_b2")}
    m["L0_cond_b1"] = a["L0_cond_b1"].reshape(A0, 1)
    m["L0_cond_v"] = a["L0_cond_v"].reshape(A0, 1)
    m["L0_ffn_wgT"] = a["L0_ffn_wg"].T
    m["L1_ffn_WqkvT"] = a["L1_ffn_Wqkv"].reshape(D, H, 3, HD).transpose(0, 2, 1, 3).reshape(D, 3 * D)
    col = lambda v: v.reshape(DC, P).T
    m["ln_cols"] = np.stack([col(a[f"L1_ffn_{n}"]) for n in ("ln1_g", "ln1_b", "ln2_g", "ln2_b")], 1)
    m["b1_cols"] = a["L1_ffn_b1"].reshape(E1, F1 // P, P).transpose(2, 0, 1)
    m.update(shape_constants())
    return {k: np.ascontiguousarray(v) for k, v in m.items()}


def kernel(**inputs):
    import concourse.bacc as _bacc
    from concourse.bass_utils import run_bass_kernel_spmd as _run

    nc = _bacc.Bacc("TRN2", target_bir_lowering=False, num_devices=1)
    arrays = lay_out(inputs)
    io = {k: nc.dram_tensor(f"in_{k}", v.shape, mybir.dt.from_np(v.dtype), kind="ExternalInput").ap() for k, v in arrays.items()}
    out = nc.dram_tensor("out_0", (B, T, D), F32, kind="ExternalOutput").ap()
    bass_adaln_ffn(nc, io, out)
    r = _run(nc, [{f"in_{k}": v for k, v in arrays.items()}], core_ids=[0])
    return r.results[0]["out_0"]
```
